# Optimizing a Trainium2 kernel written in Bass

```python
import numpy as np
import jax
import jax.numpy as jnp

def _softmax(x, axis=-1):
    return jax.nn.softmax(x, axis=axis)

def _gelu(x):
    return jax.nn.gelu(x, approximate=True)

def _silu(x):
    return jax.nn.silu(x)

def _sigmoid(x):
    return jax.nn.sigmoid(x)

def _layernorm(x, axis=-1, eps=1e-05):
    m = jnp.mean(x, axis=axis, keepdims=True)
    v = jnp.var(x, axis=axis, keepdims=True)
    return (x - m) / jnp.sqrt(v + eps)

def _scatter_add(tgt, idx, src, axis=0):
    return tgt.at[idx].add(src)

def _segment_sum(src, seg, n):
    return jax.ops.segment_sum(src, seg, n)
kernel_name = 'mk_xattn_ffn_d2_seqx_r8_fa6246'

def setup_inputs(seed: int=0):
    np.random.seed(seed)
    _w = jnp.asarray

    def _rec_inputs():
        import jax
        import jax.numpy as jnp
        _rk = jax.random.key(seed)
        x = -0.0005207 + 1.001 * jax.random.normal(jax.random.fold_in(_rk, 1), (16, 64, 256), jnp.float32)
        _lenS = 64 - jax.random.randint(jax.random.fold_in(_rk, 7), (16,), 0, max(1, 64 // 4) + 1, jnp.int32)
        _lenS2 = 64 - jax.random.randint(jax.random.fold_in(_rk, 8), (16,), 0, max(1, 64 // 4) + 1, jnp.int32)
        _ctx_2048P = jax.random.normal(jax.random.fold_in(_rk, 11), (16, 16, 256), jnp.float32)
        _ctx_2048c = jax.random.dirichlet(jax.random.fold_in(_rk, 511), 0.3 * jnp.ones((16,), jnp.float32), (16, 64))
        _ctx_2048t = jnp.einsum('bsk,bkd->bsd', _ctx_2048c, _ctx_2048P)
        _ctx_2048t = _ctx_2048t * jax.lax.rsqrt(jnp.mean(jnp.square(_ctx_2048t)) + 1e-12) * 0.953939
        ctx_2048 = -0.000514642 + 1.00011 * (_ctx_2048t + 0.3 * jax.random.normal(jax.random.fold_in(_rk, 611), (16, 64, 256), jnp.float32))
        return (x, ctx_2048)
    x, ctx_2048 = _rec_inputs()

    def _L0_xattn_setup():
        import jax, jax.numpy as jnp
        import numpy as np
        from math import sqrt
        key = jax.random.key(seed)
        kq, kk, kv = jax.random.split(key, 3)
        B, D, N = (8, 128, 256)
        Q = jax.random.normal(kq, (B, D, N), dtype=jnp.float32)
        K = jax.random.normal(kk, (B, D, N), dtype=jnp.float32)
        V = jax.random.normal(kv, (B, D, N), dtype=jnp.float32)
        return {'Q': Q, 'K': K, 'V': V}
    _L0_xattn_all = _L0_xattn_setup()
    _L0_xattn_in = {k: v for k, v in _L0_xattn_all.items() if k in ()}
    del _L0_xattn_all

    def _L0_ffn_setup():
        import jax, jax.numpy as jnp
        import numpy as np
        TOP_K = 2
        key = jax.random.key(seed)
        ks = jax.random.split(key, 5)
        B, T, D, E, H = (4, 256, 256, 8, 176)
        s = 1.0 / np.sqrt(D)
        sh = 1.0 / np.sqrt(H)
        return {'x': jax.random.normal(ks[0], (B, T, D), dtype=jnp.float32), 'Wg': jax.random.normal(ks[1], (E, D), dtype=jnp.float32) * s, 'W1': jax.random.normal(ks[2], (E, H, D), dtype=jnp.float32) * s, 'W2': jax.random.normal(ks[3], (E, H, D), dtype=jnp.float32) * s, 'W3': jax.random.normal(ks[4], (E, D, H), dtype=jnp.float32) * sh}
    _L0_ffn_all = _L0_ffn_setup()
    _L0_ffn_in = {k: v for k, v in _L0_ffn_all.items() if k in ('Wg', 'W1', 'W2', 'W3')}
    del _L0_ffn_all

    def _L1_xattn_setup():
        import jax, jax.numpy as jnp
        import numpy as np
        D_MODEL = 256
        NUM_HEADS = 16
        HEAD_DIM = D_MODEL // NUM_HEADS
        key = jax.random.key(seed)
        ks = jax.random.split(key, 10)
        B, S, T = (4, 512, 128)
        s = 1.0 / np.sqrt(D_MODEL)
        inp = {'query': jax.random.normal(ks[0], (B, S, D_MODEL), jnp.float32), 'key_value': jax.random.normal(ks[1], (B, T, D_MODEL), jnp.float32), 'Wq': jax.random.normal(ks[2], (D_MODEL, D_MODEL), jnp.float32) * s, 'bq': jnp.zeros((D_MODEL,), jnp.float32), 'Wk': jax.random.normal(ks[3], (D_MODEL, D_MODEL), jnp.float32) * s, 'bk': jnp.zeros((D_MODEL,), jnp.float32), 'Wv': jax.random.normal(ks[4], (D_MODEL, D_MODEL), jnp.float32) * s, 'bv': jnp.zeros((D_MODEL,), jnp.float32), 'Wo': jax.random.normal(ks[5], (D_MODEL, D_MODEL), jnp.float32) * s, 'bo': jnp.zeros((D_MODEL,), jnp.float32)}
        return inp
    _L1_xattn_all = _L1_xattn_setup()
    _L1_xattn_in = {k: v for k, v in _L1_xattn_all.items() if k in ('Wq', 'bq', 'Wk', 'bk', 'Wv', 'bv', 'Wo', 'bo')}
    del _L1_xattn_all

    def _L1_ffn_setup():
        import jax, jax.numpy as jnp
        import numpy as np
        import math
        B, S, D = (2, 128, 256)
        H, KVH, HD = (16, 4, 128)
        E, K, FF = (8, 2, 896)
        EPS = 1e-05
        ROPE_BASE = 1000000.0

        def rmsnorm(x, w, eps=EPS):
            xf = x.astype(jnp.float32)
            var = jnp.mean(xf * xf, axis=-1, keepdims=True)
            return (xf * jax.lax.rsqrt(var + eps)).astype(x.dtype) * w

        def apply_rope(x, cos, sin):
            x1 = x[..., 0::2]
            x2 = x[..., 1::2]
            r1 = x1 * cos - x2 * sin
            r2 = x1 * sin + x2 * cos
            return jnp.stack([r1, r2], axis=-1).reshape(x.shape)
        key = jax.random.key(seed)
        ks = jax.random.split(key, 12)
        sc = 0.02
        inp = {'x': jax.random.normal(ks[0], (B, S, D), jnp.float32), 'ln_w': jnp.ones((D,), jnp.float32), 'ff_ln_w': jnp.ones((D,), jnp.float32), 'wq': jax.random.normal(ks[1], (D, H * HD), jnp.float32) * sc, 'wk': jax.random.normal(ks[2], (D, KVH * HD), jnp.float32) * sc, 'wv': jax.random.normal(ks[3], (D, KVH * HD), jnp.float32) * sc, 'wo': jax.random.normal(ks[4], (H * HD, D), jnp.float32) * sc, 'gate_w': jax.random.normal(ks[5], (D, E), jnp.float32) * sc, 'w1': jax.random.normal(ks[6], (E, D, FF), jnp.float32) * sc, 'w3': jax.random.normal(ks[7], (E, D, FF), jnp.float32) * sc, 'w2': jax.random.normal(ks[8], (E, FF, D), jnp.float32) * sc}
        return inp
    _L1_ffn_all = _L1_ffn_setup()
    _L1_ffn_in = {k: v for k, v in _L1_ffn_all.items() if k in ('ln_w', 'ff_ln_w', 'wq', 'wk', 'wv', 'wo', 'gate_w', 'w1', 'w3', 'w2')}
    del _L1_ffn_all
    return {'x': x, 'ctx_2048': ctx_2048, 'L0_ffn_Wg': _L0_ffn_in['Wg'], 'L0_ffn_W1': _L0_ffn_in['W1'], 'L0_ffn_W2': _L0_ffn_in['W2'], 'L0_ffn_W3': _L0_ffn_in['W3'], 'L1_xattn_Wq': _L1_xattn_in['Wq'], 'L1_xattn_bq': _L1_xattn_in['bq'], 'L1_xattn_Wk': _L1_xattn_in['Wk'], 'L1_xattn_bk': _L1_xattn_in['bk'], 'L1_xattn_Wv': _L1_xattn_in['Wv'], 'L1_xattn_bv': _L1_xattn_in['bv'], 'L1_xattn_Wo': _L1_xattn_in['Wo'], 'L1_xattn_bo': _L1_xattn_in['bo'], 'L1_ffn_ln_w': _L1_ffn_in['ln_w'], 'L1_ffn_ff_ln_w': _L1_ffn_in['ff_ln_w'], 'L1_ffn_wq': _L1_ffn_in['wq'], 'L1_ffn_wk': _L1_ffn_in['wk'], 'L1_ffn_wv': _L1_ffn_in['wv'], 'L1_ffn_wo': _L1_ffn_in['wo'], 'L1_ffn_gate_w': _L1_ffn_in['gate_w'], 'L1_ffn_w1': _L1_ffn_in['w1'], 'L1_ffn_w3': _L1_ffn_in['w3'], 'L1_ffn_w2': _L1_ffn_in['w2']}

def reference(x, ctx_2048, L0_ffn_Wg, L0_ffn_W1, L0_ffn_W2, L0_ffn_W3, L1_xattn_Wq, L1_xattn_bq, L1_xattn_Wk, L1_xattn_bk, L1_xattn_Wv, L1_xattn_bv, L1_xattn_Wo, L1_xattn_bo, L1_ffn_ln_w, L1_ffn_ff_ln_w, L1_ffn_wq, L1_ffn_wk, L1_ffn_wv, L1_ffn_wo, L1_ffn_gate_w, L1_ffn_w1, L1_ffn_w3, L1_ffn_w2):
    import jax
    import jax.numpy as jnp

    def _L0_xattn_ref(Q, K, V):
        import jax, jax.numpy as jnp
        import numpy as np
        from math import sqrt
        dk = Q.shape[1]
        x = jnp.einsum('bdn,bdm->bnm', Q, K) / sqrt(dk)
        score = jax.nn.sigmoid(x)
        out = jnp.einsum('bvn,bnm->bvm', V, score)
        return out

    def _L0_ffn_ref(x, Wg, W1, W2, W3):
        import jax, jax.numpy as jnp
        import numpy as np
        TOP_K = 2
        E = Wg.shape[0]
        scores = jnp.einsum('btd,ed->bte', x, Wg)
        topk_s, topk_i = jax.lax.top_k(scores, TOP_K)
        probs = jax.nn.softmax(topk_s, axis=-1)
        onehot = (topk_i[..., None] == jnp.arange(E)).astype(x.dtype)
        w = jnp.einsum('btk,btke->bte', probs, onehot)
        y = jnp.zeros_like(x)
        for e in range(E):
            h = jax.nn.silu(jnp.einsum('btd,hd->bth', x, W1[e])) * jnp.einsum('btd,hd->bth', x, W2[e])
            y = y + w[..., e:e + 1] * jnp.einsum('bth,dh->btd', h, W3[e])
        return y

    def _L1_xattn_ref(query, key_value, Wq, bq, Wk, bk, Wv, bv, Wo, bo):
        import jax, jax.numpy as jnp
        import numpy as np
        D_MODEL = 256
        NUM_HEADS = 16
        HEAD_DIM = D_MODEL // NUM_HEADS
        B, S, _ = query.shape
        T = key_value.shape[1]
        Q = query @ Wq.T + bq
        K = key_value @ Wk.T + bk
        V = key_value @ Wv.T + bv
        Q = Q.reshape(B, S, NUM_HEADS, HEAD_DIM).transpose(0, 2, 1, 3)
        K = K.reshape(B, T, NUM_HEADS, HEAD_DIM).transpose(0, 2, 1, 3)
        V = V.reshape(B, T, NUM_HEADS, HEAD_DIM).transpose(0, 2, 1, 3)
        scale = 1.0 / np.sqrt(HEAD_DIM).astype(np.float32)
        scores = jnp.einsum('bhsd,bhtd->bhst', Q, K) * scale
        attn = jax.nn.softmax(scores, axis=-1)
        ctx = jnp.einsum('bhst,bhtd->bhsd', attn, V)
        ctx = ctx.transpose(0, 2, 1, 3).reshape(B, S, D_MODEL)
        return ctx @ Wo.T + bo

    def _L1_ffn_ref(x, ln_w, ff_ln_w, wq, wk, wv, wo, gate_w, w1, w3, w2):
        import jax, jax.numpy as jnp
        import numpy as np
        import math
        B, S, D = (2, 128, 256)
        H, KVH, HD = (16, 4, 128)
        E, K, FF = (8, 2, 896)
        EPS = 1e-05
        ROPE_BASE = 1000000.0

        def rmsnorm(x, w, eps=EPS):
            xf = x.astype(jnp.float32)
            var = jnp.mean(xf * xf, axis=-1, keepdims=True)
            return (xf * jax.lax.rsqrt(var + eps)).astype(x.dtype) * w

        def apply_rope(x, cos, sin):
            x1 = x[..., 0::2]
            x2 = x[..., 1::2]
            r1 = x1 * cos - x2 * sin
            r2 = x1 * sin + x2 * cos
            return jnp.stack([r1, r2], axis=-1).reshape(x.shape)
        Bx, Sx, Dx = x.shape
        residual = x
        h = rmsnorm(x, ln_w)
        q = (h @ wq).reshape(Bx, Sx, H, HD)
        k = (h @ wk).reshape(Bx, Sx, KVH, HD)
        v = (h @ wv).reshape(Bx, Sx, KVH, HD)
        pos = jnp.arange(Sx, dtype=jnp.float32)
        inv_freq = ROPE_BASE ** (-jnp.arange(0, HD, 2, dtype=jnp.float32) / HD)
        ang = pos[:, None] * inv_freq[None, :]
        cos = jnp.cos(ang)[None, :, None, :]
        sin = jnp.sin(ang)[None, :, None, :]
        q = apply_rope(q, cos, sin)
        k = apply_rope(k, cos, sin)
        rep = H // KVH
        k = jnp.repeat(k, rep, axis=2)
        v = jnp.repeat(v, rep, axis=2)
        scores = jnp.einsum('bqhd,bkhd->bhqk', q, k) / math.sqrt(HD)
        causal = jnp.tril(jnp.ones((Sx, Sx), dtype=bool))
        scores = jnp.where(causal[None, None], scores, jnp.finfo(scores.dtype).min)
        attn = jax.nn.softmax(scores, axis=-1)
        o = jnp.einsum('bhqk,bkhd->bqhd', attn, v).reshape(Bx, Sx, H * HD)
        x = o @ wo + residual
        residual = x
        h = rmsnorm(x, ff_ln_w)
        ht = h.reshape(-1, Dx)
        logits = ht @ gate_w
        top_vals, top_idx = jax.lax.top_k(logits, K)
        gates = jax.nn.softmax(top_vals, axis=-1)
        out = jnp.zeros_like(ht)
        for e in range(E):
            we = jnp.sum(gates * (top_idx == e), axis=-1)
            ye = jax.nn.silu(ht @ w1[e]) * (ht @ w3[e]) @ w2[e]
            out = out + we[:, None] * ye
        return out.reshape(Bx, Sx, Dx) + residual
    x = x + _L0_xattn_ref(_layernorm(x, axis=-1), ctx_2048, ctx_2048)
    x = x + _L0_ffn_ref(_layernorm(x, axis=-1), L0_ffn_Wg, L0_ffn_W1, L0_ffn_W2, L0_ffn_W3)
    x = x + _L1_xattn_ref(_layernorm(x, axis=-1), ctx_2048, L1_xattn_Wq, L1_xattn_bq, L1_xattn_Wk, L1_xattn_bk, L1_xattn_Wv, L1_xattn_bv, L1_xattn_Wo, L1_xattn_bo)
    x = x + _L1_ffn_ref(_layernorm(x, axis=-1), L1_ffn_ln_w, L1_ffn_ff_ln_w, L1_ffn_wq, L1_ffn_wk, L1_ffn_wv, L1_ffn_wo, L1_ffn_gate_w, L1_ffn_w1, L1_ffn_w3, L1_ffn_w2)
    return x

_drawn_inputs = setup_inputs


def setup_inputs(seed=0):
    import zlib

    import numpy as np

    out = dict(_drawn_inputs(seed))
    spreads = {'L1_xattn_bq': (0.0, 0.8),
     'L1_xattn_bk': (0.0, 0.8),
     'L1_xattn_bv': (0.0, 0.593),
     'L1_xattn_bo': (0.0, 0.551),
     'L1_ffn_ln_w': (1.0, 0.6),
     'L1_ffn_ff_ln_w': (1.0, 0.6)}
    factors = {'L1_ffn_wq': 8.0,
     'L1_ffn_wk': 8.0,
     'L1_ffn_wv': 3.215,
     'L1_ffn_wo': 3.15,
     'L1_ffn_gate_w': 8.0,
     'L1_ffn_w1': 8.0,
     'L1_ffn_w3': 8.0,
     'L1_ffn_w2': 8.0}
    for name, (base, spread) in spreads.items():
        noise = np.random.default_rng([zlib.crc32(name.encode()), seed]).standard_normal(out[name].shape)
        drawn = base * np.exp(spread * noise) if base else spread * noise
        out[name] = jnp.asarray(drawn.astype(out[name].dtype))
    for name, factor in factors.items():
        out[name] = (out[name] * factor).astype(out[name].dtype)
    return out
```

```python
import math
from contextlib import ExitStack

import numpy as np

import concourse.bass as bass
from concourse import mybir

F32 = mybir.dt.float32
U32 = mybir.dt.uint32
I32 = mybir.dt.int32
ALU = mybir.AluOpType
ACT = mybir.ActivationFunctionType
AX_X = mybir.AxisListType.X

P = 128
B, S, D = 16, 64, 256
T = B * S
NT = T // P
KC = D // P
E = 8
H0 = 176
HID0 = E * H0
NC0 = HID0 // P
GW = 2 * H0
NG0 = HID0 // GW
NH = 16
HDC = D // NH
HD = 128
KV = 4
FF = 896
NCF = FF // P
HF = FF // 2
WF = KC * 2 * FF + NCF * D
TILES_F = 2 * T // P + E - 1
NSLOT = 3
ROW = D + 1
LN_EPS = 1e-5
NEG = -1.0e30

CONST = {}
_at = 0
for _name, _n in (("ident", P), ("tri", P), ("ones", P), ("cos", HD), ("sin", HD), ("causal", S),
                  ("headmask", 8), ("ebase", E), ("iota_e", E), ("half", 1), ("dest", 2 * NT),
                  ("iota_t", 24), ("fill", ROW)):
    CONST[_name] = (_at, _at + _n)
    _at += _n
NCONST = _at
ROWS = ("bv", "bo", "ln_w", "ff_ln_w")


def after(eng, sem, count):
    if count > 0:
        eng.wait_ge(sem, count)


def build(nc, x, ctx_a, w_b, wg_b, w_c, b_c, rows_c, w_qkv, w_o, gate_d, w_f, consts, out):
    x_rows = x.rearrange("b s d -> (b s) d")
    out_rows = out.rearrange("b s d -> (b s) d")
    slots = nc.dram_tensor("slots", [E * T, ROW], F32)
    slot_rows = slots.ap()
    expert_out = nc.dram_tensor("expert_out", [2 * T + P, D], F32)
    result_rows = expert_out.ap()

    with ExitStack() as stack:
        def sb(name, shape, dt=F32):
            return stack.enter_context(nc.sbuf_tensor(name, shape, dt))

        def sem(name):
            return stack.enter_context(nc.semaphore(name))

        p0 = stack.enter_context(nc.psum_tensor("p0", [P, 512], F32))
        p1 = stack.enter_context(nc.psum_tensor("p1", [P, 512], F32))
        psc = stack.enter_context(nc.psum_tensor("psc", [P, 1024], F32))
        p4 = stack.enter_context(nc.psum_tensor("p4", [P, 512], F32))
        p5 = stack.enter_context(nc.psum_tensor("p5", [P, 512], F32))
        p6 = stack.enter_context(nc.psum_tensor("p6", [P, 512], F32))
        p7 = stack.enter_context(nc.psum_tensor("p7", [P, 512], F32))
        bank = [p0[:, :], p1[:, :], psc[:, 0:512], psc[:, 512:1024], p4[:, :], p5[:, :], p6[:, :], p7[:, :]]

        cst = sb("cst", [P, NCONST])
        X = sb("X", [P, NT * D])
        XP = sb("XP", [P, NT * D])
        WM = sb("WM", [P, NSLOT * WF])
        WQ = sb("WQ", [P, KC * (NH + 2 * KV) * HD])
        rows = sb("rows", [P, len(ROWS) * D])
        wg = sb("wg", [P, KC * E])
        gd = sb("gd", [P, KC * E])
        bqk = sb("bqk", [P, 2 * KC])
        R1 = sb("R1", [P, 9472])
        R2 = sb("R2", [P, 2048 + 1024 + 512])
        xn = sb("xn", [P, 2, D])
        xT = sb("xT", [P, 2, D])
        ctxb = sb("ctxb", [P, 2, 2 * D])
        vs = sb("vs", [P, 2, KV * HD])
        e_sb = sb("e_sb", [P, NH * S])
        bd = sb("bd", [P, 2, NH * P])
        aT = sb("aT", [P, NH * P])
        stat = sb("stat", [P, 2, 6])
        mv = sb("mv", [P, 2, 2])
        ve = sb("ve", [P, 2, 1])
        rstd = sb("rstd", [P, 2, 1])
        ss = sb("ss", [P, 2, 1])
        ms = sb("ms", [P, 2, 1])
        rms = sb("rms", [P, 2, 1])
        mx = sb("mx", [P, NH])
        sums = sb("sums", [P, NH])
        rsum = sb("rsum", [P, NH])
        top = sb("top", [P, 8])
        topi = sb("topi", [P, 8], U32)
        topf = sb("topf", [P, 2])
        dif = sb("dif", [P, 1])
        th = sb("th", [P, 1])
        pr = sb("pr", [P, 2 * NT])
        gates = sb("gates", [P, 2, E])
        gtmp = sb("gtmp", [P, E])
        hot = sb("hot", [P, NT, 2, E])
        cum = sb("cum", [P, NT + 1, E])
        msel = sb("msel", [P, NT, E])
        posf = sb("posf", [P, E])
        pos2 = sb("pos2", [P, 2, E])
        pos = sb("pos", [P, NT, 2], U32)
        tot_i = sb("tot_i", [P, E], I32)
        tl = sb("tl", [P, E])
        cinc = sb("cinc", [P, E])
        cmp_ = sb("cmp_", [P, 24, E])
        tabf = sb("tabf", [P, 8, 24])
        tab = sb("tab", [P, 4, 24], I32)

        def c(name, parts=slice(0, P)):
            a, b = CONST[name]
            return cst[parts, a:b]

        ident = c("ident")
        tile = lambda buf, t: buf[:, t * D:(t + 1) * D]
        bv_row, bo_row, lnw_row, ffw_row = (rows[:, i * D:(i + 1) * D] for i in range(4))
        w12_b = WM[:, 0:KC * 2 * HID0].rearrange("p (k n) -> p k n", k=KC)
        w3_b = WM[:, KC * 2 * HID0:KC * 2 * HID0 + NC0 * D].rearrange("p (c n) -> p c n", c=NC0)
        n_b = KC * 2 * HID0 + NC0 * D
        wc = WM[:, n_b:n_b + 4 * KC * D].rearrange("p (w k n) -> p w k n", w=4, k=KC)
        n_c = n_b + 4 * KC * D
        wo_d = WM[:, n_c:n_c + NH * D].rearrange("p (h n) -> p h n", h=NH)
        wqkv = WQ[:, :].rearrange("p (k n) -> p k n", k=KC)
        sg = R1[:, 0:2048].rearrange("p (q b n) -> p q b n", q=2, b=2)
        act_b = R1[:, 2048:4864].rearrange("p (q n) -> p q n", q=2)
        actT_b = R1[:, 4864:7680].rearrange("p (q n) -> p q n", q=2)
        silu_b = R1[:, 7680:8384].rearrange("p (q n) -> p q n", q=2)
        kbd = R2[:, 0:2048].rearrange("p (c b n) -> p c b n", c=KC, b=2)
        qkT = R2[:, 2048:3072].rearrange("p (q w n) -> p q w n", q=2, w=2)
        cx = R2[:, 3072:3328]
        cxT = R2[:, 3328:3584]
        ra = R1[:, 0:1024].rearrange("p (q n) -> p q n", q=2)
        rb = R1[:, 1024:2048].rearrange("p (q n) -> p q n", q=2)
        qr = R1[:, 2048:4608]
        qT = R1[:, 4608:7168]
        oT = R1[:, 7168:9216]
        h2T = R1[:, 9216:9472]
        h2r = R2[:, 0:4 * ROW].rearrange("p (q k n) -> p q k n", q=2, k=2)
        sq_junk = R2[:, 4 * ROW:4 * ROW + D]
        hs = R1[:, 0:3 * ROW].rearrange("p (q n) -> p q n", q=3)
        hsT = R1[:, 772:772 + 3 * D].rearrange("p (q n) -> p q n", q=3)
        act_f = R1[:, 1540:1540 + 3 * FF].rearrange("p (q n) -> p q n", q=3)
        actT_f = R1[:, 4228:4228 + 3 * FF].rearrange("p (q n) -> p q n", q=3)
        silu_f = R1[:, 6916:6916 + 2 * HF].rearrange("p (q n) -> p q n", q=2)
        ys = R1[:, 7812:7812 + 3 * D].rearrange("p (q n) -> p q n", q=3)
        yk = R2[:, 0:2 * 2 * D].rearrange("p (q k n) -> p q k n", q=2, k=2)

        in_cst, in_x, in_wb, in_wc, in_rows, in_wq, in_wo = (
            sem(n) for n in "in_cst in_x in_wb in_wc in_rows in_wq in_wo".split())
        in_ctx = [sem("in_ctx0"), sem("in_ctx1")]
        filled = sem("filled")
        chain = sem("v_chain")
        stats, g_ve, g_rstd, normed = (sem(n) for n in "stats g_ve g_rstd normed".split())
        res = sem("res")
        a_sc, a_sig, a_out = (sem(n) for n in "a_sc a_sig a_out".split())
        t_x, c_x = sem("t_x"), sem("c_x")
        b_lg, b_log, b_th, b_gate, b_h, b_silu, b_mul, b_t, b_tA, b_tD, b_y, b_dif = (
            sem(n) for n in "b_lg b_log b_th b_gate b_h b_silu b_mul b_t b_tA b_tD b_y b_dif".split())
        c_qk, c_qkc, c_v, c_vc, c_kbd, c_sc, c_av, c_cx, c_ct, c_ctc, c_wo = (
            sem(n) for n in "c_qk c_qkc c_v c_vc c_kbd c_sc c_av c_cx c_ct c_ctc c_wo".split())
        s_free, s_sub, s_exp, s_rs, s_nv, s_ng, s_t, s_cA, s_cD = (
            sem(n) for n in "s_free s_sub s_exp s_rs s_nv s_ng s_t s_cA s_cD".split())
        d_z, d_ss, d_ms, d_rms, d_pj, d_rope, d_radd, d_vc, d_T, d_qc, d_sc, d_av, d_oA, d_oD, d_wo, d_xp = (
            sem(n) for n in ("d_z d_ss d_ms d_rms d_pj d_rope d_radd d_vc d_T d_qc d_sc d_av d_oA "
                             "d_oD d_wo d_xp").split())
        e_ss, e_ms, e_rms, e_h2, e_h2k, e_base, e_T, e_Tc, e_lg, e_dif, e_th, e_sel, e_rank, e_pos = (
            sem(n) for n in ("e_ss e_ms e_rms e_h2 e_h2k e_base e_T e_Tc e_lg e_dif e_th e_sel "
                             "e_rank e_pos").split())
        e_sent = [sem("e_sent0"), sem("e_sent1")]
        e_tot, tables = sem("e_tot"), sem("tables")
        f_in = [sem(f"f_in{i}") for i in range(3)]
        f_w = [sem(f"f_w{i}") for i in range(3)]
        f_sent = [sem(f"f_sent{i}") for i in range(3)]
        f_t, f_tc, f_h, f_silu, f_mul, f_T, f_Tc, f_y, f_ys, f_left = (
            sem(n) for n in "f_t f_tc f_h f_silu f_mul f_T f_Tc f_y f_ys f_left".split())
        g_in = [sem("g_in0"), sem("g_in1")]
        g_sum, g_out = sem("g_sum"), sem("g_out")

        LEAD = 3
        F_PER = ((f_t, 1), (f_tc, 1), (f_h, 4), (f_silu, 2), (f_mul, 2), (f_T, 2), (f_Tc, 2), (f_y, 1), (f_ys, 1),
                 (f_left, 1))

        def at(j, per=1, g=0):
            return per * (j + LEAD) + g + 1

        block = stack.enter_context(nc.Block())

        @block.sync
        def _(sp):
            sp.dma_start(cst[:, :], consts).then_inc(in_cst, 16)
            for t in range(NT):
                sp.dma_start(tile(X, t), x_rows[t * P:(t + 1) * P, :]).then_inc(in_x, 16)
                if t < 2:
                    sp.dma_start(ctxb[:, t, :], ctx_a[t]).then_inc(in_ctx[t], 16)
            sp.dma_start(WM[:, 0:n_b], w_b).then_inc(in_wb, 16)
            sp.dma_start(wg[:, :], wg_b).then_inc(in_wb, 16)
            sp.dma_start(WM[:, n_b:n_c], w_c).then_inc(in_wc, 16)
            sp.dma_start(bqk[:, :], b_c).then_inc(in_wc, 16)
            sp.dma_start(rows[:, :], rows_c).then_inc(in_rows, 16)
            for t in range(2, NT):
                after(sp, a_out, 2 * (t - 1))
                sp.dma_start(ctxb[:, t % 2, :], ctx_a[t]).then_inc(in_ctx[t % 2], 16)
            sp.dma_start(WQ[:, :], w_qkv).then_inc(in_wq, 16)
            sp.dma_start(gd[:, :], gate_d).then_inc(in_wq, 16)
            sp.dma_start(WM[:, n_c:n_c + NH * D], w_o).then_inc(in_wo, 16)
            sp.wait_ge(in_cst, 16)
            fill = cst[:, CONST["fill"][0]:CONST["fill"][1]]
            for e in range(E):
                for r in range(T // P):
                    r0 = e * T + r * P
                    sp.dma_start(slot_rows[r0:r0 + P, :], fill).then_inc(filled, 16)
            for t in range(NT):
                after(sp, a_out, 2 * (min(t + NT - 2, NT - 1) + 1))
                after(sp, c_v, t - 1)
                sp.dma_start(ctxb[:, t % 2, D:], ctx_a[t, :, D:]).then_inc(in_ctx[t % 2], 16)

            sp.wait_ge(tables, 1)
            for u in range(2):
                sp.wait_ge(e_sent[u], 32 * (NT // 2))

            def load(j):
                base = sp.value_load(tab[0:1, 0, bass.ds(j, 1)], min_val=0, max_val=E * T - P)
                wrow = sp.value_load(tab[0:1, 1, bass.ds(j, 1)], min_val=0, max_val=(E - 1) * P)
                slot = sp.value_load(tab[0:1, 2, bass.ds(j, 1)], min_val=0, max_val=(NSLOT - 1) * WF)
                fresh = sp.value_load(tab[0:1, 3, bass.ds(j, 1)], min_val=0, max_val=1)
                return base, wrow, slot, fresh

            with sp.Fori(0, TILES_F // 3) as i:
                for u in range(3):
                    j = 3 * i + u
                    base, wrow, slot, fresh = load(j)
                    sp.wait_ge(f_y, at(j - 3))
                    sp.wait_ge(f_left, at(j - 3))
                    sp.dma_start(hs[:, u, :], slot_rows[bass.ds(base, P), :]).then_inc(f_in[u], 16)
                    sp.dma_start(WM[:, bass.ds(slot, WF)], w_f[bass.ds(wrow, P), :],
                                 cond=(fresh > 0)).then_inc(f_w[u], 16)
            for j in range(TILES_F // 3 * 3, TILES_F):
                u = j % 3
                base, wrow, slot, fresh = load(j)
                sp.wait_ge(f_y, at(j - 3))
                sp.wait_ge(f_left, at(j - 3))
                sp.dma_start(hs[:, u, :], slot_rows[bass.ds(base, P), :]).then_inc(f_in[u], 16)
                sp.dma_start(WM[:, bass.ds(slot, WF)], w_f[bass.ds(wrow, P), :],
                             cond=(fresh > 0)).then_inc(f_w[u], 16)

            sp.wait_ge(f_left, at(TILES_F - 1))
            for t in range(NT):
                after(sp, g_sum, t - 1)
                sp.dma_start(yk[:, t % 2], result_rows[2 * t * P:2 * (t + 1) * P, :]
                             .rearrange("(p k) n -> p k n", k=2)).then_inc(g_in[t % 2], 16)
                if t:
                    sp.wait_ge(g_sum, t)
                    sp.dma_start(out_rows[(t - 1) * P:t * P, :], tile(X, t - 1)).then_inc(g_out, 16)
            sp.wait_ge(g_sum, NT)
            sp.dma_start(out_rows[(NT - 1) * P:, :], tile(X, NT - 1)).then_inc(g_out, 16)
            sp.wait_ge(g_out, 16 * NT)

        @block.tensor
        def _(pe):
            pe.wait_ge(in_cst, 16)

            def a_scores(t):
                q = t % 2
                pe.wait_ge(in_ctx[q], 16 * (t // 2 + 1))
                pe.wait_ge(normed, t + 1)
                for b in range(2):
                    after(pe, a_sig, 2 * (t - 2) + b + 1)
                    r = slice(S * b, S * b + S)
                    for k in range(KC):
                        mm = pe.matmul(bank[2 * q + b][:, k * D:(k + 1) * D], xn[r, q, k * P:(k + 1) * P],
                                       ctxb[r, q, 0:D], start=True, stop=True)
                    mm.then_inc(a_sc, 1)

            def a_outs(t):
                q = t % 2
                after(pe, res, t - 1)
                for b in range(2):
                    pe.wait_ge(a_sig, 2 * t + b + 1)
                    for k in range(KC):
                        mm = pe.matmul(bank[4 + q][S * b:S * b + S, 0:D],
                                       ctxb[:, q, D + k * P + S * b:D + k * P + S * b + S],
                                       sg[:, q, b, k * D:(k + 1) * D], start=(k == 0), stop=(k == KC - 1))
                    mm.then_inc(a_out, 1)

            for s in range(NT + 1):
                if s < NT:
                    a_scores(s)
                if s >= 1:
                    a_outs(s - 1)

            def turn_x(m, dst, guard):
                pe.wait_ge(normed, NT + m + 1)
                after(pe, *guard)
                for k in range(KC):
                    mm = pe.transpose(dst[:, k * P:(k + 1) * P], xn[:, m % 2, k * P:(k + 1) * P], ident)
                mm.then_inc(t_x, 1)

            def b_gates(t):
                pe.wait_ge(c_x, t + 1)
                for k in range(KC):
                    mm = pe.matmul(bank[5][:, D:D + E], xT[:, t % 2, k * P:(k + 1) * P],
                                   wg[:, k * E:(k + 1) * E], start=(k == 0), stop=(k == KC - 1))
                mm.then_inc(b_lg, 1)

            def b_hidden(t, g):
                pe.wait_ge(c_x, t + 1)
                n = NG0 * t + g
                for w, free in ((0, b_silu), (1, b_mul)):
                    after(pe, free, n - 1)
                    for k in range(KC):
                        mm = pe.matmul(bank[2 * w + g % 2][:, 0:GW], xT[:, t % 2, k * P:(k + 1) * P],
                                       w12_b[:, k, w * HID0 + g * GW:w * HID0 + (g + 1) * GW],
                                       start=(k == 0), stop=(k == KC - 1))
                    mm.then_inc(b_h, 1)

            def b_turn(t, u):
                chunks = range(4 * u, min(4 * u + 4, NC0))
                pe.wait_ge(b_mul, NG0 * t + u + 2)
                after(pe, *((b_tA, 2 * t), (b_tD, t), (b_tA, 2 * t + 1))[u])
                for i, ch in enumerate(chunks):
                    mm = pe.transpose(bank[6 + u % 2][:, i * P:(i + 1) * P],
                                      act_b[:, t % 2, ch * P:(ch + 1) * P], ident)
                mm.then_inc(b_t, 1)

            def b_down(t):
                pe.wait_ge(b_tA, 2 * t + 2)
                pe.wait_ge(b_tD, t + 1)
                after(pe, res, NT + t)
                for ch in range(NC0):
                    mm = pe.matmul(bank[4][:, 0:D], actT_b[:, t % 2, ch * P:(ch + 1) * P], w3_b[:, ch, :],
                                   start=(ch == 0), stop=(ch == NC0 - 1))
                mm.then_inc(b_y, 1)

            pe.wait_ge(in_wb, 32)
            pe.wait_ge(res, NT)
            for s in range(NT + 2):
                t0, t1, t2 = s, s - 1, s - 2
                main = 0 <= t1 < NT
                if main:
                    b_hidden(t1, 0)
                if t2 >= 0:
                    b_turn(t2, 2)
                if main:
                    b_hidden(t1, 1)
                if t2 >= 0:
                    b_down(t2)
                if t0 < NT:
                    turn_x(t0, bank[5], (b_log, t0))
                if main:
                    b_hidden(t1, 2)
                    b_turn(t1, 0)
                if t0 < NT:
                    b_gates(t0)
                if main:
                    b_hidden(t1, 3)
                    b_turn(t1, 1)

            def turn_attn(m, u, guard):
                pe.wait_ge(s_nv, m + 1)
                pe.wait_ge(s_ng, m + 1)
                for g in guard:
                    after(pe, *g)
                for i in range(4):
                    h = 4 * u + i
                    mm = pe.transpose(bank[7 - u % 2][:, i * P:(i + 1) * P], bd[:, m % 2, h * P:(h + 1) * P], ident)
                mm.then_inc(s_t, 1)

            def c_project(t):
                m, q = NT + t, t % 2
                pe.wait_ge(c_x, m + 1)
                pe.wait_ge(in_ctx[q], 16 * ((NT + t) // 2 + 1))
                after(pe, c_qkc, 4 * t)
                for w in range(2):
                    for n in range(KC):
                        for k in range(KC):
                            rhs = xT[:, m % 2, k * P:(k + 1) * P] if w == 0 else ctxb[:, q, D + k * P:D + (k + 1) * P]
                            mm = pe.matmul(bank[1][:, (2 * w + n) * P:(2 * w + n + 1) * P],
                                           wc[:, w, k, n * P:(n + 1) * P], rhs, start=(k == 0), stop=(k == KC - 1))
                mm.then_inc(c_qk, 1)
                for k in range(KC):
                    mm = pe.matmul(bank[0][:, D:2 * D], ctxb[:, q, D + k * P:D + (k + 1) * P], wc[:, 2, k, :],
                                   start=(k == 0), stop=(k == KC - 1))
                mm.then_inc(c_v, 1)

            def c_scores(t):
                q = t % 2
                pe.wait_ge(c_kbd, 4 * t + 4)
                after(pe, s_free, t)
                for k in range(KC):
                    for b in range(2):
                        mm = pe.matmul(bank[2 + k][S * b:S * b + S, :], qkT[:, q, 0, k * P + S * b:k * P + S * b + S],
                                       kbd[:, k, b, :], start=True, stop=True)
                mm.then_inc(c_sc, 1)

            def c_values(t):
                q = t % 2
                pe.wait_ge(c_vc, t + 1)
                after(pe, c_cx, t)
                for u in range(4):
                    after(pe, (s_cA, s_cD)[u % 2], 2 * t + u // 2 + 1)
                    for h in range(4 * u, 4 * u + 4):
                        mm = pe.matmul(bank[4][:, h * HDC:(h + 1) * HDC], aT[:, h * P:(h + 1) * P],
                                       vs[:, q, h * HDC:(h + 1) * HDC], start=True, stop=True)
                mm.then_inc(c_av, 1)

            def c_turn(t):
                pe.wait_ge(c_cx, t + 1)
                after(pe, res, 2 * NT + t)
                for k in range(KC):
                    mm = pe.transpose(bank[5][:, k * P:(k + 1) * P], cx[:, k * P:(k + 1) * P], ident)
                mm.then_inc(c_ct, 1)

            def c_outs(t):
                pe.wait_ge(c_ctc, t + 1)
                for k in range(KC):
                    mm = pe.matmul(bank[5][:, D:2 * D], cxT[:, k * P:(k + 1) * P], wc[:, 3, k, :],
                                   start=(k == 0), stop=(k == KC - 1))
                mm.then_inc(c_wo, 1)

            pe.wait_ge(in_wc, 32)
            pe.wait_ge(res, 2 * NT)
            for s in range(NT + 2):
                t0, t1, t2 = s, s - 1, s - 2
                if 0 <= t1 < NT:
                    c_scores(t1)
                if t2 >= 0:
                    for u in range(4):
                        turn_attn(t2, u, [((s_cA, s_cD)[u % 2], 2 * t2 + u // 2)])
                if t0 < NT:
                    turn_x(NT + t0, bank[0], (c_vc, t0))
                if t2 >= 0:
                    c_values(t2)
                if t0 < NT:
                    c_project(t0)
                if t2 >= 0:
                    c_turn(t2)
                    c_outs(t2)

            def d_project(t, g):
                m = 2 * NT + t
                if g == 0:
                    pe.wait_ge(c_x, m + 1)
                after(pe, *((d_xp, t - 1), (e_pos, t - 2), (d_rope, 5 * t + 1), (d_rope, 5 * t + 2),
                            (d_rope, 5 * t + 3), (d_rope, 5 * t + 4))[g])
                for k in range(KC):
                    mm = pe.matmul(bank[g % 2], xT[:, m % 2, k * P:(k + 1) * P],
                                   wqkv[:, k, g * 512:(g + 1) * 512], start=(k == 0), stop=(k == KC - 1))
                mm.then_inc(d_pj, 1)

            def d_turn(t, g):
                pe.wait_ge(d_radd, 5 * t + g + 1)
                after(pe, *((c_x, 2 * NT + t + 1), (e_Tc, t - 2), (d_qc, 5 * t + 1), (d_qc, 5 * t + 2),
                            (d_qc, 5 * t + 3))[g])
                if g < 2:
                    after(pe, (s_cD, s_cA)[g], 2 * (NT + t - 1))
                for i in range(4):
                    mm = pe.transpose(bank[6 + g % 2][:, i * P:(i + 1) * P],
                                      qr[:, g * 512 + i * P:g * 512 + (i + 1) * P], ident)
                mm.then_inc(d_T, 1)

            def d_scores(t):
                pe.wait_ge(d_qc, 5 * t + 5)
                after(pe, s_free, NT + t)
                for h in range(NH):
                    kv = NH + h // (NH // KV)
                    for b in range(2):
                        mm = pe.matmul(psc[S * b:S * b + S, h * S:(h + 1) * S],
                                       qT[:, h * P + S * b:h * P + S * b + S],
                                       qT[:, kv * P + S * b:kv * P + S * b + S], start=True, stop=True)
                mm.then_inc(d_sc, 1)

            def d_values(t):
                m = NT + t
                pe.wait_ge(d_vc, t + 1)
                for kv in range(KV):
                    after(pe, (s_cA, s_cD)[kv % 2], 2 * m + kv // 2 + 1)
                    after(pe, (d_oA, d_oD)[kv % 2], 2 * t + kv // 2)
                    pe.matmul(bank[4 + kv % 2], vs[:, m % 2, kv * HD:(kv + 1) * HD],
                              aT[:, kv * 512:(kv + 1) * 512], start=True, stop=True).then_inc(d_av, 1)

            def d_outs(t, last_rope):
                after(pe, d_rope, last_rope)
                for h in range(NH):
                    if h % 4 == 0:
                        after(pe, (d_oA, d_oD)[h // 4 % 2], 2 * t + h // 8 + 1)
                    mm = pe.matmul(bank[0][:, 0:D], oT[:, h * P:(h + 1) * P], wo_d[:, h, :],
                                   start=(h == 0), stop=(h == NH - 1))
                mm.then_inc(d_wo, 1)

            def e_turn(t, guard):
                pe.wait_ge(e_h2, t + 1)
                after(pe, s_cA, guard)
                for k in range(KC):
                    mm = pe.transpose(bank[7][:, k * P:(k + 1) * P], h2r[:, t % 2, 0, k * P:(k + 1) * P], ident)
                mm.then_inc(e_T, 1)

            def e_logits(t, guard):
                pe.wait_ge(e_Tc, t + 1)
                after(pe, d_vc, guard)
                after(pe, e_pos, t)
                for k in range(KC):
                    mm = pe.matmul(bank[1][:, 0:E], h2T[:, k * P:(k + 1) * P], gd[:, k * E:(k + 1) * E],
                                   start=(k == 0), stop=(k == KC - 1))
                mm.then_inc(e_lg, 1)

            def e_ranks(t):
                pe.wait_ge(e_sel, t + 1)
                pe.matmul(bank[1][:, 8:8 + E], c("ones"), cum[:, t, :], start=True, stop=False)
                pe.matmul(bank[1][:, 8:8 + E], c("tri"), msel[:, t, :], start=False, stop=True).then_inc(e_rank, 1)

            pe.wait_ge(in_wq, 32)
            pe.wait_ge(in_wo, 16)
            pe.wait_ge(res, 3 * NT)
            for s in range(NT + 4):
                t0, t1, t2, t3, t4 = s, s - 1, s - 2, s - 3, s - 4
                main, attn = 0 <= t1 < NT, 0 <= t2 < NT
                if t4 >= 0:
                    e_ranks(t4)
                if main:
                    for g in range(6):
                        d_project(t1, g)
                        if g >= 2:
                            d_turn(t1, g - 2)
                if attn:
                    turn_attn(NT + t2, 0, [(d_qc, min(5 * t1 + 4, 5 * NT) if main or t1 == NT else 0),
                                           (s_cA, 2 * (NT + t2)), (e_Tc, t2 - 1)])
                if main:
                    d_turn(t1, 4)
                if attn:
                    turn_attn(NT + t2, 1, [(d_qc, min(5 * t1 + 5, 5 * NT)), (s_cD, 2 * (NT + t2))])
                if main:
                    d_scores(t1)
                if attn:
                    turn_attn(NT + t2, 2, [(s_cA, 2 * (NT + t2) + 1)])
                    turn_attn(NT + t2, 3, [(s_cD, 2 * (NT + t2) + 1)])
                    d_values(t2)
                if 0 <= t3 < NT:
                    e_turn(t3, min(2 * (NT + t2) + 2, 4 * NT))
                if t0 < NT:
                    turn_x(2 * NT + t0, bank[6], (s_cD, 2 * (NT + t2) + 2 if attn else 0))
                if attn:
                    d_outs(t2, min(5 * t1 + 5, 5 * NT))
                if 0 <= t3 < NT:
                    e_logits(t3, min(t1 + 1, NT))
            pe.wait_ge(e_pos, NT)
            pe.matmul(bank[1][:, 8:8 + E], c("ones"), cum[:, NT, :], start=True, stop=True).then_inc(e_tot, 1)

            def f_turn_x(j, u, k3):
                pe.wait_ge(f_in[u], 16 * k3 + 16)
                pe.wait_ge(f_tc, at(j - 1))
                for k in range(KC):
                    mm = pe.transpose(bank[5][:, k * P:(k + 1) * P], hs[:, u, k * P:(k + 1) * P], ident)
                mm.then_inc(f_t, 1)

            def f_hidden(j, u, k3, n, slot):
                if n == 0:
                    pe.wait_ge(f_tc, at(j))
                    pe.wait_ge(f_w[u], 16 * k3 + 16)
                for w, free in ((0, f_silu), (1, f_mul)):
                    pe.wait_ge(free, at(j - 1, 2, n))
                    for k in range(KC):
                        o = (2 * k + w) * FF + n * HF
                        mm = pe.matmul(bank[2 * w + n][:, 0:HF], hsT[:, u, k * P:(k + 1) * P],
                                       WM[:, bass.ds(slot + o, HF)], start=(k == 0), stop=(k == KC - 1))
                    mm.then_inc(f_h, 1)

            def f_turn(j, u, n):
                chunks = (range(0, 3), range(3, NCF))[n]
                pe.wait_ge(f_mul, at(j, 2, n))
                pe.wait_ge(f_Tc, at(j - 1, 2, n))
                for i, ch in enumerate(chunks):
                    mm = pe.transpose(bank[6 + n][:, i * P:(i + 1) * P], act_f[:, u, ch * P:(ch + 1) * P], ident)
                mm.then_inc(f_T, 1)

            def f_down(j, u, slot):
                pe.wait_ge(f_Tc, at(j, 2, 1))
                pe.wait_ge(f_ys, at(j - 1))
                for ch in range(NCF):
                    mm = pe.matmul(bank[4][:, 0:D], actT_f[:, u, ch * P:(ch + 1) * P],
                                   WM[:, bass.ds(slot + KC * 2 * FF + ch * D, D)],
                                   start=(ch == 0), stop=(ch == NCF - 1))
                mm.then_inc(f_y, 1)

            def f_step(s, sx, first=False, head=True, main=True, tail=True):
                def of(lag):
                    k3, u = sx[0], sx[1] - lag
                    return s - lag, u % 3, k3 + u // 3
                j0, u0, k0 = of(0)
                j1, u1, k1 = of(1)
                j2, u2, k2 = of(2)
                if main:
                    slot1 = pe.value_load(tab[0:1, 2, bass.ds(j1, 1)], min_val=0, max_val=(NSLOT - 1) * WF)
                    f_hidden(j1, u1, k1, 0, slot1)
                if tail:
                    f_turn(j2, u2, 1)
                if head:
                    f_turn_x(j0, u0, k0)
                if main:
                    f_hidden(j1, u1, k1, 1, slot1)
                if tail:
                    slot2 = pe.value_load(tab[0:1, 2, bass.ds(j2, 1)], min_val=0, max_val=(NSLOT - 1) * WF)
                    f_down(j2, u2, slot2)
                if main:
                    f_turn(j1, u1, 0)

            pe.wait_ge(tables, 1)
            f_step(0, (0, 0), main=False, tail=False)
            f_step(1, (0, 1), tail=False)
            with pe.Fori(0, (TILES_F - 2) // 3) as i:
                for u in range(3):
                    f_step(3 * i + 2 + u, (i + (2 + u) // 3, (2 + u) % 3))
            f_step(TILES_F, (TILES_F // 3, TILES_F % 3), head=False)
            f_step(TILES_F + 1, ((TILES_F + 1) // 3, (TILES_F + 1) % 3), head=False, main=False)

        @block.scalar
        def _(act):
            for t in range(NT):
                for b in range(2):
                    act.wait_ge(a_sc, 2 * t + b + 1)
                    after(act, a_out, 2 * (t - 2) + b + 1)
                    nc.scalar.activation(sg[:, t % 2, b, :], bank[2 * (t % 2) + b], ACT.Sigmoid,
                                         scale=1.0 / math.sqrt(S)).then_inc(a_sig, 1)

            def copy_x(m, src, free):
                act.wait_ge(t_x, m + 1)
                after(act, *free)
                nc.scalar.copy(xT[:, m % 2, :], src[:, 0:D]).then_inc(c_x, 1)

            def b_silus(t, g):
                n = NG0 * t + g
                act.wait_ge(b_h, 2 * n + 1)
                after(act, b_mul, n - 1)
                nc.scalar.activation(silu_b[:, g % 2, :], bank[g % 2][:, 0:GW], ACT.Silu).then_inc(b_silu, 1)

            def b_copy(t, u):
                act.wait_ge(b_t, 3 * t + u + 1)
                after(act, b_y, t - 1)
                n = (min(4 * u + 4, NC0) - 4 * u) * P
                nc.scalar.copy(actT_b[:, t % 2, 4 * u * P:4 * u * P + n], bank[6][:, 0:n]).then_inc(b_tA, 1)

            for s in range(NT + 2):
                t0, t1, t2 = s, s - 1, s - 2
                main = 0 <= t1 < NT
                if main:
                    b_silus(t1, 0)
                if t2 >= 0:
                    b_copy(t2, 2)
                if main:
                    b_silus(t1, 1)
                if t0 < NT:
                    copy_x(t0, bank[5], (b_h, 2 * NG0 * (t0 - 1)))
                if main:
                    b_silus(t1, 2)
                    b_copy(t1, 0)
                if t0 < NT:
                    act.wait_ge(b_dif, t0 + 1)
                    nc.scalar.activation(th[:, :], dif[:, :], ACT.Tanh, scale=0.5).then_inc(b_th, 1)
                if main:
                    b_silus(t1, 3)

            def exps(m, scale):
                act.wait_ge(s_sub, m + 1)
                nc.scalar.activation(e_sb[:, :], e_sb[:, :], ACT.Exp, scale=scale).then_inc(s_exp, 1)

            def copy_attn(m, u, free):
                act.wait_ge(s_t, 4 * m + u + 1)
                after(act, *free)
                nc.scalar.copy(aT[:, u * 512:(u + 1) * 512], bank[7]).then_inc(s_cA, 1)

            act.wait_ge(in_wc, 32)
            for s in range(NT + 2):
                t0, t1, t2 = s, s - 1, s - 2
                if t2 >= 0:
                    copy_attn(t2, 0, (c_av, t2))
                if 0 <= t1 < NT:
                    exps(t1, 1.0 / math.sqrt(HDC))
                if t2 >= 0:
                    copy_attn(t2, 2, (c_av, t2))
                if t0 < NT:
                    copy_x(NT + t0, bank[0], (c_qk, t0 - 1))
                if t2 >= 0:
                    act.wait_ge(c_av, t2 + 1)
                    after(act, c_ct, t2)
                    nc.scalar.copy(cx, bank[4][:, 0:D]).then_inc(c_cx, 1)
                if t0 < NT:
                    act.wait_ge(c_qk, t0 + 1)
                    after(act, c_sc, t0 - 1)
                    after(act, c_kbd, 4 * (t0 - 1))
                    for w in range(2):
                        for n in range(KC):
                            nc.scalar.activation(qkT[:, t0 % 2, w, n * P:(n + 1) * P],
                                                 bank[1][:, (2 * w + n) * P:(2 * w + n + 1) * P], ACT.Identity,
                                                 bias=bqk[:, 2 * w + n:2 * w + n + 1]).then_inc(c_qkc, 1)
                if t2 >= 0:
                    act.wait_ge(c_ct, t2 + 1)
                    after(act, c_wo, t2)
                    nc.scalar.copy(cxT, bank[5][:, 0:D]).then_inc(c_ctc, 1)

            for s in range(NT + 4):
                t0, t1, t2, t3 = s, s - 1, s - 2, s - 3
                main, attn = 0 <= t1 < NT, 0 <= t2 < NT
                if t0 < NT:
                    act.wait_ge(d_z, t0 + 1)
                    after(act, d_ms, t0 - 1)
                    after(act, d_ss, t0)
                    after(act, e_ss, min(t3, NT))
                    nc.scalar.activation(sq_junk, tile(XP, t0), ACT.Square, accum_out=ss[:, t0 % 2, :]).then_inc(d_ss, 1)
                if main:
                    for g in range(4):
                        act.wait_ge(d_T, 5 * t1 + g + 1)
                        after(act, d_sc, t1)
                        nc.scalar.copy(qT[:, g * 512:(g + 1) * 512], bank[6 + g % 2]).then_inc(d_qc, 1)
                        if g == 3:
                            act.wait_ge(d_pj, 6 * t1 + 6)
                            after(act, d_av, 4 * (t1 - 1))
                            nc.scalar.copy(vs[:, t1 % 2, :], bank[1]).then_inc(d_vc, 1)
                if attn:
                    copy_attn(NT + t2, 0, (d_av, 4 * t2))
                if main:
                    act.wait_ge(d_T, 5 * t1 + 5)
                    nc.scalar.copy(qT[:, 4 * 512:5 * 512], bank[6]).then_inc(d_qc, 1)
                if attn:
                    copy_attn(NT + t2, 2, (d_av, 4 * t2))
                if main:
                    exps(NT + t1, 1.0 / math.sqrt(HD))
                if attn:
                    for i in range(2):
                        act.wait_ge(d_av, 4 * t2 + 2 * i + 1)
                        after(act, d_wo, t2)
                        nc.scalar.copy(oT[:, 2 * i * 512:(2 * i + 1) * 512], bank[4]).then_inc(d_oA, 1)
                if 0 <= t3 < NT:
                    act.wait_ge(e_h2, t3 + 1)
                    nc.scalar.copy(h2r[:, t3 % 2, 1, 0:D], h2r[:, t3 % 2, 0, 0:D]).then_inc(e_h2k, 1)
                    act.wait_ge(e_T, t3 + 1)
                    after(act, e_lg, t3)
                    nc.scalar.copy(h2T, bank[7][:, 0:D]).then_inc(e_Tc, 1)
                if t0 < NT:
                    copy_x(2 * NT + t0, bank[6], (d_pj, 6 * (t0 - 1)))
                if attn:
                    act.wait_ge(d_xp, t2 + 1)
                    after(act, e_ms, t2)
                    act.wait_ge(d_ss, min(t0 + 1, NT))
                    nc.scalar.activation(sq_junk, tile(XP, t2), ACT.Square, accum_out=th[:, :]).then_inc(e_ss, 1)
                if 0 <= t3 < NT:
                    act.wait_ge(e_dif, t3 + 1)
                    nc.scalar.activation(gtmp[:, 0:1], dif[:, :], ACT.Tanh, scale=0.5).then_inc(e_th, 1)

            def f_copy_x(j, u):
                act.wait_ge(f_t, at(j))
                act.wait_ge(f_h, at(j - 3, 4, 3))
                nc.scalar.copy(hsT[:, u, :], bank[5][:, 0:D]).then_inc(f_tc, 1)

            def f_silus(j, n):
                act.wait_ge(f_h, at(j, 4, 2 * n))
                act.wait_ge(f_mul, at(j - 1, 2, n))
                nc.scalar.activation(silu_f[:, n, :], bank[n][:, 0:HF], ACT.Silu).then_inc(f_silu, 1)

            def f_copy(j, u, n):
                act.wait_ge(f_T, at(j, 2, n))
                act.wait_ge(f_y, at(j - 3))
                o, w = ((0, 3 * P), (3 * P, 4 * P))[n]
                nc.scalar.copy(actT_f[:, u, o:o + w], bank[6 + n][:, 0:w]).then_inc(f_Tc, 1)

            def f_step(s, r, head=True, main=True, tail=True):
                if main:
                    f_silus(s - 1, 0)
                if tail:
                    f_copy(s - 2, (r - 2) % 3, 1)
                if head:
                    f_copy_x(s, r % 3)
                if main:
                    f_silus(s - 1, 1)
                    f_copy(s - 1, (r - 1) % 3, 0)

            f_step(0, 0, main=False, tail=False)
            f_step(1, 1, tail=False)
            with act.Fori(0, (TILES_F - 2) // 3) as i:
                for u in range(3):
                    f_step(3 * i + 2 + u, 2 + u)
            f_step(TILES_F, TILES_F, head=False)
            f_step(TILES_F + 1, TILES_F + 1, head=False, main=False)

        @block.vector
        def _(dve):
            links = [0]

            def link(ins):
                links[0] += 1
                ins.then_inc(chain, 1)
                dve.wait_ge(chain, links[0])

            link(nc.vector.memset(bd[:, :, :], 0.0))
            link(nc.vector.memset(cum[:, 0, :], 0.0))

            def norm_stats(n):
                t, q = n % NT, n % 2
                if n < NT:
                    dve.wait_ge(in_x, 16 * NT)
                else:
                    dve.wait_ge(res, n - NT + 1)
                after(dve, g_ve, n - 1)
                link(nc.vector.bn_stats(stat[:, q, :], tile(X, t)))
                nc.vector.bn_aggr(mv[:, q, :], stat[:, q, :]).then_inc(stats, 1)

            def norm_apply(n, dst, done):
                t, q = n % NT, n % 2
                dve.wait_ge(g_rstd, n + 1)
                dve.wait_ge(stats, n + 1)
                nc.vector.tensor_scalar(dst, tile(X, t), mv[:, q, 0:1], rstd[:, q, :],
                                        ALU.subtract, ALU.mult).then_inc(done, 1)

            dve.wait_ge(in_cst, 16)
            for s in range(NT + 1):
                if s < NT:
                    norm_stats(s)
                    after(dve, a_sc, 2 * (s - 1))
                    norm_apply(s, xn[:, s % 2, :], normed)
                if s >= 1:
                    t = s - 1
                    dve.wait_ge(a_out, 2 * t + 2)
                    nc.vector.tensor_tensor(tile(X, t), tile(X, t), bank[4 + t % 2][:, 0:D], ALU.add).then_inc(res, 1)

            def top_two(logits, ready, read, dif_done, th_src, th_done, t, prob):
                dve.wait_ge(ready, t + 1)
                link(nc.vector.max(top[:, :], logits))
                ins = nc.vector.max_index(topi[:, :], top[:, :], logits)
                if read is not None:
                    ins.then_inc(read, 1)
                    dve.wait_ge(read, t + 1)
                else:
                    link(ins)
                nc.vector.tensor_tensor(dif[:, :], top[:, 1:2], top[:, 0:1], ALU.subtract).then_inc(dif_done, 1)
                link(nc.vector.tensor_copy(topf[:, :], topi[:, 0:2]))
                dve.wait_ge(th_done, t + 1)
                link(nc.vector.tensor_scalar(prob[:, 0:1], th_src, -0.5, 0.5, ALU.mult, ALU.add))
                link(nc.vector.tensor_scalar(prob[:, 1:2], th_src, 0.5, 0.5, ALU.mult, ALU.add))

            def b_gating(t):
                prob = pr[:, 0:2]
                top_two(bank[5][:, D:D + E], b_lg, b_log, b_dif, th[:, :], b_th, t, prob)
                link(nc.vector.tensor_scalar(gtmp[:, :], c("iota_e"), topf[:, 0:1], prob[:, 0:1],
                                             ALU.is_equal, ALU.mult))
                link(nc.vector.tensor_scalar(gates[:, t % 2, :], c("iota_e"), topf[:, 1:2], prob[:, 1:2],
                                             ALU.is_equal, ALU.mult))
                link(nc.vector.tensor_tensor(gates[:, t % 2, :], gates[:, t % 2, :], gtmp[:, :], ALU.add))

            def b_muls(t, g):
                n = NG0 * t + g
                dve.wait_ge(b_silu, n + 1)
                dve.wait_ge(b_h, 2 * n + 2)
                after(dve, b_t, 3 * (t - 1))
                for i in range(2):
                    e = 2 * g + i
                    ins = nc.vector.scalar_tensor_tensor(
                        out=act_b[:, t % 2, e * H0:(e + 1) * H0], in0=silu_b[:, g % 2, i * H0:(i + 1) * H0],
                        scalar=gates[:, t % 2, e:e + 1], in1=bank[2 + g % 2][:, i * H0:(i + 1) * H0],
                        op0=ALU.mult, op1=ALU.mult)
                ins.then_inc(b_mul, 1)

            for s in range(NT + 2):
                t0, t1, t2 = s, s - 1, s - 2
                main = 0 <= t1 < NT
                if t0 < NT:
                    norm_stats(NT + t0)
                    after(dve, t_x, t0 - 1)
                    norm_apply(NT + t0, xn[:, t0 % 2, :], normed)
                if main:
                    b_muls(t1, 0)
                    b_muls(t1, 1)
                if t2 >= 0:
                    dve.wait_ge(b_y, t2 + 1)
                    nc.vector.tensor_tensor(tile(X, t2), tile(X, t2), bank[4][:, 0:D], ALU.add).then_inc(res, 1)
                if main:
                    b_muls(t1, 2)
                if t0 < NT:
                    b_gating(t0)
                if main:
                    b_muls(t1, 3)
                    dve.wait_ge(b_t, 3 * t1 + 2)
                    after(dve, b_y, t1 - 1)
                    nc.vector.tensor_copy(actT_b[:, t1 % 2, 512:1024], bank[7]).then_inc(b_tD, 1)

            sc_v = psc[:, :].rearrange("p (h k) -> p h k", h=NH)
            e_v = e_sb[:, :].rearrange("p (h k) -> p h k", h=NH)

            def over_keys(v, parts=slice(0, P)):
                return v[parts, :].rearrange("p (h o) -> p h o", o=1).to_broadcast([v[parts, :].shape[0], NH, S])

            def softmax_shift(m, ready, count, causal):
                dve.wait_ge(ready, count)
                after(dve, s_nv, m)
                after(dve, s_ng, m)
                src = sc_v
                if causal:
                    mask = c("causal").rearrange("p (o k) -> p o k", o=1).to_broadcast([P, NH, S])
                    nc.vector.tensor_tensor(e_v, sc_v, mask, ALU.add).then_inc(s_free, 1)
                    dve.wait_ge(s_free, m + 1)
                    src = e_v
                link(nc.vector.tensor_reduce(mx[:, :], src, AX_X, ALU.max))
                ins = nc.vector.tensor_tensor(e_v, src, over_keys(mx), ALU.subtract)
                if not causal:
                    ins.then_inc(s_free, 1)
                    dve.wait_ge(s_free, m + 1)
                    ins = nc.vector.tensor_copy(mx[:, 0:1], mx[:, 0:1])
                ins.then_inc(s_sub, 1)

            def softmax_weights(m):
                dve.wait_ge(s_exp, m + 1)
                link(nc.vector.tensor_reduce(sums[:, :], e_v, AX_X, ALU.add))
                after(dve, s_ng, m)
                nc.vector.reciprocal(rsum[:, :], sums[:, :]).then_inc(s_rs, 1)
                dve.wait_ge(s_rs, m + 1)
                after(dve, s_t, 4 * (m - 1))
                v = bd[0:S, m % 2, :].rearrange("p (h k) -> p h k", h=NH)[:, :, 0:S]
                nc.vector.tensor_tensor(v, e_v[0:S], over_keys(rsum, slice(0, S)), ALU.mult).then_inc(s_nv, 1)

            def copy_attn(m, u, free):
                dve.wait_ge(s_t, 4 * m + u + 1)
                after(dve, *free)
                nc.vector.tensor_copy(aT[:, u * 512:(u + 1) * 512], bank[6]).then_inc(s_cD, 1)

            dve.wait_ge(in_rows, 16)
            for s in range(NT + 2):
                t0, t1, t2 = s, s - 1, s - 2
                if t0 < NT:
                    norm_stats(2 * NT + t0)
                if 0 <= t1 < NT:
                    softmax_shift(t1, c_sc, t1 + 1, False)
                if t0 < NT:
                    after(dve, t_x, NT + t0 - 1)
                    norm_apply(2 * NT + t0, xn[:, t0 % 2, :], normed)
                if t2 >= 0:
                    copy_attn(t2, 1, (c_av, t2))
                    copy_attn(t2, 3, (c_av, t2))
                if 0 <= t1 < NT:
                    softmax_weights(t1)
                if t0 < NT:
                    dve.wait_ge(c_v, t0 + 1)
                    after(dve, c_av, t0 - 1)
                    nc.vector.tensor_tensor(vs[:, t0 % 2, 0:D], bank[0][:, D:2 * D], bv_row, ALU.add).then_inc(c_vc, 1)
                if t2 >= 0:
                    dve.wait_ge(c_wo, t2 + 1)
                    link(nc.vector.tensor_tensor(tile(X, t2), tile(X, t2), bank[5][:, D:2 * D], ALU.add))
                    nc.vector.tensor_tensor(tile(X, t2), tile(X, t2), bo_row, ALU.add).then_inc(res, 1)

            def heads(v):
                return v.rearrange("p (h x n) -> p h x n", h=4, x=2)

            def rope(t, g):
                n = 5 * t + g
                dve.wait_ge(d_pj, 6 * t + g + 1)
                after(dve, d_radd, n - 1)
                src = heads(bank[g % 2])
                cos, sin = (c(w).rearrange("p (o n) -> p o n", o=1).to_broadcast([P, 4, HD])
                            for w in ("cos", "sin"))
                nc.vector.tensor_tensor(ra[:, g % 2, :].rearrange("p (h n) -> p h n", h=4),
                                        bank[g % 2].rearrange("p (h n) -> p h n", h=4), cos, ALU.mult)
                rbv = heads(rb[:, g % 2, :])
                for half in range(2):
                    a, b = CONST["sin"]
                    sn = cst[:, a + half * (HD // 2):a + (half + 1) * (HD // 2)].rearrange(
                        "p (o n) -> p o n", o=1).to_broadcast([P, 4, HD // 2])
                    ins = nc.vector.tensor_tensor(rbv[:, :, half, :], src[:, :, 1 - half, :], sn, ALU.mult)
                ins.then_inc(d_rope, 1)

            def route(t):
                prob = pr[:, 2 * t:2 * t + 2]
                top_two(bank[1][:, 0:E], e_lg, None, e_dif, gtmp[:, 0:1], e_th, t, prob)
                link(nc.vector.tensor_scalar(hot[:, t, 0, :], c("iota_e"), topf[:, 0:1], None, ALU.is_equal))
                link(nc.vector.tensor_scalar(hot[:, t, 1, :], c("iota_e"), topf[:, 1:2], None, ALU.is_equal))
                link(nc.vector.tensor_tensor(msel[:, t, :], hot[:, t, 0, :], hot[:, t, 1, :], ALU.add))
                nc.vector.tensor_tensor(cum[:, t + 1, :], cum[:, t, :], msel[:, t, :], ALU.add).then_inc(e_sel, 1)

            def places(t):
                dve.wait_ge(e_rank, t + 1)
                link(nc.vector.tensor_tensor(posf[:, :], bank[1][:, 8:8 + E], c("ebase"), ALU.add))
                link(nc.vector.tensor_tensor(pos2[:, :, :], hot[:, t, :, :],
                                             posf[:, :].rearrange("p (o n) -> p o n", o=1).to_broadcast([P, 2, E]),
                                             ALU.mult))
                link(nc.vector.tensor_reduce(topf[:, :], pos2[:, :, :], AX_X, ALU.add))
                nc.vector.tensor_copy(pos[:, t, :], topf[:, :]).then_inc(e_pos, 1)
                dve.wait_ge(e_pos, t + 1)

            for s in range(NT + 4):
                t0, t1, t2, t3, t4 = s, s - 1, s - 2, s - 3, s - 4
                main, attn = 0 <= t1 < NT, 0 <= t2 < NT
                if t4 >= 0:
                    places(t4)
                if t0 < NT:
                    norm_stats(3 * NT + t0)
                if main:
                    rope(t1, 0)
                if t0 < NT:
                    norm_apply(3 * NT + t0, tile(XP, t0), d_z)
                if main:
                    for g in range(1, 5):
                        rope(t1, g)
                if t0 < NT:
                    dve.wait_ge(d_rms, t0 + 1)
                    after(dve, t_x, 2 * NT + t0 - 1)
                    nc.vector.scalar_tensor_tensor(out=xn[:, t0 % 2, :], in0=tile(XP, t0), scalar=rms[:, t0 % 2, :],
                                                   in1=lnw_row, op0=ALU.mult, op1=ALU.mult).then_inc(normed, 1)
                if attn:
                    copy_attn(NT + t2, 1, (d_av, 4 * t2))
                if main:
                    softmax_shift(NT + t1, d_sc, t1 + 1, True)
                if attn:
                    copy_attn(NT + t2, 3, (d_av, 4 * t2))
                    for i in range(2):
                        dve.wait_ge(d_av, 4 * t2 + 2 * i + 2)
                        after(dve, d_wo, t2)
                        nc.vector.tensor_copy(oT[:, (2 * i + 1) * 512:(2 * i + 2) * 512], bank[5]).then_inc(d_oD, 1)
                if main:
                    softmax_weights(NT + t1)
                if attn:
                    dve.wait_ge(d_wo, t2 + 1)
                    nc.vector.tensor_tensor(tile(XP, t2), tile(XP, t2), bank[0][:, 0:D], ALU.add).then_inc(d_xp, 1)
                    dve.wait_ge(d_xp, t2 + 1)
                    dve.wait_ge(e_rms, t2 + 1)
                    after(dve, e_sent[t2 % 2], 32 * (t2 // 2))
                    after(dve, e_Tc, t2 - 1)
                    nc.vector.tensor_copy(h2r[:, t2 % 2, :, D].bitcast(U32),
                                          cst[:, CONST["dest"][0] + 2 * t2:CONST["dest"][0] + 2 * t2 + 2].bitcast(U32))
                    nc.vector.scalar_tensor_tensor(out=h2r[:, t2 % 2, 0, 0:D], in0=tile(XP, t2),
                                                   scalar=th[:, :], in1=ffw_row, op0=ALU.mult, op1=ALU.mult).then_inc(e_h2, 1)
                if 0 <= t3 < NT:
                    route(t3)

            dve.wait_ge(e_tot, 1)
            link(nc.vector.tensor_scalar(tot_i[:, :], bank[1][:, 8:8 + E], float(P - 1), None, ALU.add))
            link(nc.vector.tensor_scalar(tot_i[:, :], tot_i[:, :], 7, None, ALU.logical_shift_right))
            link(nc.vector.tensor_copy(tl[:, :], tot_i[:, :]))
            link(nc.vector.tensor_tensor_scan(cinc[:, :], c("ones")[:, 0:E], tl[:, :], 0.0, ALU.mult, ALU.add))
            b24 = lambda v: v.rearrange("p (n o) -> p n o", o=1).to_broadcast([P, 24, E])
            b8 = lambda v: v.rearrange("p (o n) -> p o n", o=1).to_broadcast([P, 24, E])
            link(nc.vector.tensor_tensor(cmp_[:, :, :], b24(c("iota_t")), b8(cinc[:, :]), ALU.is_ge))
            link(nc.vector.tensor_reduce(tabf[:, 0, :], cmp_[:, :, :], AX_X, ALU.add))
            link(nc.vector.tensor_tensor(cmp_[:, :, :], cmp_[:, :, :], b8(tl[:, :]), ALU.mult))
            link(nc.vector.tensor_reduce(tabf[:, 1, :], cmp_[:, :, :], AX_X, ALU.add))
            link(nc.vector.tensor_scalar(tabf[:, 0, :], tabf[:, 0, :], float(E - 1), None, ALU.min))
            link(nc.vector.tensor_tensor(tabf[:, 1, :], c("iota_t"), tabf[:, 1, :], ALU.subtract))
            link(nc.vector.tensor_scalar(tabf[:, 1, :], tabf[:, 1, :], float(T // P - 1), float(P), ALU.min, ALU.mult))
            link(nc.vector.scalar_tensor_tensor(out=tabf[:, 1, :], in0=tabf[:, 0, :], scalar=float(T),
                                                in1=tabf[:, 1, :], op0=ALU.mult, op1=ALU.add))
            link(nc.vector.tensor_copy(tab[:, 0, :], tabf[:, 1, :]))
            link(nc.vector.memset(tabf[:, 2, 0:1], 1.0))
            link(nc.vector.tensor_tensor(tabf[:, 2, 1:24], tabf[:, 0, 1:24], tabf[:, 0, 0:23], ALU.not_equal))
            link(nc.vector.tensor_copy(tab[:, 3, :], tabf[:, 2, :]))
            link(nc.vector.tensor_scalar(tabf[:, 3, :], tabf[:, 0, :], float(P), None, ALU.mult))
            link(nc.vector.tensor_copy(tab[:, 1, :], tabf[:, 3, :]))
            link(nc.vector.tensor_tensor_scan(tabf[:, 4, :], c("ones")[:, 0:24], tabf[:, 2, :], -1.0, ALU.mult, ALU.add))
            link(nc.vector.tensor_scalar(tabf[:, 5, :], tabf[:, 4, :], float(NSLOT), float(-NSLOT), ALU.is_ge, ALU.mult))
            link(nc.vector.tensor_scalar(tabf[:, 6, :], tabf[:, 4, :], float(2 * NSLOT), float(-NSLOT), ALU.is_ge, ALU.mult))
            link(nc.vector.tensor_tensor(tabf[:, 4, :], tabf[:, 4, :], tabf[:, 5, :], ALU.add))
            link(nc.vector.tensor_tensor(tabf[:, 4, :], tabf[:, 4, :], tabf[:, 6, :], ALU.add))
            link(nc.vector.tensor_scalar(tabf[:, 4, :], tabf[:, 4, :], float(WF), None, ALU.mult))
            nc.vector.tensor_copy(tab[:, 2, :], tabf[:, 4, :]).then_inc(tables, 1)

            def f_muls(j, u, n):
                dve.wait_ge(f_silu, at(j, 2, n))
                dve.wait_ge(f_h, at(j, 4, 2 * n + 1))
                dve.wait_ge(f_T, at(j - 3, 2, 1))
                nc.vector.tensor_tensor(act_f[:, u, n * HF:(n + 1) * HF], silu_f[:, n, :], bank[2 + n][:, 0:HF],
                                        ALU.mult).then_inc(f_mul, 1)

            def f_copy_y(j, u):
                dve.wait_ge(f_y, at(j))
                dve.wait_ge(f_left, at(j - 3))
                nc.vector.tensor_copy(ys[:, u, :], bank[4][:, 0:D]).then_inc(f_ys, 1)

            def f_step(s, sx, main=True, tail=True):
                if main:
                    f_muls(s - 1, (sx[1] - 1) % 3, 0)
                    f_muls(s - 1, (sx[1] - 1) % 3, 1)
                if tail:
                    u = sx[1] - 2
                    f_copy_y(s - 2, u % 3)

            f_step(1, (0, 1), tail=False)
            with dve.Fori(0, (TILES_F - 2) // 3) as i:
                for u in range(3):
                    f_step(3 * i + 2 + u, (i + (2 + u) // 3, (2 + u) % 3))
            f_step(TILES_F, (TILES_F // 3, TILES_F % 3))
            f_step(TILES_F + 1, ((TILES_F + 1) // 3, (TILES_F + 1) % 3), main=False)

            dve.wait_ge(e_base, NT)
            for t in range(NT):
                dve.wait_ge(g_in[t % 2], 16 * (t // 2 + 1))
                link(nc.vector.scalar_tensor_tensor(out=tile(X, t), in0=yk[:, t % 2, 0, :], scalar=pr[:, 2 * t:2 * t + 1],
                                                    in1=tile(X, t), op0=ALU.mult, op1=ALU.add))
                nc.vector.scalar_tensor_tensor(out=tile(X, t), in0=yk[:, t % 2, 1, :], scalar=pr[:, 2 * t + 1:2 * t + 2],
                                               in1=tile(X, t), op0=ALU.mult, op1=ALU.add).then_inc(g_sum, 1)

        @block.gpsimd
        def _(pool):
            for s_, per in F_PER:
                pool.sem_inc(s_, per * LEAD)
            pool.wait_ge(in_cst, 16)
            half = c("half")

            def inv_sqrt(src, scale, tmp, tmp_done, count, dst, done):
                nc.gpsimd.tensor_scalar(tmp, src, scale, LN_EPS, ALU.mult, ALU.add).then_inc(tmp_done, 1)
                pool.wait_ge(tmp_done, count)
                nc.gpsimd.tensor_tensor(dst, tmp, half, ALU.pow).then_inc(done, 1)

            def norm(n, last):
                q = n % 2
                pool.wait_ge(stats, n + 1)
                after(pool, *last)
                inv_sqrt(mv[:, q, 1:2], 1.0, ve[:, q, :], g_ve, n + 1, rstd[:, q, :], g_rstd)

            for n in range(2 * NT):
                norm(n, (normed, n - 1))

            def weights(m, own, count):
                after(pool, own, count)
                pool.wait_ge(s_exp, m + 1)
                pool.wait_ge(s_rs, m + 1)
                after(pool, s_t, 4 * (m - 1))
                v = bd[S:P, m % 2, :].rearrange("p (h k) -> p h k", h=NH)[:, :, S:P]
                e_v = e_sb[S:P, :].rearrange("p (h k) -> p h k", h=NH)
                r = rsum[S:P, :].rearrange("p (h o) -> p h o", o=1).to_broadcast([S, NH, S])
                nc.gpsimd.tensor_tensor(v, e_v, r, ALU.mult).then_inc(s_ng, 1)
                pool.wait_ge(s_ng, m + 1)

            hm = c("headmask").rearrange("p (h o) -> p h o", o=1).to_broadcast([P, 8, S])
            for s in range(NT + 2):
                t0, t1 = s, s - 1
                if t0 < NT:
                    norm(2 * NT + t0, (normed, 2 * NT + t0 - 1))
                if 0 <= t1 < NT:
                    weights(t1, g_rstd, min(2 * NT + t0 + 1, 3 * NT))
                    pool.wait_ge(c_kbd, 4 * t1 + 4)
                if t0 < NT:
                    after(pool, c_sc, t0)
                    for k in range(KC):
                        pool.wait_ge(c_qkc, 4 * t0 + 3 + k)
                        for b in range(2):
                            kT = qkT[:, t0 % 2, 1, k * P + S * b:k * P + S * b + S]
                            nc.gpsimd.tensor_tensor(
                                kbd[:, k, b, :].rearrange("p (h n) -> p h n", h=8),
                                kT.rearrange("p (o n) -> p o n", o=1).to_broadcast([P, 8, S]), hm,
                                ALU.mult).then_inc(c_kbd, 1)

            for s in range(NT + 4):
                t0, t1, t2, t3, t4 = s, s - 1, s - 2, s - 3, s - 4
                main, attn = 0 <= t1 < NT, 0 <= t2 < NT
                if t4 >= 0:
                    pool.wait_ge(e_pos, t4 + 1)
                    pool.wait_ge(e_h2k, t4 + 1)
                    pool.wait_ge(filled, 16 * E * (T // P))
                    for k in range(2):
                        nc.gpsimd.indirect_dma_start(
                            slot_rows, bass.IndirectOffsetOnAxis(ap=pos[:, t4, k:k + 1], axis=0),
                            h2r[:, t4 % 2, k, :], None).then_inc(e_sent[t4 % 2], 16)
                if t0 < NT:
                    norm(3 * NT + t0, (d_z, t0 - 1))
                if main:
                    for g in range(5):
                        pool.wait_ge(d_rope, 5 * t1 + g + 1)
                        after(pool, d_T, 5 * (t1 - 1) + g + 1)
                        nc.gpsimd.tensor_tensor(qr[:, g * 512:(g + 1) * 512], ra[:, g % 2, :], rb[:, g % 2, :],
                                                ALU.add).then_inc(d_radd, 1)
                        if g == 1 and t0 < NT:
                            pool.wait_ge(d_ss, t0 + 1)
                            after(pool, normed, 3 * NT + t0 - 1)
                            inv_sqrt(ss[:, t0 % 2, :], 1.0 / D, ms[:, t0 % 2, :], d_ms, t0 + 1, rms[:, t0 % 2, :], d_rms)
                elif t0 < NT:
                    pool.wait_ge(d_ss, t0 + 1)
                    inv_sqrt(ss[:, t0 % 2, :], 1.0 / D, ms[:, t0 % 2, :], d_ms, t0 + 1, rms[:, t0 % 2, :], d_rms)
                if main:
                    if t4 >= 0:
                        pool.wait_ge(e_sent[t4 % 2], 32 * (t4 // 2 + 1))
                    weights(NT + t1, d_radd, 5 * t1 + 5)
                if attn:
                    pool.wait_ge(e_ss, t2 + 1)
                    nc.gpsimd.tensor_scalar(gtmp[:, 4:5], th[:, :], 1.0 / D, LN_EPS, ALU.mult, ALU.add).then_inc(e_ms, 1)
                    pool.wait_ge(e_ms, t2 + 1)
                    nc.gpsimd.tensor_tensor(th[:, :], gtmp[:, 4:5], half, ALU.pow).then_inc(e_rms, 1)
                    nc.gpsimd.tensor_tensor(tile(X, t2), tile(X, t2), tile(XP, t2), ALU.add).then_inc(e_base, 1)

            def send(j, u):
                pool.wait_ge(f_ys, at(j))
                nc.gpsimd.indirect_dma_start(
                    result_rows, bass.IndirectOffsetOnAxis(ap=hs[:, u, D:D + 1].bitcast(U32), axis=0),
                    ys[:, u, :], None).then_inc(f_sent[u], 16)
                pool.wait_ge(f_sent[u], 16 * (j // 3 + 1))
                pool.sem_inc(f_left, 1)

            for j in range(TILES_F):
                send(j, j % 3)


def _constants():
    c = np.zeros((P, NCONST), np.float32)
    def put(name, v):
        a, b = CONST[name]
        c[:, a:b] = v
    p = np.arange(P)
    put("ident", np.eye(P))
    put("tri", p[:, None] < p[None, :])
    put("ones", 1.0)
    inv = np.float32(1000000.0) ** (-np.arange(0, HD, 2, dtype=np.float32) / np.float32(HD))
    ang = np.arange(S, dtype=np.float32)[p % S, None] * inv[None, :].astype(np.float32)
    put("cos", np.concatenate([np.cos(ang), np.cos(ang)], 1))
    put("sin", np.concatenate([-np.sin(ang), np.sin(ang)], 1))
    put("causal", np.where(np.arange(S)[None, :] <= (p % S)[:, None], 0.0, NEG))
    put("headmask", (p // HDC)[:, None] == np.arange(8)[None, :])
    put("ebase", T * np.arange(E)[None, :])
    put("iota_e", np.arange(E)[None, :])
    put("half", -0.5)
    put("iota_t", np.arange(24)[None, :])
    words = c.view(np.uint32)
    t, k = np.meshgrid(np.arange(NT), np.arange(2), indexing="ij")
    a, b = CONST["dest"]
    words[:, a:b] = 2 * (t.reshape(1, -1) * P + p[:, None]) + k.reshape(1, -1)
    words[:, CONST["fill"][1] - 1] = 2 * T + p
    return c


_OUT = ((B, S, D), "float32")


def kernel(**inputs):
    import numpy as _np
    import concourse.bacc as _bacc
    from concourse import mybir as _mybir
    from concourse.bass_utils import run_bass_kernel_spmd as _run

    a = {k: _np.asarray(v) for k, v in inputs.items()}

    def chunks(w):
        n = w.shape[0] // P
        return w.reshape(n, P, w.shape[1]).transpose(1, 0, 2).reshape(P, -1)

    ctx = a["ctx_2048"].reshape(NT, P, D)
    ctxT = ctx.reshape(NT, P, KC, P).transpose(0, 3, 2, 1).reshape(NT, P, D)
    w1, w2 = (a[f"L0_ffn_{n}"].reshape(HID0, D).T for n in ("W1", "W2"))
    w3 = a["L0_ffn_W3"].transpose(0, 2, 1).reshape(HID0, D)
    even_odd = _np.concatenate([_np.arange(0, HD, 2), _np.arange(1, HD, 2)])
    wq = a["L1_ffn_wq"].reshape(D, NH, HD)[:, :, even_odd].reshape(D, NH * HD)
    wk = a["L1_ffn_wk"].reshape(D, KV, HD)[:, :, even_odd].reshape(D, KV * HD)
    f13 = _np.stack([a["L1_ffn_w1"], a["L1_ffn_w3"]], 2)
    f13 = f13.reshape(E, KC, P, 2 * FF).transpose(0, 2, 1, 3).reshape(E, P, KC * 2 * FF)
    f2 = a["L1_ffn_w2"].reshape(E, NCF, P, D).transpose(0, 2, 1, 3).reshape(E, P, NCF * D)
    arrays = {
        "x": a["x"],
        "ctx_a": _np.concatenate([ctx, ctxT], 2),
        "w_b": _np.concatenate([chunks(_np.concatenate([w1, w2], 1)), chunks(w3)], 1),
        "wg_b": chunks(a["L0_ffn_Wg"].T),
        "w_c": _np.concatenate([chunks(a[f"L1_xattn_W{n}"].T) for n in "qkvo"], 1),
        "b_c": _np.concatenate([a["L1_xattn_bq"].reshape(KC, P).T, a["L1_xattn_bk"].reshape(KC, P).T], 1),
        "rows_c": _np.broadcast_to(_np.concatenate([a["L1_xattn_bv"], a["L1_xattn_bo"], a["L1_ffn_ln_w"],
                                                    a["L1_ffn_ff_ln_w"]])[None, :], (P, len(ROWS) * D)),
        "w_qkv": chunks(_np.concatenate([wq, wk, a["L1_ffn_wv"]], 1)),
        "w_o": chunks(a["L1_ffn_wo"]),
        "gate_d": chunks(a["L1_ffn_gate_w"]),
        "w_f": _np.concatenate([f13, f2], 2).reshape(E * P, WF),
        "consts": _constants(),
    }
    nc = _bacc.Bacc("TRN2", target_bir_lowering=False, num_devices=1)
    feed, args = {}, {}
    for name, v in arrays.items():
        v = _np.ascontiguousarray(v)
        feed[f"in_{name}_dram"] = v
        args[name] = nc.dram_tensor(f"in_{name}_dram", v.shape, _mybir.dt.from_np(v.dtype), kind="ExternalInput").ap()
    out = nc.dram_tensor("out_0_dram", _OUT[0], _mybir.dt.from_np(_np.dtype(_OUT[1])), kind="ExternalOutput").ap()
    build(nc, out=out, **args)
    r = _run(nc, [feed], core_ids=[0])
    return r.results[0]["out_0_dram"]
```

```python
import math
from contextlib import ExitStack

import numpy as np

import concourse.bass as bass
from concourse import mybir

F32 = mybir.dt.float32
U32 = mybir.dt.uint32
I32 = mybir.dt.int32
ALU = mybir.AluOpType
ACT = mybir.ActivationFunctionType
AX_X = mybir.AxisListType.X

P = 128
B, S, D = 16, 64, 256
T = B * S
NT = T // P
KC = D // P
E = 8
H0 = 176
HID0 = E * H0
NC0 = HID0 // P
GW = 2 * H0
NG0 = HID0 // GW
NH = 16
HDC = D // NH
HD = 128
KV = 4
FF = 896
NCF = FF // P
HF = FF // 2
WF = KC * 2 * FF + NCF * D
TILES_F = 2 * T // P + E - 1
NSLOT = 3
ROW = D + 1
LN_EPS = 1e-5
NEG = -1.0e30

CONST = {}
_at = 0
for _name, _n in (("ident", P), ("tri", P), ("ones", P), ("cos", HD), ("sin", HD), ("causal", S),
                  ("headmask", 8), ("ebase", E), ("iota_e", E), ("dest", 2 * NT),
                  ("iota_t", 24), ("fill", ROW)):
    CONST[_name] = (_at, _at + _n)
    _at += _n
NCONST = _at
ROWS = ("bv", "bo", "ln_w", "ff_ln_w")


def after(eng, sem, count):
    if count > 0:
        eng.wait_ge(sem, count)


def build(nc, x, ctx_a, w_b, wg_b, w_c, b_c, rows_c, w_qkv, w_o, gate_d, w_f, consts, out):
    x_rows = x.rearrange("b s d -> (b s) d")
    out_rows = out.rearrange("b s d -> (b s) d")
    slots = nc.dram_tensor("slots", [E * T, ROW], F32)
    slot_rows = slots.ap()
    expert_out = nc.dram_tensor("expert_out", [2 * T + P, D], F32)
    result_rows = expert_out.ap()

    with ExitStack() as stack:
        def sb(name, shape, dt=F32):
            return stack.enter_context(nc.sbuf_tensor(name, shape, dt))

        def sem(name):
            return stack.enter_context(nc.semaphore(name))

        p0 = stack.enter_context(nc.psum_tensor("p0", [P, 512], F32))
        p1 = stack.enter_context(nc.psum_tensor("p1", [P, 512], F32))
        psc = stack.enter_context(nc.psum_tensor("psc", [P, 1024], F32))
        p4 = stack.enter_context(nc.psum_tensor("p4", [P, 512], F32))
        p5 = stack.enter_context(nc.psum_tensor("p5", [P, 512], F32))
        p6 = stack.enter_context(nc.psum_tensor("p6", [P, 512], F32))
        p7 = stack.enter_context(nc.psum_tensor("p7", [P, 512], F32))
        bank = [p0[:, :], p1[:, :], psc[:, 0:512], psc[:, 512:1024], p4[:, :], p5[:, :], p6[:, :], p7[:, :]]

        cst = sb("cst", [P, NCONST])
        X = sb("X", [P, NT * D])
        XP = sb("XP", [P, NT * D])
        WM = sb("WM", [P, NSLOT * WF])
        WQ = sb("WQ", [P, KC * (NH + 2 * KV) * HD])
        rows = sb("rows", [P, len(ROWS) * D])
        wg = sb("wg", [P, KC * E])
        gd = sb("gd", [P, KC * E])
        bqk = sb("bqk", [P, 2 * KC])
        R1 = sb("R1", [P, 9472])
        R2 = sb("R2", [P, 2048 + 1024 + 512])
        xn = sb("xn", [P, 2, D])
        xT = sb("xT", [P, 2, D])
        vs = sb("vs", [P, 2, KV * HD])
        e_sb = sb("e_sb", [P, NH * S])
        bd = sb("bd", [P, 2, NH * P])
        aT = sb("aT", [P, NH * P])
        stat = sb("stat", [P, 2, 6])
        mv = sb("mv", [P, 2, 2])
        ve = sb("ve", [P, 2, 1])
        rstd = sb("rstd", [P, 2, 1])
        ss = sb("ss", [P, 2, 1])
        ms = sb("ms", [P, 2, 1])
        rms = sb("rms", [P, 2, 1])
        mx = sb("mx", [P, NH])
        sums = sb("sums", [P, NH])
        rsum = sb("rsum", [P, NH])
        top = sb("top", [P, 8])
        topi = sb("topi", [P, 8], U32)
        topf = sb("topf", [P, 2])
        dif = sb("dif", [P, 1])
        th = sb("th", [P, 1])
        half_ = sb("half", [P, 1])
        pr = sb("pr", [P, 2 * NT])
        ids = sb("ids", [P, 3], U32)
        gates = sb("gates", [P, 2, E])
        gtmp = sb("gtmp", [P, E])
        hot = sb("hot", [P, NT, 2, E])
        cum = sb("cum", [P, NT + 1, E])
        msel = sb("msel", [P, NT, E])
        posf = sb("posf", [P, E])
        pos2 = sb("pos2", [P, 2, E])
        pos = sb("pos", [P, NT, 2], U32)
        tot_i = sb("tot_i", [P, E], I32)
        tl = sb("tl", [P, E])
        cinc = sb("cinc", [P, E])
        cmp_ = sb("cmp_", [P, 24, E])
        tabf = sb("tabf", [P, 8, 24])
        tab = sb("tab", [P, 4, 24], I32)

        def c(name, parts=slice(0, P)):
            a, b = CONST[name]
            return cst[parts, a:b]

        ident = c("ident")
        tile = lambda buf, t: buf[:, t * D:(t + 1) * D]
        bv_row, bo_row, lnw_row, ffw_row = (rows[:, i * D:(i + 1) * D] for i in range(4))
        w12_b = WM[:, 0:KC * 2 * HID0].rearrange("p (k n) -> p k n", k=KC)
        w3_b = WM[:, KC * 2 * HID0:KC * 2 * HID0 + NC0 * D].rearrange("p (c n) -> p c n", c=NC0)
        n_b = KC * 2 * HID0 + NC0 * D
        wc = WM[:, n_b:n_b + 4 * KC * D].rearrange("p (w k n) -> p w k n", w=4, k=KC)
        n_c = 2 * WF
        wo_d = WM[:, n_c:n_c + NH * D].rearrange("p (h n) -> p h n", h=NH)
        wqkv = WQ[:, :].rearrange("p (k n) -> p k n", k=KC)
        ctxb = WQ[:, 0:NT * 2 * D].rearrange("p (t n) -> p t n", t=NT)
        sg = R1[:, 0:2048].rearrange("p (q b n) -> p q b n", q=2, b=2)
        act_b = R1[:, 2048:4864].rearrange("p (q n) -> p q n", q=2)
        actT_b = R1[:, 4864:7680].rearrange("p (q n) -> p q n", q=2)
        silu_b = R1[:, 7680:8384].rearrange("p (q n) -> p q n", q=2)
        kbd = R2[:, 0:2048].rearrange("p (c b n) -> p c b n", c=KC, b=2)
        qkT = R2[:, 2048:3072].rearrange("p (q w n) -> p q w n", q=2, w=2)
        cx = R2[:, 3072:3328]
        cxT = R2[:, 3328:3584]
        vs_c = vs[:, :, :].rearrange("p q (r n) -> p (q r) n", r=2)
        ra = R1[:, 0:1024].rearrange("p (q n) -> p q n", q=2)
        rb = R1[:, 1024:2048].rearrange("p (q n) -> p q n", q=2)
        qr = R1[:, 2048:4608]
        qT = R1[:, 4608:7168]
        oT = R1[:, 7168:9216]
        h2T = R1[:, 9216:9472]
        h2r = R2[:, 0:4 * ROW].rearrange("p (q k n) -> p q k n", q=2, k=2)
        sq_junk = R2[:, 4 * ROW:4 * ROW + D]
        hs = R1[:, 0:3 * ROW].rearrange("p (q n) -> p q n", q=3)
        hsT = R1[:, 772:772 + 3 * D].rearrange("p (q n) -> p q n", q=3)
        act_f = R1[:, 1540:1540 + 3 * FF].rearrange("p (q n) -> p q n", q=3)
        actT_f = R1[:, 4228:4228 + 3 * FF].rearrange("p (q n) -> p q n", q=3)
        silu_f = R1[:, 6916:6916 + 2 * HF].rearrange("p (q n) -> p q n", q=2)
        ys = R1[:, 7812:7812 + 3 * D].rearrange("p (q n) -> p q n", q=3)
        yk = WQ[:, 0:NT * 2 * D].rearrange("p (t k n) -> p t k n", t=NT, k=2)

        in_cst, in_wb, in_wc, in_rows, in_wq, in_wo, in_wf = (
            sem(n) for n in "in_cst in_wb in_wc in_rows in_wq in_wo in_wf".split())
        in_x = [sem("in_x0"), sem("in_x1"), sem("in_x_rest")]
        in_ctx = [sem(f"in_ctx{t}") for t in range(NT)]
        filled, halved = sem("filled"), sem("halved")
        chain = sem("v_chain")
        stats, g_ve, g_rstd, normed = (sem(n) for n in "stats g_ve g_rstd normed".split())
        res = sem("res")
        a_sc, a_sig, a_out = (sem(n) for n in "a_sc a_sig a_out".split())
        t_x, c_x = sem("t_x"), sem("c_x")
        b_lg, b_log, b_th, b_gate, b_h, b_silu, b_mul, b_t, b_tA, b_tD, b_y, b_dif = (
            sem(n) for n in "b_lg b_log b_th b_gate b_h b_silu b_mul b_t b_tA b_tD b_y b_dif".split())
        c_qk, c_qkc, c_v, c_vc, c_kbd, c_sc, c_av, c_cx, c_ct, c_ctc, c_wo = (
            sem(n) for n in "c_qk c_qkc c_v c_vc c_kbd c_sc c_av c_cx c_ct c_ctc c_wo".split())
        s_free, s_sub, s_exp, s_rs, s_nv, s_ng, s_t, s_cA, s_cD = (
            sem(n) for n in "s_free s_sub s_exp s_rs s_nv s_ng s_t s_cA s_cD".split())
        d_z, d_ss, d_ms, d_rms, d_pj, d_rope, d_radd, d_vc, d_T, d_qc, d_sc, d_av, d_oA, d_oD, d_wo, d_xp = (
            sem(n) for n in ("d_z d_ss d_ms d_rms d_pj d_rope d_radd d_vc d_T d_qc d_sc d_av d_oA "
                             "d_oD d_wo d_xp").split())
        e_ss, e_ms, e_rms, e_h2, e_h2k, e_base, e_T, e_Tc, e_lg, e_dif, e_th, e_sel, e_rank, e_pos = (
            sem(n) for n in ("e_ss e_ms e_rms e_h2 e_h2k e_base e_T e_Tc e_lg e_dif e_th e_sel "
                             "e_rank e_pos").split())
        e_sent = [sem("e_sent0"), sem("e_sent1")]
        e_tot, tables = sem("e_tot"), sem("tables")
        f_in = [sem(f"f_in{i}") for i in range(3)]
        f_w = [sem(f"f_w{i}") for i in range(3)]
        f_sent = [sem(f"f_sent{i}") for i in range(3)]
        f_t, f_tc, f_h, f_silu, f_mul, f_T, f_Tc, f_y, f_ys, f_left, f_ids = (
            sem(n) for n in "f_t f_tc f_h f_silu f_mul f_T f_Tc f_y f_ys f_left f_ids".split())
        g_in = [sem(f"g_in{t}") for t in range(NT)]
        g_sum, g_out = sem("g_sum"), sem("g_out")

        LEAD = 3
        F_PER = ((f_t, 1), (f_tc, 1), (f_h, 4), (f_silu, 2), (f_mul, 2), (f_T, 2), (f_Tc, 2), (f_y, 1), (f_ys, 1),
                 (f_left, 1), (f_ids, 1))

        def at(j, per=1, g=0):
            return per * (j + LEAD) + g + 1

        def attn_bank(m, u):
            return bank[((7, 6, 5, 6) if m < NT else (4, 5, 7, 6))[u]]

        block = stack.enter_context(nc.Block())

        @block.sync
        def _(sp):
            for t in range(NT):
                sp.dma_start(tile(X, t), x_rows[t * P:(t + 1) * P, :]).then_inc(in_x[min(t, 2)], 16)
                sp.dma_start(ctxb[:, t, :], ctx_a[t]).then_inc(in_ctx[t], 16)
            sp.dma_start(cst[:, :], consts).then_inc(in_cst, 16)
            sp.dma_start(WM[:, 0:n_b], w_b).then_inc(in_wb, 16)
            sp.dma_start(wg[:, :], wg_b).then_inc(in_wb, 16)
            sp.dma_start(WM[:, n_b:n_b + 4 * KC * D], w_c).then_inc(in_wc, 16)
            sp.dma_start(bqk[:, :], b_c).then_inc(in_wc, 16)
            sp.dma_start(rows[:, :], rows_c).then_inc(in_rows, 16)
            sp.dma_start(gd[:, :], gate_d).then_inc(in_wq, 16)
            sp.dma_start(WM[:, n_c:n_c + NH * D], w_o).then_inc(in_wo, 16)
            sp.wait_ge(in_cst, 16)
            fill = cst[:, CONST["fill"][0]:CONST["fill"][1]]
            for e in range(E):
                for r in range(T // P):
                    r0 = e * T + r * P
                    sp.dma_start(slot_rows[r0:r0 + P, :], fill).then_inc(filled, 16)
            sp.wait_ge(c_v, NT)
            sp.dma_start(WQ[:, :], w_qkv).then_inc(in_wq, 16)

            sp.wait_ge(res, 3 * NT)
            for e in range(2):
                sp.dma_start(WM[:, e * WF:(e + 1) * WF], w_f[e * P:(e + 1) * P, :]).then_inc(in_wf, 16)
            for u in range(2):
                sp.wait_ge(e_sent[u], 32 * (NT // 2))
            sp.dma_start(hs[:, 0, :], slot_rows[0:P, :]).then_inc(f_in[0], 16)
            sp.wait_ge(tables, 1)

            def load(j):
                base = sp.value_load(tab[0:1, 0, bass.ds(j, 1)], min_val=0, max_val=E * T - P)
                wrow = sp.value_load(tab[0:1, 1, bass.ds(j, 1)], min_val=0, max_val=(E - 1) * P)
                slot = sp.value_load(tab[0:1, 2, bass.ds(j, 1)], min_val=0, max_val=(NSLOT - 1) * WF)
                fresh = sp.value_load(tab[0:1, 3, bass.ds(j, 1)], min_val=0, max_val=1)
                return base, wrow, slot, fresh

            def fetch(j, u):
                base, wrow, slot, fresh = load(j)
                sp.wait_ge(f_t, at(j - 3))
                sp.wait_ge(f_ids, at(j - 3))
                sp.dma_start(hs[:, u, :], slot_rows[bass.ds(base, P), :]).then_inc(f_in[u], 16)
                sp.wait_ge(f_y, at(j - 3))
                sp.dma_start(WM[:, bass.ds(slot, WF)], w_f[bass.ds(wrow, P), :],
                             cond=(fresh > 0)).then_inc(f_w[u], 16)

            with sp.Fori(0, (TILES_F - 1) // 3) as i:
                for u in range(1, 4):
                    fetch(3 * i + u, u % 3)
            for j in range((TILES_F - 1) // 3 * 3 + 1, TILES_F):
                fetch(j, j % 3)

            sp.wait_ge(f_left, at(TILES_F - 1))
            for t in range(NT):
                sp.dma_start(yk[:, t], result_rows[2 * t * P:2 * (t + 1) * P, :]
                             .rearrange("(p k) n -> p k n", k=2)).then_inc(g_in[t], 16)
            for t in range(NT):
                sp.wait_ge(g_sum, t + 1)
                sp.dma_start(out_rows[t * P:(t + 1) * P, :], tile(X, t)).then_inc(g_out, 16)
            sp.wait_ge(g_out, 16 * NT)

        @block.tensor
        def _(pe):
            def a_scores(t):
                q = t % 2
                pe.wait_ge(in_ctx[t], 16)
                pe.wait_ge(normed, t + 1)
                for b in range(2):
                    after(pe, a_sig, 2 * (t - 2) + b + 1)
                    r = slice(S * b, S * b + S)
                    for k in range(KC):
                        mm = pe.matmul(bank[2 * q + b][:, k * D:(k + 1) * D], xn[r, q, k * P:(k + 1) * P],
                                       ctxb[r, t, 0:D], start=True, stop=True)
                    mm.then_inc(a_sc, 1)

            def a_outs(t):
                q = t % 2
                after(pe, res, t - 1)
                for b in range(2):
                    pe.wait_ge(a_sig, 2 * t + b + 1)
                    for k in range(KC):
                        mm = pe.matmul(bank[4 + q][S * b:S * b + S, 0:D],
                                       ctxb[:, t, D + k * P + S * b:D + k * P + S * b + S],
                                       sg[:, q, b, k * D:(k + 1) * D], start=(k == 0), stop=(k == KC - 1))
                    mm.then_inc(a_out, 1)

            for s in range(NT + 1):
                if s < NT:
                    a_scores(s)
                if s >= 1:
                    a_outs(s - 1)

            def turn_x(m, dst, guard):
                pe.wait_ge(normed, NT + m + 1)
                after(pe, *guard)
                for k in range(KC):
                    mm = pe.transpose(dst[:, k * P:(k + 1) * P], xn[:, m % 2, k * P:(k + 1) * P], ident)
                mm.then_inc(t_x, 1)

            def b_gates(t):
                pe.wait_ge(c_x, t + 1)
                for k in range(KC):
                    mm = pe.matmul(bank[5][:, D:D + E], xT[:, t % 2, k * P:(k + 1) * P],
                                   wg[:, k * E:(k + 1) * E], start=(k == 0), stop=(k == KC - 1))
                mm.then_inc(b_lg, 1)

            def b_hidden(t, g):
                pe.wait_ge(c_x, t + 1)
                n = NG0 * t + g
                for w, free in ((0, b_silu), (1, b_mul)):
                    after(pe, free, n - 1)
                    for k in range(KC):
                        mm = pe.matmul(bank[2 * w + g % 2][:, 0:GW], xT[:, t % 2, k * P:(k + 1) * P],
                                       w12_b[:, k, w * HID0 + g * GW:w * HID0 + (g + 1) * GW],
                                       start=(k == 0), stop=(k == KC - 1))
                    mm.then_inc(b_h, 1)

            def b_turn(t, u):
                chunks = range(4 * u, min(4 * u + 4, NC0))
                pe.wait_ge(b_mul, NG0 * t + u + 2)
                after(pe, *((b_tA, 2 * t), (b_tD, t), (b_tA, 2 * t + 1))[u])
                for i, ch in enumerate(chunks):
                    mm = pe.transpose(bank[6 + u % 2][:, i * P:(i + 1) * P],
                                      act_b[:, t % 2, ch * P:(ch + 1) * P], ident)
                mm.then_inc(b_t, 1)

            def b_down(t):
                pe.wait_ge(b_tA, 2 * t + 2)
                pe.wait_ge(b_tD, t + 1)
                after(pe, res, NT + t)
                for ch in range(NC0):
                    mm = pe.matmul(bank[4][:, 0:D], actT_b[:, t % 2, ch * P:(ch + 1) * P], w3_b[:, ch, :],
                                   start=(ch == 0), stop=(ch == NC0 - 1))
                mm.then_inc(b_y, 1)

            pe.wait_ge(in_cst, 16)
            pe.wait_ge(in_wb, 32)
            pe.wait_ge(res, NT)
            for s in range(NT + 2):
                t0, t1, t2 = s, s - 1, s - 2
                main = 0 <= t1 < NT
                if main:
                    b_hidden(t1, 0)
                if t2 >= 0:
                    b_turn(t2, 2)
                if main:
                    b_hidden(t1, 1)
                if t2 >= 0:
                    b_down(t2)
                if t0 < NT:
                    turn_x(t0, bank[5], (b_log, t0))
                if main:
                    b_hidden(t1, 2)
                    b_turn(t1, 0)
                if t0 < NT:
                    b_gates(t0)
                if main:
                    b_hidden(t1, 3)
                    b_turn(t1, 1)

            def turn_attn(m, u, guard):
                pe.wait_ge(s_nv, m + 1)
                pe.wait_ge(s_ng, m + 1)
                for g in guard:
                    after(pe, *g)
                for i in range(4):
                    h = 4 * u + i
                    mm = pe.transpose(attn_bank(m, u)[:, i * P:(i + 1) * P], bd[:, m % 2, h * P:(h + 1) * P], ident)
                mm.then_inc(s_t, 1)

            def c_project(t):
                m, q = NT + t, t % 2
                pe.wait_ge(c_x, m + 1)
                after(pe, c_qkc, 4 * t)
                for w in (1, 0):
                    for n in range(KC):
                        for k in range(KC):
                            rhs = xT[:, m % 2, k * P:(k + 1) * P] if w == 0 else ctxb[:, t, D + k * P:D + (k + 1) * P]
                            mm = pe.matmul(bank[1][:, (2 * w + n) * P:(2 * w + n + 1) * P],
                                           wc[:, w, k, n * P:(n + 1) * P], rhs, start=(k == 0), stop=(k == KC - 1))
                    mm.then_inc(c_qk, 1)
                for k in range(KC):
                    mm = pe.matmul(bank[0][:, D:2 * D], ctxb[:, t, D + k * P:D + (k + 1) * P], wc[:, 2, k, :],
                                   start=(k == 0), stop=(k == KC - 1))
                mm.then_inc(c_v, 1)

            def c_scores(t):
                q = t % 2
                pe.wait_ge(c_kbd, 4 * t + 4)
                pe.wait_ge(c_qkc, 4 * t + 4)
                after(pe, s_sub, t)
                for k in range(KC):
                    for b in range(2):
                        mm = pe.matmul(bank[2 + k][S * b:S * b + S, :], qkT[:, q, 0, k * P + S * b:k * P + S * b + S],
                                       kbd[:, k, b, :], start=True, stop=True)
                mm.then_inc(c_sc, 1)

            def c_values(t):
                q = t % 2
                pe.wait_ge(c_vc, t + 1)
                after(pe, c_cx, t)
                for u in range(4):
                    after(pe, (s_cA, s_cD)[u % 2], 2 * t + u // 2 + 1)
                    for h in range(4 * u, 4 * u + 4):
                        mm = pe.matmul(bank[4][:, h * HDC:(h + 1) * HDC], aT[:, h * P:(h + 1) * P],
                                       vs_c[:, t % 4, h * HDC:(h + 1) * HDC], start=True, stop=True)
                mm.then_inc(c_av, 1)

            def c_turn(t):
                pe.wait_ge(c_cx, t + 1)
                after(pe, s_cA, 2 * (t + 1))
                after(pe, res, 2 * NT + t)
                for k in range(KC):
                    mm = pe.transpose(bank[5][:, k * P:(k + 1) * P], cx[:, k * P:(k + 1) * P], ident)
                mm.then_inc(c_ct, 1)

            def c_outs(t):
                pe.wait_ge(c_ctc, t + 1)
                for k in range(KC):
                    mm = pe.matmul(bank[5][:, D:2 * D], cxT[:, k * P:(k + 1) * P], wc[:, 3, k, :],
                                   start=(k == 0), stop=(k == KC - 1))
                mm.then_inc(c_wo, 1)

            pe.wait_ge(in_wc, 32)
            pe.wait_ge(res, 2 * NT)
            turn_x(NT, bank[0], (c_vc, 0))
            for s in range(NT + 3):
                t0, t1, t2, t3 = s, s - 1, s - 2, s - 3
                attn = 0 <= t2 < NT
                if 0 <= t1 < NT:
                    c_scores(t1)
                if t3 >= 0:
                    c_turn(t3)
                if t0 < NT:
                    c_project(t0)
                if t3 >= 0:
                    c_outs(t3)
                if attn:
                    for u in range(2):
                        turn_attn(t2, u, [((s_cA, s_cD)[u % 2], 2 * t2 + u // 2)])
                if t0 + 1 < NT:
                    turn_x(NT + t0 + 1, bank[0], (c_vc, t0 + 1))
                if attn:
                    turn_attn(t2, 2, [(res, 2 * NT + t3 + 1)])
                    turn_attn(t2, 3, [(s_cD, 2 * t2 + 1)])
                    c_values(t2)

            def d_project(t, g):
                m = 2 * NT + t
                if g == 0:
                    pe.wait_ge(c_x, m + 1)
                after(pe, *((d_xp, t - 1), (d_vc, t), (d_rope, 5 * t + 1), (d_rope, 5 * t + 2),
                            (d_rope, 5 * t + 3), (d_rope, 5 * t + 4))[g])
                for k in range(KC):
                    mm = pe.matmul(bank[g % 2], xT[:, m % 2, k * P:(k + 1) * P],
                                   wqkv[:, k, g * 512:(g + 1) * 512], start=(k == 0), stop=(k == KC - 1))
                mm.then_inc(d_pj, 1)

            def d_turn(t, g):
                pe.wait_ge(d_radd, 5 * t + g + 1)
                after(pe, *((c_x, 2 * NT + t + 1), (e_Tc, t - 2), (d_qc, 5 * t + 1), (d_qc, 5 * t + 2),
                            (d_qc, 5 * t + 3))[g])
                if g < 2:
                    after(pe, (s_cD, s_cA)[g], 2 * (NT + t - 1))
                for i in range(4):
                    mm = pe.transpose(bank[6 + g % 2][:, i * P:(i + 1) * P],
                                      qr[:, g * 512 + i * P:g * 512 + (i + 1) * P], ident)
                mm.then_inc(d_T, 1)

            def d_scores(t):
                pe.wait_ge(d_qc, 5 * t + 5)
                after(pe, *((s_free, t) if t else (s_sub, NT)))
                for h in range(NH):
                    kv = NH + h // (NH // KV)
                    for b in range(2):
                        mm = pe.matmul(psc[S * b:S * b + S, h * S:(h + 1) * S],
                                       qT[:, h * P + S * b:h * P + S * b + S],
                                       qT[:, kv * P + S * b:kv * P + S * b + S], start=True, stop=True)
                mm.then_inc(d_sc, 1)

            def d_values(t):
                m = NT + t
                pe.wait_ge(d_vc, t + 1)
                for kv in range(KV):
                    after(pe, (s_cA, s_cD)[kv % 2], 2 * m + kv // 2 + 1)
                    after(pe, (d_oA, d_oD)[kv % 2], 2 * t + kv // 2)
                    pe.matmul(bank[4 + kv % 2], vs[:, m % 2, kv * HD:(kv + 1) * HD],
                              aT[:, kv * 512:(kv + 1) * 512], start=True, stop=True).then_inc(d_av, 1)

            def d_outs(t, last_rope):
                after(pe, d_rope, last_rope)
                for h in range(NH):
                    if h % 4 == 0:
                        after(pe, (d_oA, d_oD)[h // 4 % 2], 2 * t + h // 8 + 1)
                    mm = pe.matmul(bank[0][:, 0:D], oT[:, h * P:(h + 1) * P], wo_d[:, h, :],
                                   start=(h == 0), stop=(h == NH - 1))
                mm.then_inc(d_wo, 1)

            def e_turn(t, guard):
                pe.wait_ge(e_h2, t + 1)
                after(pe, s_cA, guard)
                for k in range(KC):
                    mm = pe.transpose(bank[7][:, k * P:(k + 1) * P], h2r[:, t % 2, 0, k * P:(k + 1) * P], ident)
                mm.then_inc(e_T, 1)

            def e_logits(t):
                pe.wait_ge(e_Tc, t + 1)
                after(pe, d_oD, 2 * min(t + 2, NT))
                after(pe, e_pos, t)
                for k in range(KC):
                    mm = pe.matmul(bank[5][:, 0:E], h2T[:, k * P:(k + 1) * P], gd[:, k * E:(k + 1) * E],
                                   start=(k == 0), stop=(k == KC - 1))
                mm.then_inc(e_lg, 1)

            def e_ranks(t):
                pe.wait_ge(e_sel, t + 1)
                pe.matmul(bank[5][:, 8:8 + E], c("ones"), cum[:, t, :], start=True, stop=False)
                pe.matmul(bank[5][:, 8:8 + E], c("tri"), msel[:, t, :], start=False, stop=True).then_inc(e_rank, 1)

            pe.wait_ge(in_wq, 32)
            pe.wait_ge(in_wo, 16)
            pe.wait_ge(res, 3 * NT)
            for s in range(NT + 4):
                t0, t1, t2, t3, t4 = s, s - 1, s - 2, s - 3, s - 4
                main, attn = 0 <= t1 < NT, 0 <= t2 < NT
                for g in range(6):
                    if main:
                        d_project(t1, g)
                        if g >= 2:
                            d_turn(t1, g - 2)
                    if g == 3 and t4 >= 0:
                        e_ranks(t4)
                if attn:
                    turn_attn(NT + t2, 0, [(d_oA, 2 * t2)])
                    turn_attn(NT + t2, 1, [(d_oD, 2 * t2), (e_pos, t2 - 1)])
                if main:
                    d_turn(t1, 4)
                if attn:
                    turn_attn(NT + t2, 2, [(d_qc, min(5 * t1 + 4, 5 * NT)), (e_Tc, t2 - 1)])
                    turn_attn(NT + t2, 3, [(d_qc, min(5 * t1 + 5, 5 * NT))])
                if main:
                    d_scores(t1)
                if attn:
                    d_values(t2)
                if 0 <= t3 < NT:
                    e_turn(t3, min(2 * (NT + t2) + 2, 4 * NT))
                if t0 < NT:
                    turn_x(2 * NT + t0, bank[6], (s_cD, 2 * (NT + t2) + 2 if attn else 0))
                if attn:
                    d_outs(t2, min(5 * t1 + 5, 5 * NT))
                if 0 <= t3 < NT:
                    e_logits(t3)
            pe.wait_ge(e_pos, NT)
            pe.wait_ge(d_oA, 2 * NT)
            pe.matmul(bank[4][:, 8:8 + E], c("ones"), cum[:, NT, :], start=True, stop=True).then_inc(e_tot, 1)

            def f_turn_x(j, u, k3):
                pe.wait_ge(f_in[u], 16 * k3 + 16)
                pe.wait_ge(f_tc, at(j - 1))
                for k in range(KC):
                    mm = pe.transpose(bank[5][:, k * P:(k + 1) * P], hs[:, u, k * P:(k + 1) * P], ident)
                mm.then_inc(f_t, 1)

            def f_hidden(j, u, k3, n, slot, first):
                if n == 0:
                    pe.wait_ge(f_tc, at(j))
                    if first:
                        pe.wait_ge(in_wf, 32)
                    else:
                        pe.wait_ge(f_w[u], 16 * k3 + (16 if u else 0))
                for w, free in ((0, f_silu), (1, f_mul)):
                    pe.wait_ge(free, at(j - 1, 2, n))
                    for k in range(KC):
                        o = (2 * k + w) * FF + n * HF
                        mm = pe.matmul(bank[2 * w + n][:, 0:HF], hsT[:, u, k * P:(k + 1) * P],
                                       WM[:, bass.ds(slot + o, HF)], start=(k == 0), stop=(k == KC - 1))
                    mm.then_inc(f_h, 1)

            def f_turn(j, u, n):
                chunks = (range(0, 3), range(3, NCF))[n]
                pe.wait_ge(f_mul, at(j, 2, n))
                pe.wait_ge(f_Tc, at(j - 1, 2, n))
                for i, ch in enumerate(chunks):
                    mm = pe.transpose(bank[6 + n][:, i * P:(i + 1) * P], act_f[:, u, ch * P:(ch + 1) * P], ident)
                mm.then_inc(f_T, 1)

            def f_down(j, u, slot):
                pe.wait_ge(f_Tc, at(j, 2, 1))
                pe.wait_ge(f_ys, at(j - 1))
                for ch in range(NCF):
                    mm = pe.matmul(bank[4][:, 0:D], actT_f[:, u, ch * P:(ch + 1) * P],
                                   WM[:, bass.ds(slot + KC * 2 * FF + ch * D, D)],
                                   start=(ch == 0), stop=(ch == NCF - 1))
                mm.then_inc(f_y, 1)

            def f_step(s, sx, first=False, head=True, main=True, tail=True):
                def of(lag):
                    k3, u = sx[0], sx[1] - lag
                    return s - lag, u % 3, k3 + u // 3
                j0, u0, k0 = of(0)
                j1, u1, k1 = of(1)
                j2, u2, k2 = of(2)
                if main:
                    slot1 = 0
                    if not first:
                        slot1 = pe.value_load(tab[0:1, 2, bass.ds(j1, 1)], min_val=0, max_val=(NSLOT - 1) * WF)
                    f_hidden(j1, u1, k1, 0, slot1, first)
                if tail:
                    f_turn(j2, u2, 1)
                if head:
                    f_turn_x(j0, u0, k0)
                if main:
                    f_hidden(j1, u1, k1, 1, slot1, first)
                if tail:
                    slot2 = pe.value_load(tab[0:1, 2, bass.ds(j2, 1)], min_val=0, max_val=(NSLOT - 1) * WF)
                    f_down(j2, u2, slot2)
                if main:
                    f_turn(j1, u1, 0)

            f_step(0, (0, 0), main=False, tail=False)
            f_step(1, (0, 1), first=True, tail=False)
            pe.wait_ge(tables, 1)
            with pe.Fori(0, (TILES_F - 2) // 3) as i:
                for u in range(3):
                    f_step(3 * i + 2 + u, (i + (2 + u) // 3, (2 + u) % 3))
            f_step(TILES_F, (TILES_F // 3, TILES_F % 3), head=False)
            f_step(TILES_F + 1, ((TILES_F + 1) // 3, (TILES_F + 1) % 3), head=False, main=False)

        @block.scalar
        def _(act):
            for t in range(NT):
                for b in range(2):
                    act.wait_ge(a_sc, 2 * t + b + 1)
                    after(act, a_out, 2 * (t - 2) + b + 1)
                    nc.scalar.activation(sg[:, t % 2, b, :], bank[2 * (t % 2) + b], ACT.Sigmoid,
                                         scale=1.0 / math.sqrt(S)).then_inc(a_sig, 1)

            def copy_x(m, src, free):
                act.wait_ge(t_x, m + 1)
                after(act, *free)
                nc.scalar.copy(xT[:, m % 2, :], src[:, 0:D]).then_inc(c_x, 1)

            def b_silus(t, g):
                n = NG0 * t + g
                act.wait_ge(b_h, 2 * n + 1)
                after(act, b_mul, n - 1)
                nc.scalar.activation(silu_b[:, g % 2, :], bank[g % 2][:, 0:GW], ACT.Silu).then_inc(b_silu, 1)

            def b_copy(t, u):
                act.wait_ge(b_t, 3 * t + u + 1)
                after(act, b_y, t - 1)
                n = (min(4 * u + 4, NC0) - 4 * u) * P
                nc.scalar.copy(actT_b[:, t % 2, 4 * u * P:4 * u * P + n], bank[6][:, 0:n]).then_inc(b_tA, 1)

            for s in range(NT + 2):
                t0, t1, t2 = s, s - 1, s - 2
                main = 0 <= t1 < NT
                if main:
                    b_silus(t1, 0)
                if t2 >= 0:
                    b_copy(t2, 2)
                if main:
                    b_silus(t1, 1)
                if t0 < NT:
                    copy_x(t0, bank[5], (b_h, 2 * NG0 * (t0 - 1)))
                if main:
                    b_silus(t1, 2)
                    b_copy(t1, 0)
                if t0 < NT:
                    act.wait_ge(b_dif, t0 + 1)
                    nc.scalar.activation(th[:, :], dif[:, :], ACT.Tanh, scale=0.5).then_inc(b_th, 1)
                if main:
                    b_silus(t1, 3)

            def exps(m, scale):
                act.wait_ge(s_sub, m + 1)
                nc.scalar.activation(e_sb[:, :], e_sb[:, :], ACT.Exp, scale=scale).then_inc(s_exp, 1)

            def copy_attn(m, u, free):
                act.wait_ge(s_t, 4 * m + u + 1)
                after(act, *free)
                nc.scalar.copy(aT[:, u * 512:(u + 1) * 512], attn_bank(m, u)).then_inc(s_cA, 1)

            act.wait_ge(in_wc, 32)
            def copy_qk(t):
                act.wait_ge(c_qk, 2 * t + 2)
                after(act, c_sc, t - 1)
                after(act, c_kbd, 4 * (t - 1))
                for w in (1, 0):
                    for n in range(KC):
                        nc.scalar.activation(qkT[:, t % 2, w, n * P:(n + 1) * P],
                                             bank[1][:, (2 * w + n) * P:(2 * w + n + 1) * P], ACT.Identity,
                                             bias=bqk[:, 2 * w + n:2 * w + n + 1]).then_inc(c_qkc, 1)

            copy_x(NT, bank[0], (c_x, NT))
            for s in range(NT + 3):
                t0, t1, t2, t3 = s, s - 1, s - 2, s - 3
                attn = 0 <= t2 < NT
                if t3 >= 0:
                    act.wait_ge(c_ct, t3 + 1)
                    after(act, c_wo, t3)
                    nc.scalar.copy(cxT, bank[5][:, 0:D]).then_inc(c_ctc, 1)
                if t0 < NT:
                    copy_qk(t0)
                if attn:
                    copy_attn(t2, 0, (c_av, t2))
                if 0 <= t1 < NT:
                    exps(t1, 1.0 / math.sqrt(HDC))
                if t0 + 1 < NT:
                    copy_x(NT + t0 + 1, bank[0], (c_qk, 2 * t0))
                if attn:
                    copy_attn(t2, 2, (c_av, t2))
                    act.wait_ge(c_av, t2 + 1)
                    after(act, c_ct, t2)
                    nc.scalar.copy(cx, bank[4][:, 0:D]).then_inc(c_cx, 1)

            for s in range(NT + 4):
                t0, t1, t2, t3 = s, s - 1, s - 2, s - 3
                main, attn = 0 <= t1 < NT, 0 <= t2 < NT
                if t0 < NT:
                    act.wait_ge(d_z, t0 + 1)
                    after(act, d_ms, t0 - 1)
                    after(act, d_ss, t0)
                    after(act, e_ss, min(t3, NT))
                    nc.scalar.activation(sq_junk, tile(XP, t0), ACT.Square, accum_out=ss[:, t0 % 2, :]).then_inc(d_ss, 1)
                if main:
                    for g in range(4):
                        act.wait_ge(d_T, 5 * t1 + g + 1)
                        after(act, d_sc, t1)
                        nc.scalar.copy(qT[:, g * 512:(g + 1) * 512], bank[6 + g % 2]).then_inc(d_qc, 1)
                        if g == 3:
                            act.wait_ge(d_pj, 6 * t1 + 6)
                            after(act, d_av, 4 * (t1 - 1))
                            nc.scalar.copy(vs[:, t1 % 2, :], bank[1]).then_inc(d_vc, 1)
                if attn:
                    copy_attn(NT + t2, 0, (d_av, 4 * t2))
                if main:
                    act.wait_ge(d_T, 5 * t1 + 5)
                    nc.scalar.copy(qT[:, 4 * 512:5 * 512], bank[6]).then_inc(d_qc, 1)
                if attn:
                    copy_attn(NT + t2, 2, (d_av, 4 * t2))
                if attn:
                    for i in range(2):
                        act.wait_ge(d_av, 4 * t2 + 2 * i + 1)
                        after(act, d_wo, t2)
                        nc.scalar.copy(oT[:, 2 * i * 512:(2 * i + 1) * 512], bank[4]).then_inc(d_oA, 1)
                if 0 <= t3 < NT:
                    act.wait_ge(e_h2, t3 + 1)
                    nc.scalar.copy(h2r[:, t3 % 2, 1, 0:D], h2r[:, t3 % 2, 0, 0:D]).then_inc(e_h2k, 1)
                    act.wait_ge(e_T, t3 + 1)
                    after(act, e_lg, t3)
                    nc.scalar.copy(h2T, bank[7][:, 0:D]).then_inc(e_Tc, 1)
                if t0 < NT:
                    copy_x(2 * NT + t0, bank[6], (d_pj, 6 * (t0 - 1)))
                if main:
                    exps(NT + t1, 1.0 / math.sqrt(HD))
                if attn:
                    act.wait_ge(d_xp, t2 + 1)
                    after(act, e_ms, t2)
                    act.wait_ge(d_ss, min(t0 + 1, NT))
                    nc.scalar.activation(sq_junk, tile(XP, t2), ACT.Square, accum_out=th[:, :]).then_inc(e_ss, 1)
                if 0 <= t3 < NT:
                    act.wait_ge(e_dif, t3 + 1)
                    nc.scalar.activation(gtmp[:, 0:1], dif[:, :], ACT.Tanh, scale=0.5).then_inc(e_th, 1)

            def f_copy_x(j, u):
                act.wait_ge(f_t, at(j))
                act.wait_ge(f_h, at(j - 3, 4, 3))
                nc.scalar.copy(hsT[:, u, :], bank[5][:, 0:D]).then_inc(f_tc, 1)

            def f_silus(j, n):
                act.wait_ge(f_h, at(j, 4, 2 * n))
                act.wait_ge(f_mul, at(j - 1, 2, n))
                nc.scalar.activation(silu_f[:, n, :], bank[n][:, 0:HF], ACT.Silu).then_inc(f_silu, 1)

            def f_copy(j, u, n):
                act.wait_ge(f_T, at(j, 2, n))
                act.wait_ge(f_y, at(j - 3))
                o, w = ((0, 3 * P), (3 * P, 4 * P))[n]
                nc.scalar.copy(actT_f[:, u, o:o + w], bank[6 + n][:, 0:w]).then_inc(f_Tc, 1)

            def f_step(s, r, head=True, main=True, tail=True):
                if main:
                    f_silus(s - 1, 0)
                if tail:
                    f_copy(s - 2, (r - 2) % 3, 1)
                if head:
                    f_copy_x(s, r % 3)
                if main:
                    f_silus(s - 1, 1)
                    f_copy(s - 1, (r - 1) % 3, 0)

            f_step(0, 0, main=False, tail=False)
            f_step(1, 1, tail=False)
            with act.Fori(0, (TILES_F - 2) // 3) as i:
                for u in range(3):
                    f_step(3 * i + 2 + u, 2 + u)
            f_step(TILES_F, TILES_F, head=False)
            f_step(TILES_F + 1, TILES_F + 1, head=False, main=False)

        @block.vector
        def _(dve):
            links = [0]

            def link(ins):
                links[0] += 1
                ins.then_inc(chain, 1)
                dve.wait_ge(chain, links[0])


            def norm_stats(n):
                t, q = n % NT, n % 2
                if n < NT:
                    dve.wait_ge(in_x[min(t, 2)], 16 if t < 2 else 16 * (NT - 2))
                else:
                    dve.wait_ge(res, n - NT + 1)
                after(dve, g_ve, n - 1)
                link(nc.vector.bn_stats(stat[:, q, :], tile(X, t)))
                nc.vector.bn_aggr(mv[:, q, :], stat[:, q, :]).then_inc(stats, 1)

            def norm_apply(n, dst, done):
                t, q = n % NT, n % 2
                dve.wait_ge(g_rstd, n + 1)
                dve.wait_ge(stats, n + 1)
                nc.vector.tensor_scalar(dst, tile(X, t), mv[:, q, 0:1], rstd[:, q, :],
                                        ALU.subtract, ALU.mult).then_inc(done, 1)

            norm_stats(0)
            norm_apply(0, xn[:, 0, :], normed)
            norm_stats(1)
            norm_apply(1, xn[:, 1, :], normed)
            norm_stats(2)
            link(nc.vector.memset(bd[:, :, :], 0.0))
            link(nc.vector.memset(cum[:, 0, :], 0.0))
            for s in range(1, NT + 1):
                if s + 1 < NT:
                    after(dve, a_sc, 2 * s)
                    norm_apply(s + 1, xn[:, (s + 1) % 2, :], normed)
                if s + 2 < NT:
                    norm_stats(s + 2)
                if s >= 1:
                    t = s - 1
                    dve.wait_ge(a_out, 2 * t + 2)
                    nc.vector.tensor_tensor(tile(X, t), tile(X, t), bank[4 + t % 2][:, 0:D], ALU.add).then_inc(res, 1)

            dve.wait_ge(in_cst, 16)

            def top_two(logits, ready, read, dif_done, th_src, th_done, t, prob):
                dve.wait_ge(ready, t + 1)
                link(nc.vector.max(top[:, :], logits))
                ins = nc.vector.max_index(topi[:, :], top[:, :], logits)
                if read is not None:
                    ins.then_inc(read, 1)
                    dve.wait_ge(read, t + 1)
                else:
                    link(ins)
                nc.vector.tensor_tensor(dif[:, :], top[:, 1:2], top[:, 0:1], ALU.subtract).then_inc(dif_done, 1)
                link(nc.vector.tensor_copy(topf[:, :], topi[:, 0:2]))
                dve.wait_ge(th_done, t + 1)
                link(nc.vector.tensor_scalar(prob[:, 0:1], th_src, -0.5, 0.5, ALU.mult, ALU.add))
                link(nc.vector.tensor_scalar(prob[:, 1:2], th_src, 0.5, 0.5, ALU.mult, ALU.add))

            def b_gating(t):
                prob = pr[:, 0:2]
                top_two(bank[5][:, D:D + E], b_lg, b_log, b_dif, th[:, :], b_th, t, prob)
                link(nc.vector.tensor_scalar(gtmp[:, :], c("iota_e"), topf[:, 0:1], prob[:, 0:1],
                                             ALU.is_equal, ALU.mult))
                link(nc.vector.tensor_scalar(gates[:, t % 2, :], c("iota_e"), topf[:, 1:2], prob[:, 1:2],
                                             ALU.is_equal, ALU.mult))
                link(nc.vector.tensor_tensor(gates[:, t % 2, :], gates[:, t % 2, :], gtmp[:, :], ALU.add))

            def b_muls(t, g):
                n = NG0 * t + g
                dve.wait_ge(b_silu, n + 1)
                dve.wait_ge(b_h, 2 * n + 2)
                after(dve, b_t, 3 * (t - 1))
                for i in range(2):
                    e = 2 * g + i
                    ins = nc.vector.scalar_tensor_tensor(
                        out=act_b[:, t % 2, e * H0:(e + 1) * H0], in0=silu_b[:, g % 2, i * H0:(i + 1) * H0],
                        scalar=gates[:, t % 2, e:e + 1], in1=bank[2 + g % 2][:, i * H0:(i + 1) * H0],
                        op0=ALU.mult, op1=ALU.mult)
                ins.then_inc(b_mul, 1)

            for s in range(NT + 2):
                t0, t1, t2 = s, s - 1, s - 2
                main = 0 <= t1 < NT
                if t0 < NT:
                    norm_stats(NT + t0)
                    after(dve, t_x, t0 - 1)
                    norm_apply(NT + t0, xn[:, t0 % 2, :], normed)
                if main:
                    b_muls(t1, 0)
                    b_muls(t1, 1)
                if t2 >= 0:
                    dve.wait_ge(b_y, t2 + 1)
                    nc.vector.tensor_tensor(tile(X, t2), tile(X, t2), bank[4][:, 0:D], ALU.add).then_inc(res, 1)
                if main:
                    b_muls(t1, 2)
                if t0 < NT:
                    b_gating(t0)
                if main:
                    b_muls(t1, 3)
                    dve.wait_ge(b_t, 3 * t1 + 2)
                    after(dve, b_y, t1 - 1)
                    nc.vector.tensor_copy(actT_b[:, t1 % 2, 512:1024], bank[7]).then_inc(b_tD, 1)

            sc_v = psc[:, :].rearrange("p (h k) -> p h k", h=NH)
            e_v = e_sb[:, :].rearrange("p (h k) -> p h k", h=NH)

            def over_keys(v, parts=slice(0, P)):
                return v[parts, :].rearrange("p (h o) -> p h o", o=1).to_broadcast([v[parts, :].shape[0], NH, S])

            def softmax_mask(m, ready, count):
                dve.wait_ge(ready, count)
                after(dve, s_nv, m)
                after(dve, s_ng, m)
                mask = c("causal").rearrange("p (o k) -> p o k", o=1).to_broadcast([P, NH, S])
                nc.vector.tensor_tensor(e_v, sc_v, mask, ALU.add).then_inc(s_free, 1)

            def softmax_shift(m, src):
                if src is e_v:
                    dve.wait_ge(s_free, m - NT + 1)
                link(nc.vector.tensor_reduce(mx[:, :], src, AX_X, ALU.max))
                after(dve, s_nv, m)
                after(dve, s_ng, m)
                nc.vector.tensor_tensor(e_v, src, over_keys(mx), ALU.subtract).then_inc(s_sub, 1)

            def softmax_weights(m):
                dve.wait_ge(s_exp, m + 1)
                link(nc.vector.tensor_reduce(sums[:, :], e_v, AX_X, ALU.add))
                after(dve, s_ng, m)
                nc.vector.reciprocal(rsum[:, :], sums[:, :]).then_inc(s_rs, 1)
                dve.wait_ge(s_rs, m + 1)
                after(dve, s_t, 4 * (m - 1))
                v = bd[0:S, m % 2, :].rearrange("p (h k) -> p h k", h=NH)[:, :, 0:S]
                nc.vector.tensor_tensor(v, e_v[0:S], over_keys(rsum, slice(0, S)), ALU.mult).then_inc(s_nv, 1)

            def copy_attn(m, u, free):
                dve.wait_ge(s_t, 4 * m + u + 1)
                after(dve, *free)
                nc.vector.tensor_copy(aT[:, u * 512:(u + 1) * 512], attn_bank(m, u)).then_inc(s_cD, 1)

            dve.wait_ge(in_rows, 16)
            norm_stats(2 * NT)
            norm_apply(2 * NT, xn[:, 0, :], normed)
            for s in range(NT + 3):
                t0, t1, t2, t3 = s, s - 1, s - 2, s - 3
                attn = 0 <= t2 < NT
                if t0 + 1 < NT:
                    norm_stats(2 * NT + t0 + 1)
                if 0 <= t1 < NT:
                    dve.wait_ge(c_sc, t1 + 1)
                    softmax_shift(t1, sc_v)
                if t3 >= 0:
                    dve.wait_ge(c_wo, t3 + 1)
                    link(nc.vector.tensor_tensor(tile(X, t3), tile(X, t3), bank[5][:, D:2 * D], ALU.add))
                    nc.vector.tensor_tensor(tile(X, t3), tile(X, t3), bo_row, ALU.add).then_inc(res, 1)
                if t0 + 1 < NT:
                    after(dve, t_x, NT + t0)
                    norm_apply(2 * NT + t0 + 1, xn[:, (t0 + 1) % 2, :], normed)
                if t0 < NT:
                    dve.wait_ge(c_v, t0 + 1)
                    after(dve, c_av, t0 - 3)
                    nc.vector.tensor_tensor(vs_c[:, t0 % 4, :], bank[0][:, D:2 * D], bv_row, ALU.add).then_inc(c_vc, 1)
                if attn:
                    copy_attn(t2, 1, (c_av, t2))
                    copy_attn(t2, 3, (c_av, t2))
                if 0 <= t1 < NT:
                    softmax_weights(t1)

            def heads(v):
                return v.rearrange("p (h x n) -> p h x n", h=4, x=2)

            def rope(t, g):
                n = 5 * t + g
                dve.wait_ge(d_pj, 6 * t + g + 1)
                after(dve, d_radd, n - 1)
                src = heads(bank[g % 2])
                cos, sin = (c(w).rearrange("p (o n) -> p o n", o=1).to_broadcast([P, 4, HD])
                            for w in ("cos", "sin"))
                nc.vector.tensor_tensor(ra[:, g % 2, :].rearrange("p (h n) -> p h n", h=4),
                                        bank[g % 2].rearrange("p (h n) -> p h n", h=4), cos, ALU.mult)
                rbv = heads(rb[:, g % 2, :])
                for half in range(2):
                    a, b = CONST["sin"]
                    sn = cst[:, a + half * (HD // 2):a + (half + 1) * (HD // 2)].rearrange(
                        "p (o n) -> p o n", o=1).to_broadcast([P, 4, HD // 2])
                    ins = nc.vector.tensor_tensor(rbv[:, :, half, :], src[:, :, 1 - half, :], sn, ALU.mult)
                ins.then_inc(d_rope, 1)

            def route(t):
                prob = pr[:, 2 * t:2 * t + 2]
                top_two(bank[5][:, 0:E], e_lg, None, e_dif, gtmp[:, 0:1], e_th, t, prob)
                link(nc.vector.tensor_scalar(hot[:, t, 0, :], c("iota_e"), topf[:, 0:1], None, ALU.is_equal))
                link(nc.vector.tensor_scalar(hot[:, t, 1, :], c("iota_e"), topf[:, 1:2], None, ALU.is_equal))
                link(nc.vector.tensor_tensor(msel[:, t, :], hot[:, t, 0, :], hot[:, t, 1, :], ALU.add))
                nc.vector.tensor_tensor(cum[:, t + 1, :], cum[:, t, :], msel[:, t, :], ALU.add).then_inc(e_sel, 1)

            def places(t):
                dve.wait_ge(e_rank, t + 1)
                link(nc.vector.tensor_tensor(posf[:, :], bank[5][:, 8:8 + E], c("ebase"), ALU.add))
                link(nc.vector.tensor_tensor(pos2[:, :, :], hot[:, t, :, :],
                                             posf[:, :].rearrange("p (o n) -> p o n", o=1).to_broadcast([P, 2, E]),
                                             ALU.mult))
                link(nc.vector.tensor_reduce(topf[:, :], pos2[:, :, :], AX_X, ALU.add))
                nc.vector.tensor_copy(pos[:, t, :], topf[:, :]).then_inc(e_pos, 1)
                dve.wait_ge(e_pos, t + 1)

            def slot_rows_of(t):
                dve.wait_ge(d_xp, t + 1)
                dve.wait_ge(e_rms, t + 1)
                after(dve, e_sent[t % 2], 32 * (t // 2))
                after(dve, e_Tc, t - 1)
                nc.vector.tensor_copy(h2r[:, t % 2, :, D].bitcast(U32),
                                      cst[:, CONST["dest"][0] + 2 * t:CONST["dest"][0] + 2 * t + 2].bitcast(U32))
                nc.vector.scalar_tensor_tensor(out=h2r[:, t % 2, 0, 0:D], in0=tile(XP, t),
                                               scalar=th[:, :], in1=ffw_row, op0=ALU.mult, op1=ALU.mult).then_inc(e_h2, 1)

            for s in range(NT + 4):
                t0, t1, t2, t3, t4 = s, s - 1, s - 2, s - 3, s - 4
                main, attn = 0 <= t1 < NT, 0 <= t2 < NT
                if t0 < NT:
                    norm_stats(3 * NT + t0)
                if main:
                    rope(t1, 0)
                if t0 < NT:
                    norm_apply(3 * NT + t0, tile(XP, t0), d_z)
                if main:
                    rope(t1, 1)
                if 0 <= t3 < NT:
                    slot_rows_of(t3)
                if main:
                    for g in range(2, 4):
                        rope(t1, g)
                if t4 >= 0:
                    places(t4)
                if main:
                    rope(t1, 4)
                if t0 < NT:
                    dve.wait_ge(d_rms, t0 + 1)
                    after(dve, t_x, 2 * NT + t0 - 1)
                    nc.vector.scalar_tensor_tensor(out=xn[:, t0 % 2, :], in0=tile(XP, t0), scalar=rms[:, t0 % 2, :],
                                                   in1=lnw_row, op0=ALU.mult, op1=ALU.mult).then_inc(normed, 1)
                if attn:
                    copy_attn(NT + t2, 1, (d_av, 4 * t2))
                if attn:
                    copy_attn(NT + t2, 3, (d_av, 4 * t2))
                for i in range(2):
                    if main and i == 0:
                        softmax_mask(NT + t1, d_sc, t1 + 1)
                    if attn:
                        dve.wait_ge(d_av, 4 * t2 + 2 * i + 2)
                        after(dve, d_wo, t2)
                        nc.vector.tensor_copy(oT[:, (2 * i + 1) * 512:(2 * i + 2) * 512], bank[5]).then_inc(d_oD, 1)
                if main:
                    softmax_shift(NT + t1, e_v)
                    softmax_weights(NT + t1)
                if attn:
                    dve.wait_ge(d_wo, t2 + 1)
                    nc.vector.tensor_tensor(tile(XP, t2), tile(XP, t2), bank[0][:, 0:D], ALU.add).then_inc(d_xp, 1)
                if 0 <= t3 < NT:
                    route(t3)

            dve.wait_ge(e_tot, 1)
            link(nc.vector.tensor_scalar(tot_i[:, :], bank[4][:, 8:8 + E], float(P - 1), None, ALU.add))
            link(nc.vector.tensor_scalar(tot_i[:, :], tot_i[:, :], 7, None, ALU.logical_shift_right))
            link(nc.vector.tensor_copy(tl[:, :], tot_i[:, :]))
            link(nc.vector.tensor_scalar(tl[:, :], tl[:, :], 1.0, None, ALU.max))
            link(nc.vector.tensor_tensor_scan(cinc[:, :], c("ones")[:, 0:E], tl[:, :], 0.0, ALU.mult, ALU.add))
            b24 = lambda v: v.rearrange("p (n o) -> p n o", o=1).to_broadcast([P, 24, E])
            b8 = lambda v: v.rearrange("p (o n) -> p o n", o=1).to_broadcast([P, 24, E])
            link(nc.vector.tensor_tensor(cmp_[:, :, :], b24(c("iota_t")), b8(cinc[:, :]), ALU.is_ge))
            link(nc.vector.tensor_reduce(tabf[:, 0, :], cmp_[:, :, :], AX_X, ALU.add))
            link(nc.vector.tensor_tensor(cmp_[:, :, :], cmp_[:, :, :], b8(tl[:, :]), ALU.mult))
            link(nc.vector.tensor_reduce(tabf[:, 1, :], cmp_[:, :, :], AX_X, ALU.add))
            link(nc.vector.tensor_scalar(tabf[:, 0, :], tabf[:, 0, :], float(E - 1), None, ALU.min))
            link(nc.vector.tensor_tensor(tabf[:, 1, :], c("iota_t"), tabf[:, 1, :], ALU.subtract))
            link(nc.vector.tensor_scalar(tabf[:, 1, :], tabf[:, 1, :], float(T // P - 1), float(P), ALU.min, ALU.mult))
            link(nc.vector.scalar_tensor_tensor(out=tabf[:, 1, :], in0=tabf[:, 0, :], scalar=float(T),
                                                in1=tabf[:, 1, :], op0=ALU.mult, op1=ALU.add))
            link(nc.vector.tensor_copy(tab[:, 0, :], tabf[:, 1, :]))
            link(nc.vector.memset(tabf[:, 2, 0:1], 0.0))
            link(nc.vector.tensor_tensor(tabf[:, 2, 1:24], tabf[:, 0, 1:24], tabf[:, 0, 0:23], ALU.not_equal))
            link(nc.vector.scalar_tensor_tensor(out=tabf[:, 2, :], in0=tabf[:, 0, :], scalar=2.0, in1=tabf[:, 2, :],
                                                op0=ALU.is_ge, op1=ALU.mult))
            link(nc.vector.tensor_copy(tab[:, 3, :], tabf[:, 2, :]))
            link(nc.vector.tensor_scalar(tabf[:, 3, :], tabf[:, 0, :], float(P), None, ALU.mult))
            link(nc.vector.tensor_copy(tab[:, 1, :], tabf[:, 3, :]))
            link(nc.vector.tensor_scalar(tabf[:, 5, :], tabf[:, 0, :], float(NSLOT), float(-NSLOT), ALU.is_ge, ALU.mult))
            link(nc.vector.tensor_scalar(tabf[:, 6, :], tabf[:, 0, :], float(2 * NSLOT), float(-NSLOT), ALU.is_ge, ALU.mult))
            link(nc.vector.tensor_tensor(tabf[:, 4, :], tabf[:, 0, :], tabf[:, 5, :], ALU.add))
            link(nc.vector.tensor_tensor(tabf[:, 4, :], tabf[:, 4, :], tabf[:, 6, :], ALU.add))
            link(nc.vector.tensor_scalar(tabf[:, 4, :], tabf[:, 4, :], float(WF), None, ALU.mult))
            nc.vector.tensor_copy(tab[:, 2, :], tabf[:, 4, :]).then_inc(tables, 1)

            def f_muls(j, u, n):
                dve.wait_ge(f_silu, at(j, 2, n))
                dve.wait_ge(f_h, at(j, 4, 2 * n + 1))
                dve.wait_ge(f_T, at(j - 3, 2, 1))
                nc.vector.tensor_tensor(act_f[:, u, n * HF:(n + 1) * HF], silu_f[:, n, :], bank[2 + n][:, 0:HF],
                                        ALU.mult).then_inc(f_mul, 1)

            def f_copy_y(j, u):
                dve.wait_ge(f_y, at(j))
                dve.wait_ge(f_left, at(j - 3))
                nc.vector.tensor_copy(ys[:, u, :], bank[4][:, 0:D]).then_inc(f_ys, 1)

            def f_step(s, sx, main=True, tail=True):
                if main:
                    f_muls(s - 1, (sx[1] - 1) % 3, 0)
                    f_muls(s - 1, (sx[1] - 1) % 3, 1)
                if tail:
                    u = sx[1] - 2
                    f_copy_y(s - 2, u % 3)

            f_step(1, (0, 1), tail=False)
            with dve.Fori(0, (TILES_F - 2) // 3) as i:
                for u in range(3):
                    f_step(3 * i + 2 + u, (i + (2 + u) // 3, (2 + u) % 3))
            f_step(TILES_F, (TILES_F // 3, TILES_F % 3))
            f_step(TILES_F + 1, ((TILES_F + 1) // 3, (TILES_F + 1) % 3), main=False)

            dve.wait_ge(e_base, NT)
            for t in range(NT):
                dve.wait_ge(g_in[t], 16)
                link(nc.vector.scalar_tensor_tensor(out=tile(X, t), in0=yk[:, t, 0, :], scalar=pr[:, 2 * t:2 * t + 1],
                                                    in1=tile(X, t), op0=ALU.mult, op1=ALU.add))
                nc.vector.scalar_tensor_tensor(out=tile(X, t), in0=yk[:, t, 1, :], scalar=pr[:, 2 * t + 1:2 * t + 2],
                                               in1=tile(X, t), op0=ALU.mult, op1=ALU.add).then_inc(g_sum, 1)

        @block.gpsimd
        def _(pool):
            for s_, per in F_PER:
                pool.sem_inc(s_, per * LEAD)
            half = half_[:, :]
            nc.gpsimd.memset(half, -0.5).then_inc(halved, 1)
            pool.wait_ge(halved, 1)

            def inv_sqrt(src, scale, tmp, tmp_done, count, dst, done):
                nc.gpsimd.tensor_scalar(tmp, src, scale, LN_EPS, ALU.mult, ALU.add).then_inc(tmp_done, 1)
                pool.wait_ge(tmp_done, count)
                nc.gpsimd.tensor_tensor(dst, tmp, half, ALU.pow).then_inc(done, 1)

            def norm(n, last):
                q = n % 2
                pool.wait_ge(stats, n + 1)
                after(pool, *last)
                inv_sqrt(mv[:, q, 1:2], 1.0, ve[:, q, :], g_ve, n + 1, rstd[:, q, :], g_rstd)

            for n in range(2 * NT):
                norm(n, (normed, n - 1))

            def weights(m, own, count):
                after(pool, own, count)
                pool.wait_ge(s_exp, m + 1)
                pool.wait_ge(s_rs, m + 1)
                after(pool, s_t, 4 * (m - 1))
                v = bd[S:P, m % 2, :].rearrange("p (h k) -> p h k", h=NH)[:, :, S:P]
                e_v = e_sb[S:P, :].rearrange("p (h k) -> p h k", h=NH)
                r = rsum[S:P, :].rearrange("p (h o) -> p h o", o=1).to_broadcast([S, NH, S])
                nc.gpsimd.tensor_tensor(v, e_v, r, ALU.mult).then_inc(s_ng, 1)
                pool.wait_ge(s_ng, m + 1)

            pool.wait_ge(in_cst, 16)
            hm = c("headmask").rearrange("p (h o) -> p h o", o=1).to_broadcast([P, 8, S])
            norm(2 * NT, (normed, 2 * NT - 1))
            for s in range(NT + 1):
                t0, t1 = s, s - 1
                if t0 + 1 < NT:
                    norm(2 * NT + t0 + 1, (normed, 2 * NT + t0))
                if t0 < NT:
                    after(pool, c_sc, t0)
                    for k in range(KC):
                        pool.wait_ge(c_qkc, 4 * t0 + 1 + k)
                        for b in range(2):
                            kT = qkT[:, t0 % 2, 1, k * P + S * b:k * P + S * b + S]
                            nc.gpsimd.tensor_tensor(
                                kbd[:, k, b, :].rearrange("p (h n) -> p h n", h=8),
                                kT.rearrange("p (o n) -> p o n", o=1).to_broadcast([P, 8, S]), hm,
                                ALU.mult).then_inc(c_kbd, 1)
                if t1 >= 0:
                    weights(t1, c_kbd, 4 * min(t0 + 1, NT))

            for s in range(NT + 4):
                t0, t1, t2, t3, t4 = s, s - 1, s - 2, s - 3, s - 4
                main, attn = 0 <= t1 < NT, 0 <= t2 < NT
                if t0 < NT:
                    norm(3 * NT + t0, (d_z, t0 - 1))
                if main:
                    for g in range(5):
                        pool.wait_ge(d_rope, 5 * t1 + g + 1)
                        after(pool, d_T, 5 * (t1 - 1) + g + 1)
                        nc.gpsimd.tensor_tensor(qr[:, g * 512:(g + 1) * 512], ra[:, g % 2, :], rb[:, g % 2, :],
                                                ALU.add).then_inc(d_radd, 1)
                        if g == 1 and t0 < NT:
                            pool.wait_ge(d_ss, t0 + 1)
                            after(pool, normed, 3 * NT + t0 - 1)
                            inv_sqrt(ss[:, t0 % 2, :], 1.0 / D, ms[:, t0 % 2, :], d_ms, t0 + 1, rms[:, t0 % 2, :], d_rms)
                elif t0 < NT:
                    pool.wait_ge(d_ss, t0 + 1)
                    inv_sqrt(ss[:, t0 % 2, :], 1.0 / D, ms[:, t0 % 2, :], d_ms, t0 + 1, rms[:, t0 % 2, :], d_rms)
                if main:
                    if t4 >= 1:
                        pool.wait_ge(e_sent[(t4 - 1) % 2], 32 * ((t4 - 1) // 2 + 1))
                    weights(NT + t1, d_radd, 5 * t1 + 5)
                if attn:
                    pool.wait_ge(e_ss, t2 + 1)
                    nc.gpsimd.tensor_scalar(gtmp[:, 4:5], th[:, :], 1.0 / D, LN_EPS, ALU.mult, ALU.add).then_inc(e_ms, 1)
                    pool.wait_ge(e_ms, t2 + 1)
                    nc.gpsimd.tensor_tensor(th[:, :], gtmp[:, 4:5], half, ALU.pow).then_inc(e_rms, 1)
                    nc.gpsimd.tensor_tensor(tile(X, t2), tile(X, t2), tile(XP, t2), ALU.add).then_inc(e_base, 1)
                if t4 >= 0:
                    pool.wait_ge(e_pos, t4 + 1)
                    pool.wait_ge(e_h2k, t4 + 1)
                    pool.wait_ge(filled, 16 * E * (T // P))
                    for k in range(2):
                        nc.gpsimd.indirect_dma_start(
                            slot_rows, bass.IndirectOffsetOnAxis(ap=pos[:, t4, k:k + 1], axis=0),
                            h2r[:, t4 % 2, k, :], None).then_inc(e_sent[t4 % 2], 16)

            def destinations(j, u):
                pool.wait_ge(f_in[u], 16 * (j // 3 + 1))
                nc.gpsimd.tensor_copy(ids[:, u:u + 1], hs[:, u, D:D + 1].bitcast(U32)).then_inc(f_ids, 1)
                pool.wait_ge(f_ids, at(j))

            def send(j, u):
                pool.wait_ge(f_ys, at(j))
                nc.gpsimd.indirect_dma_start(
                    result_rows, bass.IndirectOffsetOnAxis(ap=ids[:, u:u + 1], axis=0),
                    ys[:, u, :], None).then_inc(f_sent[u], 16)
                pool.wait_ge(f_sent[u], 16 * (j // 3 + 1))
                pool.sem_inc(f_left, 1)

            for j in range(TILES_F + 2):
                if j >= 2:
                    send(j - 2, (j - 2) % 3)
                if j < TILES_F:
                    destinations(j, j % 3)


def _constants():
    c = np.zeros((P, NCONST), np.float32)
    def put(name, v):
        a, b = CONST[name]
        c[:, a:b] = v
    p = np.arange(P)
    put("ident", np.eye(P))
    put("tri", p[:, None] < p[None, :])
    put("ones", 1.0)
    inv = np.float32(1000000.0) ** (-np.arange(0, HD, 2, dtype=np.float32) / np.float32(HD))
    ang = np.arange(S, dtype=np.float32)[p % S, None] * inv[None, :].astype(np.float32)
    put("cos", np.concatenate([np.cos(ang), np.cos(ang)], 1))
    put("sin", np.concatenate([-np.sin(ang), np.sin(ang)], 1))
    put("causal", np.where(np.arange(S)[None, :] <= (p % S)[:, None], 0.0, NEG))
    put("headmask", (p // HDC)[:, None] == np.arange(8)[None, :])
    put("ebase", T * np.arange(E)[None, :])
    put("iota_e", np.arange(E)[None, :])
    put("iota_t", np.arange(24)[None, :])
    words = c.view(np.uint32)
    t, k = np.meshgrid(np.arange(NT), np.arange(2), indexing="ij")
    a, b = CONST["dest"]
    words[:, a:b] = 2 * (t.reshape(1, -1) * P + p[:, None]) + k.reshape(1, -1)
    words[:, CONST["fill"][1] - 1] = 2 * T + p
    return c


_OUT = ((B, S, D), "float32")


def kernel(**inputs):
    import numpy as _np
    import concourse.bacc as _bacc
    from concourse import mybir as _mybir
    from concourse.bass_utils import run_bass_kernel_spmd as _run

    a = {k: _np.asarray(v) for k, v in inputs.items()}

    def chunks(w):
        n = w.shape[0] // P
        return w.reshape(n, P, w.shape[1]).transpose(1, 0, 2).reshape(P, -1)

    ctx = a["ctx_2048"].reshape(NT, P, D)
    ctxT = ctx.reshape(NT, P, KC, P).transpose(0, 3, 2, 1).reshape(NT, P, D)
    w1, w2 = (a[f"L0_ffn_{n}"].reshape(HID0, D).T for n in ("W1", "W2"))
    w3 = a["L0_ffn_W3"].transpose(0, 2, 1).reshape(HID0, D)
    even_odd = _np.concatenate([_np.arange(0, HD, 2), _np.arange(1, HD, 2)])
    wq = a["L1_ffn_wq"].reshape(D, NH, HD)[:, :, even_odd].reshape(D, NH * HD)
    wk = a["L1_ffn_wk"].reshape(D, KV, HD)[:, :, even_odd].reshape(D, KV * HD)
    f13 = _np.stack([a["L1_ffn_w1"], a["L1_ffn_w3"]], 2)
    f13 = f13.reshape(E, KC, P, 2 * FF).transpose(0, 2, 1, 3).reshape(E, P, KC * 2 * FF)
    f2 = a["L1_ffn_w2"].reshape(E, NCF, P, D).transpose(0, 2, 1, 3).reshape(E, P, NCF * D)
    arrays = {
        "x": a["x"],
        "ctx_a": _np.concatenate([ctx, ctxT], 2),
        "w_b": _np.concatenate([chunks(_np.concatenate([w1, w2], 1)), chunks(w3)], 1),
        "wg_b": chunks(a["L0_ffn_Wg"].T),
        "w_c": _np.concatenate([chunks(a[f"L1_xattn_W{n}"].T) for n in "qkvo"], 1),
        "b_c": _np.concatenate([a["L1_xattn_bq"].reshape(KC, P).T, a["L1_xattn_bk"].reshape(KC, P).T], 1),
        "rows_c": _np.broadcast_to(_np.concatenate([a["L1_xattn_bv"], a["L1_xattn_bo"], a["L1_ffn_ln_w"],
                                                    a["L1_ffn_ff_ln_w"]])[None, :], (P, len(ROWS) * D)),
        "w_qkv": chunks(_np.concatenate([wq, wk, a["L1_ffn_wv"]], 1)),
        "w_o": chunks(a["L1_ffn_wo"]),
        "gate_d": chunks(a["L1_ffn_gate_w"]),
        "w_f": _np.concatenate([f13, f2], 2).reshape(E * P, WF),
        "consts": _constants(),
    }
    nc = _bacc.Bacc("TRN2", target_bir_lowering=False, num_devices=1)
    feed, args = {}, {}
    for name, v in arrays.items():
        v = _np.ascontiguousarray(v)
        feed[f"in_{name}_dram"] = v
        args[name] = nc.dram_tensor(f"in_{name}_dram", v.shape, _mybir.dt.from_np(v.dtype), kind="ExternalInput").ap()
    out = nc.dram_tensor("out_0_dram", _OUT[0], _mybir.dt.from_np(_np.dtype(_OUT[1])), kind="ExternalOutput").ap()
    build(nc, out=out, **args)
    r = _run(nc, [feed], core_ids=[0])
    return r.results[0]["out_0_dram"]
```

```python
import math
from contextlib import ExitStack

import numpy as np

import concourse.bass as bass
from concourse import mybir

F32 = mybir.dt.float32
F32R = mybir.dt.float32r
U32 = mybir.dt.uint32
I32 = mybir.dt.int32
ALU = mybir.AluOpType
ACT = mybir.ActivationFunctionType
AX_X = mybir.AxisListType.X

P = 128
B, S, D = 16, 64, 256
T = B * S
NT = T // P
KC = D // P
KBD_SHARED = 1
E = 8
H0 = 176
HID0 = E * H0
NC0 = HID0 // P
GW = 2 * H0
NG0 = HID0 // GW
NH = 16
HDC = D // NH
HD = 128
KV = 4
FF = 896
NCF = FF // P
HF = FF // 2
WF = KC * 2 * FF + NCF * D
WB = KC * 2 * HID0 + NC0 * D
PIECE_B = WB // 6
TILES_F = 2 * T // P + E - 1
NSLOT = 3
ROW = D + 1
LN_EPS = 1e-5
NEG = -1.0e30

CONST = {}
_at = 0
for _name, _n in (("ident", P), ("tri", P), ("ones", P), ("cos", HD), ("sin", HD), ("causal", S),
                  ("headmask", 8), ("ebase", E), ("iota_e", E), ("dest", 2 * NT),
                  ("iota_t", 24), ("fill", ROW)):
    CONST[_name] = (_at, _at + _n)
    _at += _n
NCONST = _at
ROWS = ("bv", "bo", "ln_w", "ff_ln_w")


def after(eng, sem, count):
    if count > 0:
        eng.wait_ge(sem, count)


def build(nc, x, ctx_a, w_b, wg_b, w_c, b_c, rows_c, w_qkv, w_o, gate_d, w_f, consts, out):
    x_rows = x.rearrange("b s d -> (b s) d")
    out_rows = out.rearrange("b s d -> (b s) d")
    slots = nc.dram_tensor("slots", [E * T, ROW], F32)
    slot_rows = slots.ap()
    expert_out = nc.dram_tensor("expert_out", [2 * T + P, D], F32)
    result_rows = expert_out.ap()

    with ExitStack() as stack:
        def sb(name, shape, dt=F32):
            return stack.enter_context(nc.sbuf_tensor(name, shape, dt))

        def sem(name):
            return stack.enter_context(nc.semaphore(name))

        p0 = stack.enter_context(nc.psum_tensor("p0", [P, 512], F32))
        p1 = stack.enter_context(nc.psum_tensor("p1", [P, 512], F32))
        psc = stack.enter_context(nc.psum_tensor("psc", [P, 1024], F32))
        p4 = stack.enter_context(nc.psum_tensor("p4", [P, 512], F32))
        p5 = stack.enter_context(nc.psum_tensor("p5", [P, 512], F32))
        p6 = stack.enter_context(nc.psum_tensor("p6", [P, 512], F32))
        p7 = stack.enter_context(nc.psum_tensor("p7", [P, 512], F32))
        bank = [p0[:, :], p1[:, :], psc[:, 0:512], psc[:, 512:1024], p4[:, :], p5[:, :], p6[:, :], p7[:, :]]

        shapes = {
            "WM": [P, 2 * WB],
            "WQ": [P, KC * (NH + 2 * KV) * HD],
            "R1": [P, 9472],
            "R2": [P, 2048 + 1024 + 512],
            "aT": [P, NH * P],
            "xT": [P, 2, D],
            "xTl": [P, 2, D],
        }
        with ExitStack() as plain:
            tensors = {n: plain.enter_context(nc.sbuf_tensor(n, s, F32)) for n, s in shapes.items()}
        halves = {n: sb(n + "_halves", s, F32R) for n, s in shapes.items()}
        WM, WQ, R1, R2, aT, xT, xTl = tensors.values()

        def half(v):
            return bass.AP(halves[v.tensor.name], v.offset, v.ap)

        def half_value(v):
            return half(v).bitcast(F32)

        cst = sb("cst", [P, NCONST])
        X = sb("X", [P, NT * D])
        XP = sb("XP", [P, NT * D])
        rows = sb("rows", [P, len(ROWS) * D])
        wg = sb("wg", [P, KC * E])
        gd = sb("gd", [P, KC * E])
        bqk = sb("bqk", [P, 2 * KC])
        xn = sb("xn", [P, 2, D])
        vs = sb("vs", [P, 2, KV * HD])
        e_sb = sb("e_sb", [P, NH * S])
        bd = sb("bd", [P, 2, NH * P])
        stat = sb("stat", [P, 2, 6])
        mv = sb("mv", [P, 2, 2])
        ve = sb("ve", [P, 2, 1])
        rstd = sb("rstd", [P, 2, 1])
        ss = sb("ss", [P, 2, 1])
        ms = sb("ms", [P, 2, 1])
        rms = sb("rms", [P, 2, 1])
        mx = sb("mx", [P, NH])
        sums = sb("sums", [P, NH])
        rsum = sb("rsum", [P, NH])
        top = sb("top", [P, 8])
        topi = sb("topi", [P, 8], U32)
        topf = sb("topf", [P, 2])
        dif = sb("dif", [P, 1])
        th = sb("th", [P, 1])
        minus_half = sb("minus_half", [P, 1])
        pr = sb("pr", [P, 2 * NT])
        ids = sb("ids", [P, 3], U32)
        gates = sb("gates", [P, 2, E])
        gtmp = sb("gtmp", [P, E])
        hot = sb("hot", [P, NT, 2, E])
        cum = sb("cum", [P, NT + 1, E])
        msel = sb("msel", [P, NT, E])
        posf = sb("posf", [P, E])
        pos2 = sb("pos2", [P, 2, E])
        pos = sb("pos", [P, NT, 2], U32)
        tot_i = sb("tot_i", [P, E], I32)
        tl = sb("tl", [P, E])
        cinc = sb("cinc", [P, E])
        cmp_ = sb("cmp_", [P, 24, E])
        tabf = sb("tabf", [P, 8, 24])
        tab = sb("tab", [P, 4, 24], I32)

        def c(name, parts=slice(0, P)):
            a, b = CONST[name]
            return cst[parts, a:b]

        ident = c("ident")
        tile = lambda buf, t: buf[:, t * D:(t + 1) * D]
        bv_row, bo_row, lnw_row, ffw_row = (rows[:, i * D:(i + 1) * D] for i in range(4))
        wb_high, wb_low = WM[:, 0:WB], WM[:, WB:2 * WB]
        w12_b = [v[:, 0:KC * 2 * HID0].rearrange("p (k n) -> p k n", k=KC) for v in (wb_high, wb_low)]
        w3_b = [v[:, KC * 2 * HID0:].rearrange("p (c n) -> p c n", c=NC0) for v in (wb_high, wb_low)]
        wc = R1[:, 0:4 * KC * D].rearrange("p (w k n) -> p w k n", w=4, k=KC)
        n_q = KC * (NH + 2 * KV) * HD
        n_o = NH * D
        wq_high, wq_low = WQ[:, :], WM[:, 0:n_q]
        wo_low, wo_high = WM[:, n_q:n_q + n_o], WM[:, n_q + n_o:n_q + 2 * n_o]
        sq_junk = WM[:, n_q + 2 * n_o:n_q + 2 * n_o + D]
        n_m = n_q + 2 * n_o + D
        ident_h, causal_h = WM[:, n_m:n_m + P], WM[:, n_m + P:n_m + P + S]
        last_pieces = ((0, 6), (1, 7, 2), (3, 4, 5))
        wqkv = [v.rearrange("p (k n) -> p k n", k=KC) for v in (wq_high, wq_low)]
        wo_d = [v.rearrange("p (h n) -> p h n", h=NH) for v in (wo_high, wo_low)]
        ctxb = WQ[:, 0:NT * 2 * D].rearrange("p (t n) -> p t n", t=NT)
        sg = R1[:, 0:2048].rearrange("p (q b n) -> p q b n", q=2, b=2)
        xz = R1[:, 2048:3072].rearrange("p (q b n) -> p q b n", q=2, b=2)
        act_b = R1[:, 2048:4864].rearrange("p (q n) -> p q n", q=2)
        actT_b = R1[:, 4864:7680].rearrange("p (q n) -> p q n", q=2)
        actTl_b = [aT[:, 0:NC0 * P], R2[:, 0:NC0 * P]]
        silu_b = R1[:, 7680:8384].rearrange("p (q n) -> p q n", q=2)
        kbd = R2[:, 0:2048].rearrange("p (c b n) -> p c b n", c=KC, b=2)
        qkT = R2[:, 2048:3072].rearrange("p (q w n) -> p q w n", q=2, w=2)
        cx = R2[:, 3072:3328]
        cxT = R2[:, 3328:3584]
        vs_c = vs[:, :, :].rearrange("p q (r n) -> p (q r) n", r=2)
        ra = R1[:, 0:1024].rearrange("p (q n) -> p q n", q=2)
        rb = R1[:, 1024:2048].rearrange("p (q n) -> p q n", q=2)
        qr = R1[:, 2048:4608]
        qT = R1[:, 4608:7168]
        oT = [R1[:, 7168:9216], R2[:, 1536:3584]]
        h2T = R1[:, 9216:9472]
        h2r = R2[:, 0:4 * ROW].rearrange("p (q k n) -> p q k n", q=2, k=2)
        hs = R1[:, 0:3 * ROW].rearrange("p (q n) -> p q n", q=3)
        hsT = R1[:, 772:772 + 3 * D].rearrange("p (q n) -> p q n", q=3)
        act_f = R1[:, 1540:1540 + 3 * FF].rearrange("p (q n) -> p q n", q=3)
        actT_f = R1[:, 4228:4228 + 3 * FF].rearrange("p (q n) -> p q n", q=3)
        silu_f = R1[:, 6916:6916 + 2 * HF].rearrange("p (q n) -> p q n", q=2)
        ys = R1[:, 7812:7812 + 3 * D].rearrange("p (q n) -> p q n", q=3)
        yk = WQ[:, 0:NT * 2 * D].rearrange("p (t k n) -> p t k n", t=NT, k=2)

        in_cst, in_wg, in_wc, in_rows, in_wq, in_wo, in_gd, in_wf = (
            sem(n) for n in "in_cst in_wg in_wc in_rows in_wq in_wo in_gd in_wf".split())
        in_wb = [sem("in_wb0"), sem("in_wb1")]
        wb_hi, wb_lo, wq_hi, wq_lo, wo_hi, wo_lo = (sem(n) for n in "wb_hi wb_lo wq_hi wq_lo wo_hi wo_lo".split())
        in_x = [sem("in_x0"), sem("in_x1"), sem("in_x_rest")]
        in_ctx = [sem(f"in_ctx{t}") for t in range(NT)]
        filled, halved, zeroed, masked = sem("filled"), sem("halved"), sem("zeroed"), sem("masked")
        chain = sem("v_chain")
        stats, g_ve, g_rstd, normed = (sem(n) for n in "stats g_ve g_rstd normed".split())
        res = sem("res")
        a_sc, a_sig, a_out = (sem(n) for n in "a_sc a_sig a_out".split())
        t_x, c_x, c_xl = sem("t_x"), sem("c_x"), sem("c_xl")
        b_lg, b_log, b_th, b_gate, b_h, b_silu, b_mul, b_t, b_tA, b_tD, b_y, b_dif = (
            sem(n) for n in "b_lg b_log b_th b_gate b_h b_silu b_mul b_t b_tA b_tD b_y b_dif".split())
        c_qk, c_qkc, c_v, c_vc, c_kbd, c_sc, c_av, c_cx, c_ct, c_ctc, c_wo = (
            sem(n) for n in "c_qk c_qkc c_v c_vc c_kbd c_sc c_av c_cx c_ct c_ctc c_wo".split())
        s_sub, s_exp, s_rs, s_nv, s_ng, s_t, s_cA, s_cD = (
            sem(n) for n in "s_sub s_exp s_rs s_nv s_ng s_t s_cA s_cD".split())
        d_z, d_ss, d_ms, d_rms, d_pj, d_rope, d_radd, d_vc, d_T, d_qc, d_sc, d_av, d_oA, d_oD, d_wo, d_xp = (
            sem(n) for n in ("d_z d_ss d_ms d_rms d_pj d_rope d_radd d_vc d_T d_qc d_sc d_av d_oA "
                             "d_oD d_wo d_xp").split())
        e_ss, e_ms, e_rms, e_h2, e_h2k, e_base, e_T, e_Tc, e_lg, e_dif, e_th, e_sel, e_rank, e_pos = (
            sem(n) for n in ("e_ss e_ms e_rms e_h2 e_h2k e_base e_T e_Tc e_lg e_dif e_th e_sel "
                             "e_rank e_pos").split())
        e_sent = [sem("e_sent0"), sem("e_sent1")]
        e_tot, tables = sem("e_tot"), sem("tables")
        f_in = [sem(f"f_in{i}") for i in range(3)]
        f_w = [sem(f"f_w{i}") for i in range(3)]
        f_sent = [sem(f"f_sent{i}") for i in range(3)]
        f_t, f_tc, f_h, f_silu, f_mul, f_T, f_Tc, f_y, f_ys, f_left, f_ids = (
            sem(n) for n in "f_t f_tc f_h f_silu f_mul f_T f_Tc f_y f_ys f_left f_ids".split())
        g_in = [sem(f"g_in{t}") for t in range(NT)]
        g_first, g_sum, g_out = sem("g_first"), sem("g_sum"), sem("g_out")

        LEAD = 3
        F_PER = ((f_t, 1), (f_tc, 1), (f_h, 4), (f_silu, 2), (f_mul, 2), (f_T, 2), (f_Tc, 2), (f_y, 1), (f_ys, 1),
                 (f_left, 1), (f_ids, 1))

        def at(j, per=1, g=0):
            return per * (j + LEAD) + g + 1

        def attn_bank(m, u):
            return bank[((7, 6, 5, 6) if m < NT else (4, 5, 7, 6))[u]]

        def proj_bank(g):
            return bank[(0, 1, 4, 5, 0, 1)[g]]

        def steps(eng):
            eng.wait_ge(tables, 1)
            return eng.value_load(tab[0:1, 0, TILES_F:TILES_F + 1], min_val=2 * T // P + 2, max_val=TILES_F + 2)

        block = stack.enter_context(nc.Block())

        @block.sync
        def _(sp):
            for t in range(NT):
                sp.dma_start(tile(X, t), x_rows[t * P:(t + 1) * P, :]).then_inc(in_x[min(t, 2)], 16)
                sp.dma_start(ctxb[:, t, :], ctx_a[t]).then_inc(in_ctx[t], 16)
            sp.dma_start(cst[:, :], consts).then_inc(in_cst, 16)
            n12 = KC * 2 * HID0
            sp.dma_start(wb_low[:, 0:n12], w_b[:, 0:n12]).then_inc(in_wb[0], 16)
            sp.dma_start(wb_low[:, n12:], w_b[:, n12:]).then_inc(in_wb[1], 16)
            sp.dma_start(wg[:, :], wg_b).then_inc(in_wg, 16)
            sp.dma_start(bqk[:, :], b_c).then_inc(in_wc, 16)
            sp.dma_start(rows[:, :], rows_c).then_inc(in_rows, 16)
            sp.dma_start(gd[:, :], gate_d).then_inc(in_gd, 16)
            sp.wait_ge(a_out, 2 * NT)
            sp.dma_start(R1[:, 0:4 * KC * D], w_c).then_inc(in_wc, 16)
            sp.wait_ge(in_cst, 16)
            fill = cst[:, CONST["fill"][0]:CONST["fill"][1]]
            for e in range(E):
                for r in range(T // P):
                    r0 = e * T + r * P
                    sp.dma_start(slot_rows[r0:r0 + P, :], fill).then_inc(filled, 16)
            sp.wait_ge(b_y, NT)
            sp.dma_start(wq_low, w_qkv).then_inc(in_wq, 16)
            sp.dma_start(wo_low, w_o).then_inc(in_wo, 16)
            for e, (done, count) in enumerate(((d_pj, 6 * NT), (d_wo, NT))):
                sp.wait_ge(done, count)
                sp.dma_start(WM[:, e * WF:(e + 1) * WF], w_f[e * P:(e + 1) * P, :]).then_inc(in_wf, 16)
            for u in range(2):
                sp.wait_ge(e_sent[u], 32 * (NT // 2))
            sp.dma_start(hs[:, 0, :], slot_rows[0:P, :]).then_inc(f_in[0], 16)
            count = steps(sp)

            def load(j):
                base = sp.value_load(tab[0:1, 0, bass.ds(j, 1)], min_val=0, max_val=E * T - P)
                wrow = sp.value_load(tab[0:1, 1, bass.ds(j, 1)], min_val=0, max_val=(E - 1) * P)
                slot = sp.value_load(tab[0:1, 2, bass.ds(j, 1)], min_val=0, max_val=(NSLOT - 1) * WF)
                fresh = sp.value_load(tab[0:1, 3, bass.ds(j, 1)], min_val=0, max_val=1)
                return base, wrow, slot, fresh

            def fetch(j, u):
                base, wrow, slot, fresh = load(j)
                with sp.If(count > j):
                    sp.wait_ge(f_t, at(j - 3))
                    sp.wait_ge(f_ids, at(j - 3))
                    sp.dma_start(hs[:, u, :], slot_rows[bass.ds(base, P), :]).then_inc(f_in[u], 16)
                with sp.If(count > j + 1):
                    sp.wait_ge(f_y, at(j - 3))
                    sp.dma_start(WM[:, bass.ds(slot, WF)], w_f[bass.ds(wrow, P), :],
                                 cond=(fresh > 0)).then_inc(f_w[u], 16)

            with sp.Fori(0, (TILES_F - 1) // 3) as i:
                for u in range(1, 4):
                    fetch(3 * i + u, u % 3)
            for j in range((TILES_F - 1) // 3 * 3 + 1, TILES_F):
                fetch(j, j % 3)

            sp.wait_ge(f_left, count - 2 + LEAD)
            for t in range(NT):
                sp.dma_start(yk[:, t], result_rows[2 * t * P:2 * (t + 1) * P, :]
                             .rearrange("(p k) n -> p k n", k=2)).then_inc(g_in[t], 16)
            for t in range(NT):
                sp.wait_ge(g_sum, t + 1)
                sp.dma_start(out_rows[t * P:(t + 1) * P, :], tile(X, t)).then_inc(g_out, 16)
            sp.wait_ge(g_out, 16 * NT)

        @block.tensor
        def _(pe):
            def products(out, terms):
                terms = [(a[i], b[j]) for a, b in terms for i, j in ((0, 0), (0, 1), (1, 0))]
                for n, (a, b) in enumerate(terms):
                    mm = pe.matmul(out, half(a), half(b), start=(n == 0), stop=(n == len(terms) - 1))
                return mm

            def x_halves(m, k):
                return [v[:, m % 2, k * P:(k + 1) * P] for v in (xT, xTl)]

            def a_scores(t):
                q = t % 2
                pe.wait_ge(in_ctx[t], 16)
                pe.wait_ge(normed, t + 1)
                for b in range(2):
                    after(pe, a_sig, 2 * (t - 2) + b + 1)
                    for k in range(KC):
                        mm = pe.matmul(bank[2 * q + b][:, k * D:(k + 1) * D], xz[:, q, b, k * P:(k + 1) * P],
                                       ctxb[:, t, 0:D], start=True, stop=True)
                    mm.then_inc(a_sc, 1)

            def a_outs(t):
                q = t % 2
                after(pe, res, t - 1)
                for b in range(2):
                    pe.wait_ge(a_sig, 2 * t + b + 1)
                    for k in range(KC):
                        mm = pe.matmul(bank[4 + q][S * b:S * b + S, 0:D],
                                       ctxb[:, t, D + k * P + S * b:D + k * P + S * b + S],
                                       sg[:, q, b, k * D:(k + 1) * D], start=(k == 0), stop=(k == KC - 1))
                    mm.then_inc(a_out, 1)

            for s in range(NT + 1):
                if s < NT:
                    a_scores(s)
                if s >= 1:
                    a_outs(s - 1)

            def turn_x(m, dst, guard):
                pe.wait_ge(normed, NT + m + 1)
                after(pe, *guard)
                for k in range(KC):
                    mm = pe.transpose(dst[:, k * P:(k + 1) * P], xn[:, m % 2, k * P:(k + 1) * P], ident)
                mm.then_inc(t_x, 1)

            def b_gates(t):
                pe.wait_ge(c_xl, t + 1)
                for k in range(KC):
                    for i, x_ in enumerate(x_halves(t, k)):
                        mm = pe.matmul(bank[5][:, D:D + E], half_value(x_), wg[:, k * E:(k + 1) * E],
                                       start=(k == 0 and i == 0), stop=(k == KC - 1 and i == 1))
                mm.then_inc(b_lg, 1)

            def b_hidden(t, g):
                pe.wait_ge(c_xl, t + 1)
                pe.wait_ge(wb_lo, 4)
                n = NG0 * t + g
                for w, free in ((0, b_silu), (1, b_mul)):
                    after(pe, free, n - 1)
                    o = w * HID0 + g * GW
                    products(bank[2 * w + g % 2][:, 0:GW],
                             [(x_halves(t, k), [v[:, k, o:o + GW] for v in w12_b]) for k in range(KC)]).then_inc(b_h, 1)

            def b_turn(t, u):
                chunks = range(4 * u, min(4 * u + 4, NC0))
                pe.wait_ge(b_mul, NG0 * t + u + 2)
                after(pe, b_tD, (3 * t, 3 * t - 1, 3 * t + 1)[u])
                for i, ch in enumerate(chunks):
                    mm = pe.transpose(bank[6 + u % 2][:, i * P:(i + 1) * P],
                                      act_b[:, t % 2, ch * P:(ch + 1) * P], ident)
                mm.then_inc(b_t, 1)

            def b_down(t):
                pe.wait_ge(b_tD, 3 * t + 3)
                pe.wait_ge(wb_lo, 6)
                after(pe, res, NT + t)
                halves = (actT_b[:, t % 2, :], actTl_b[t % 2])
                products(bank[4][:, 0:D], [([v[:, ch * P:(ch + 1) * P] for v in halves], [v[:, ch, :] for v in w3_b])
                                           for ch in range(NC0)]).then_inc(b_y, 1)

            pe.wait_ge(in_cst, 16)
            pe.wait_ge(in_wg, 16)
            pe.wait_ge(res, NT)
            for s in range(NT + 2):
                t0, t1, t2 = s, s - 1, s - 2
                main = 0 <= t1 < NT
                if main:
                    b_hidden(t1, 0)
                if t2 >= 0:
                    b_turn(t2, 2)
                if main:
                    b_hidden(t1, 1)
                if t0 < NT:
                    turn_x(t0, bank[5], (b_log, t0))
                if main:
                    b_hidden(t1, 2)
                if t2 >= 0:
                    b_down(t2)
                if main:
                    b_turn(t1, 0)
                if t0 < NT:
                    b_gates(t0)
                if main:
                    b_hidden(t1, 3)
                    b_turn(t1, 1)

            def turn_attn(m, u, guard):
                pe.wait_ge(s_nv, m + 1)
                pe.wait_ge(s_ng, m + 1)
                for g in guard:
                    after(pe, *g)
                for i in range(4):
                    h = 4 * u + i
                    mm = pe.transpose(attn_bank(m, u)[:, i * P:(i + 1) * P], bd[:, m % 2, h * P:(h + 1) * P], ident)
                mm.then_inc(s_t, 1)

            def c_project(t):
                m, q = NT + t, t % 2
                pe.wait_ge(c_x, m + 1)
                after(pe, c_qkc, 4 * t)
                for w in (1, 0):
                    for n in range(KC):
                        for k in range(KC):
                            rhs = xT[:, m % 2, k * P:(k + 1) * P] if w == 0 else ctxb[:, t, D + k * P:D + (k + 1) * P]
                            mm = pe.matmul(bank[1][:, (2 * w + n) * P:(2 * w + n + 1) * P],
                                           wc[:, w, k, n * P:(n + 1) * P], rhs, start=(k == 0), stop=(k == KC - 1))
                    mm.then_inc(c_qk, 1)
                for k in range(KC):
                    mm = pe.matmul(bank[0][:, D:2 * D], ctxb[:, t, D + k * P:D + (k + 1) * P], wc[:, 2, k, :],
                                   start=(k == 0), stop=(k == KC - 1))
                mm.then_inc(c_v, 1)

            def c_scores(t):
                q = t % 2
                pe.wait_ge(c_kbd, 4 * t + 4)
                pe.wait_ge(c_qkc, 4 * t + 4)
                after(pe, s_sub, t)
                for k in range(KC):
                    for b in range(2):
                        mm = pe.matmul(bank[2 + k][S * b:S * b + S, :], qkT[:, q, 0, k * P + S * b:k * P + S * b + S],
                                       kbd[:, k, b, :], start=True, stop=True)
                mm.then_inc(c_sc, 1)

            def c_values(t):
                q = t % 2
                pe.wait_ge(c_vc, t + 1)
                after(pe, c_cx, t)
                for u in range(4):
                    after(pe, (s_cA, s_cD)[u % 2], 2 * t + u // 2 + 1)
                    for h in range(4 * u, 4 * u + 4):
                        mm = pe.matmul(bank[4][:, h * HDC:(h + 1) * HDC], aT[:, h * P:(h + 1) * P],
                                       vs_c[:, t % 4, h * HDC:(h + 1) * HDC], start=True, stop=True)
                mm.then_inc(c_av, 1)

            def c_turn(t):
                pe.wait_ge(c_cx, t + 1)
                after(pe, s_cA, 2 * (t + 1))
                after(pe, res, 2 * NT + t)
                for k in range(KC):
                    mm = pe.transpose(bank[5][:, k * P:(k + 1) * P], cx[:, k * P:(k + 1) * P], ident)
                mm.then_inc(c_ct, 1)

            def c_outs(t):
                pe.wait_ge(c_ctc, t + 1)
                for k in range(KC):
                    mm = pe.matmul(bank[5][:, D:2 * D], cxT[:, k * P:(k + 1) * P], wc[:, 3, k, :],
                                   start=(k == 0), stop=(k == KC - 1))
                mm.then_inc(c_wo, 1)

            pe.wait_ge(in_wc, 32)
            pe.wait_ge(res, 2 * NT)
            turn_x(NT, bank[0], (c_vc, 0))
            for s in range(NT + 3):
                t0, t1, t2, t3 = s, s - 1, s - 2, s - 3
                attn = 0 <= t2 < NT
                if 0 <= t1 < NT:
                    c_scores(t1)
                if t3 >= 0:
                    c_turn(t3)
                if t0 < NT:
                    c_project(t0)
                if t3 >= 0:
                    c_outs(t3)
                if attn:
                    for u in range(2):
                        turn_attn(t2, u, [((s_cA, s_cD)[u % 2], 2 * t2 + u // 2)])
                if t0 + 1 < NT:
                    turn_x(NT + t0 + 1, bank[0], (c_vc, t0 + 1))
                if attn:
                    turn_attn(t2, 2, [(res, 2 * NT + t3 + 1)])
                    turn_attn(t2, 3, [(s_cD, 2 * t2 + 1)])
                    c_values(t2)
                if s == NT + 1:
                    turn_x(2 * NT, bank[6], (s_cA, 2 * NT))

            def d_project(t, g):
                m = 2 * NT + t
                if g == 0:
                    pe.wait_ge(c_xl, NT + t + 1)
                if t == 0:
                    pe.wait_ge(wq_lo, (6, 8, 9, 10, 11, 12)[g])
                    if g == 2:
                        pe.wait_ge(res, 3 * NT)
                if g == 0:
                    after(pe, e_pos, t - 3)
                after(pe, *((d_rope, 5 * t), (d_xp, t - 1), (d_oD, 4 * (t - 1)), (d_oD, 4 * (t - 1)),
                            (d_rope, 5 * t + 1), (d_rope, 5 * t + 2))[g])
                products(proj_bank(g), [(x_halves(m, k), [v[:, k, g * 512:(g + 1) * 512] for v in wqkv])
                                       for k in range(KC)]).then_inc(d_pj, 1)

            def d_turn(t, g):
                pe.wait_ge(d_radd, 5 * t + g + 1)
                after(pe, *((c_xl, NT + t + 1), (d_oD, 4 * (t - 1)), (d_qc, 5 * t + 1), (d_qc, 5 * t + 2),
                            (d_qc, 5 * t + 3))[g])
                if g < 2:
                    after(pe, (s_cD, s_cA)[g], 2 * (NT + t - 1))
                for i in range(4):
                    mm = pe.transpose(bank[6 + g % 2][:, i * P:(i + 1) * P],
                                      qr[:, g * 512 + i * P:g * 512 + (i + 1) * P], ident)
                mm.then_inc(d_T, 1)

            def d_scores(t):
                pe.wait_ge(d_qc, 5 * t + 5)
                pe.wait_ge(s_sub, NT + t)
                pe.wait_ge(masked, 2)
                causal = half(causal_h).rearrange("p (o k) -> p o k", o=1).to_broadcast([P, NH // 2, S])
                for i in range(2):
                    pe.matmul(psc[:, i * 512:(i + 1) * 512].rearrange("p (h k) -> p h k", h=NH // 2),
                              half(ident_h), causal, start=True, stop=False)
                for h in range(NH):
                    kv = NH + h // (NH // KV)
                    for b in range(2):
                        mm = pe.matmul(psc[S * b:S * b + S, h * S:(h + 1) * S],
                                       qT[:, h * P + S * b:h * P + S * b + S],
                                       qT[:, kv * P + S * b:kv * P + S * b + S],
                                       start=False, stop=(h % 8 == 7))
                mm.then_inc(d_sc, 1)

            def d_values(t):
                m = NT + t
                pe.wait_ge(d_vc, t + 1)
                for kv in range(KV):
                    after(pe, (s_cA, s_cD)[kv % 2], 2 * m + kv // 2 + 1)
                    pe.matmul(attn_bank(m, kv), vs[:, m % 2, kv * HD:(kv + 1) * HD],
                              aT[:, kv * 512:(kv + 1) * 512], start=True, stop=True).then_inc(d_av, 1)

            def d_outs(t, last_values, heads):
                if heads.start == 0:
                    pe.wait_ge(wo_lo, 4)
                    after(pe, d_vc, last_values)
                for h in heads:
                    if h % 4 == 0:
                        pe.wait_ge(d_oD, 4 * t + h // 4 + 1)
                    for i, j in ((0, 0), (0, 1), (1, 0)):
                        mm = pe.matmul(bank[1][:, 0:D], half(oT[i][:, h * P:(h + 1) * P]), half(wo_d[j][:, h, :]),
                                       start=(h == 0 and i == j), stop=(h == NH - 1 and i == 1))
                if heads.stop == NH:
                    mm.then_inc(d_wo, 1)

            def e_turn(t):
                pe.wait_ge(e_h2, t + 1)
                pe.wait_ge(d_rope, 5 * min(t + 3, NT))
                after(pe, e_pos, t)
                for k in range(KC):
                    mm = pe.transpose(bank[0][:, k * P:(k + 1) * P], h2r[:, t % 2, 0, k * P:(k + 1) * P], ident)
                mm.then_inc(e_T, 1)

            def e_logits(t):
                pe.wait_ge(e_Tc, t + 1)
                for k in range(KC):
                    mm = pe.matmul(bank[0][:, D:D + E], h2T[:, k * P:(k + 1) * P], gd[:, k * E:(k + 1) * E],
                                   start=(k == 0), stop=(k == KC - 1))
                mm.then_inc(e_lg, 1)

            def e_ranks(t):
                pe.wait_ge(e_sel, t + 1)
                out = bank[0][:, D + E:D + 2 * E]
                pe.matmul(out, c("ones"), cum[:, t, :], start=True, stop=False)
                pe.matmul(out, c("tri"), msel[:, t, :], start=False, stop=True).then_inc(e_rank, 1)

            pe.wait_ge(in_gd, 16)
            for s in range(1, NT + 3):
                t0, t1, t2, t3 = s, s - 1, s - 2, s - 3
                main, attn = 0 <= t1 < NT, 0 <= t2 < NT
                if main:
                    for g in range(6):
                        d_project(t1, g)
                        if g >= 3:
                            d_turn(t1, g - 3)
                if attn:
                    turn_attn(NT + t2, 0, [(d_oD, 4 * t2), (d_rope, min(5 * t1 + 3, 5 * NT))])
                if main:
                    d_turn(t1, 3)
                if attn:
                    turn_attn(NT + t2, 1, [(d_oD, 4 * t2), (d_rope, min(5 * t1 + 4, 5 * NT))])
                if main:
                    d_turn(t1, 4)
                if t3 >= 0:
                    e_turn(t3)
                if attn:
                    turn_attn(NT + t2, 2, [(d_qc, min(5 * t1 + 4, 5 * NT))])
                    turn_attn(NT + t2, 3, [(d_qc, min(5 * t1 + 5, 5 * NT))])
                if main:
                    d_scores(t1)
                if t3 >= 0:
                    e_logits(t3)
                if attn:
                    d_values(t2)
                    d_outs(t2, min(t1 + 1, NT), range(0, NH // 2))
                if t0 < NT:
                    turn_x(2 * NT + t0, bank[6], (d_oD, 4 * t2 + 4 if attn else 0))
                if t3 >= 0:
                    e_ranks(t3)
                if attn:
                    d_outs(t2, min(t1 + 1, NT), range(NH // 2, NH))
            pe.wait_ge(e_pos, NT)
            pe.wait_ge(d_oD, 4 * NT)
            pe.matmul(bank[4][:, 8:8 + E], c("ones"), cum[:, NT, :], start=True, stop=True).then_inc(e_tot, 1)

            def f_turn_x(j, u, k3):
                pe.wait_ge(f_in[u], 16 * k3 + 16)
                pe.wait_ge(f_tc, at(j - 1))
                for k in range(KC):
                    mm = pe.transpose(bank[5][:, k * P:(k + 1) * P], hs[:, u, k * P:(k + 1) * P], ident)
                mm.then_inc(f_t, 1)

            def f_hidden(j, u, k3, n, slot, first):
                if n == 0:
                    pe.wait_ge(f_tc, at(j))
                    if first:
                        pe.wait_ge(in_wf, 32)
                    else:
                        pe.wait_ge(f_w[u], 16 * k3 + (16 if u else 0))
                for w, free in ((0, f_silu), (1, f_mul)):
                    pe.wait_ge(free, at(j - 1, 2, n))
                    for k in range(KC):
                        o = (2 * k + w) * FF + n * HF
                        mm = pe.matmul(bank[2 * w + n][:, 0:HF], hsT[:, u, k * P:(k + 1) * P],
                                       WM[:, bass.ds(slot + o, HF)], start=(k == 0), stop=(k == KC - 1))
                    mm.then_inc(f_h, 1)

            def f_turn(j, u, n):
                chunks = (range(0, 3), range(3, NCF))[n]
                pe.wait_ge(f_mul, at(j, 2, n))
                pe.wait_ge(f_Tc, at(j - 1, 2, n))
                for i, ch in enumerate(chunks):
                    mm = pe.transpose(bank[6 + n][:, i * P:(i + 1) * P], act_f[:, u, ch * P:(ch + 1) * P], ident)
                mm.then_inc(f_T, 1)

            def f_down(j, u, slot):
                pe.wait_ge(f_Tc, at(j, 2, 1))
                pe.wait_ge(f_ys, at(j - 1))
                for ch in range(NCF):
                    mm = pe.matmul(bank[4][:, 0:D], actT_f[:, u, ch * P:(ch + 1) * P],
                                   WM[:, bass.ds(slot + KC * 2 * FF + ch * D, D)],
                                   start=(ch == 0), stop=(ch == NCF - 1))
                mm.then_inc(f_y, 1)

            def f_step(s, sx, first=False, head=True, main=True, tail=True):
                def of(lag):
                    k3, u = sx[0], sx[1] - lag
                    return s - lag, u % 3, k3 + u // 3
                j0, u0, k0 = of(0)
                j1, u1, k1 = of(1)
                j2, u2, k2 = of(2)
                if main:
                    slot1 = 0
                    if not first:
                        slot1 = pe.value_load(tab[0:1, 2, bass.ds(j1, 1)], min_val=0, max_val=(NSLOT - 1) * WF)
                    f_hidden(j1, u1, k1, 0, slot1, first)
                if tail:
                    f_turn(j2, u2, 1)
                if head:
                    f_turn_x(j0, u0, k0)
                if main:
                    f_hidden(j1, u1, k1, 1, slot1, first)
                if tail:
                    slot2 = pe.value_load(tab[0:1, 2, bass.ds(j2, 1)], min_val=0, max_val=(NSLOT - 1) * WF)
                    f_down(j2, u2, slot2)
                if main:
                    f_turn(j1, u1, 0)

            f_step(0, (0, 0), main=False, tail=False)
            f_step(1, (0, 1), first=True, tail=False)
            count = steps(pe)
            with pe.Fori(0, (TILES_F - 2) // 3) as i:
                for u in range(3):
                    with pe.If(count > 3 * i + 2 + u):
                        f_step(3 * i + 2 + u, (i + (2 + u) // 3, (2 + u) % 3))
            with pe.If(count > TILES_F):
                f_step(TILES_F, (TILES_F // 3, TILES_F % 3), head=False)
            with pe.If(count > TILES_F + 1):
                f_step(TILES_F + 1, ((TILES_F + 1) // 3, (TILES_F + 1) % 3), head=False, main=False)

        @block.scalar
        def _(act):
            def split_b(i):
                act.wait_ge(in_wb[i * PIECE_B // (KC * 2 * HID0)], 16)
                v = slice(i * PIECE_B, (i + 1) * PIECE_B)
                nc.scalar.copy(half(wb_high[:, v]), wb_low[:, v]).then_inc(wb_hi, 1)

            for t in range(NT):
                for b in range(2):
                    act.wait_ge(a_sc, 2 * t + b + 1)
                    after(act, a_out, 2 * (t - 2) + b + 1)
                    nc.scalar.activation(sg[:, t % 2, b, :], bank[2 * (t % 2) + b], ACT.Sigmoid,
                                         scale=1.0 / math.sqrt(S)).then_inc(a_sig, 1)
                if t >= 4:
                    split_b(t - 4)
            split_b(4)
            split_b(5)

            def copy_x(m, src, free):
                act.wait_ge(t_x, m + 1)
                after(act, *free)
                dst = xT[:, m % 2, :]
                nc.scalar.copy(dst if NT <= m < 2 * NT else half(dst), src[:, 0:D]).then_inc(c_x, 1)

            def b_silus(t, g):
                n = NG0 * t + g
                act.wait_ge(b_h, 2 * n + 1)
                after(act, b_mul, n - 1)
                nc.scalar.activation(silu_b[:, g % 2, :], bank[g % 2][:, 0:GW], ACT.Silu).then_inc(b_silu, 1)

            def b_copy(t, u):
                act.wait_ge(b_t, 3 * t + u + 1)
                after(act, b_y, t - 1)
                n = (min(4 * u + 4, NC0) - 4 * u) * P
                nc.scalar.copy(half(actT_b[:, t % 2, 4 * u * P:4 * u * P + n]), bank[6 + u % 2][:, 0:n]).then_inc(b_tA, 1)

            for s in range(NT + 2):
                t0, t1, t2 = s, s - 1, s - 2
                main = 0 <= t1 < NT
                if main:
                    b_silus(t1, 0)
                if t2 >= 0:
                    b_copy(t2, 2)
                if main:
                    b_silus(t1, 1)
                if t0 < NT:
                    copy_x(t0, bank[5], (b_h, 2 * NG0 * (t0 - 1)))
                if main:
                    b_silus(t1, 2)
                    b_copy(t1, 0)
                if t0 < NT:
                    act.wait_ge(b_dif, t0 + 1)
                    nc.scalar.activation(th[:, :], dif[:, :], ACT.Tanh, scale=0.5).then_inc(b_th, 1)
                if main:
                    b_silus(t1, 3)
                    b_copy(t1, 1)

            def exps(m, scale):
                act.wait_ge(s_sub, m + 1)
                nc.scalar.activation(e_sb[:, :], e_sb[:, :], ACT.Exp, scale=scale).then_inc(s_exp, 1)

            def copy_attn(m, u, free):
                act.wait_ge(s_t, 4 * m + u + 1)
                after(act, *free)
                nc.scalar.copy(aT[:, u * 512:(u + 1) * 512], attn_bank(m, u)).then_inc((s_cA, s_cD)[u % 2], 1)

            act.wait_ge(in_wc, 32)
            def copy_qk(t):
                act.wait_ge(c_qk, 2 * t + 2)
                after(act, c_sc, t - 1)
                after(act, c_kbd, 4 * (t - 1))
                for w in (1, 0):
                    for n in range(KC):
                        nc.scalar.activation(qkT[:, t % 2, w, n * P:(n + 1) * P],
                                             bank[1][:, (2 * w + n) * P:(2 * w + n + 1) * P], ACT.Identity,
                                             bias=bqk[:, 2 * w + n:2 * w + n + 1]).then_inc(c_qkc, 1)

            def split(high, low, i, n, ready, done):
                act.wait_ge(ready, 16)
                v = slice(i * n, (i + 1) * n)
                nc.scalar.copy(half(high[:, v]), low[:, v]).then_inc(done, 1)

            def squares(t):
                act.wait_ge(d_z, t + 1)
                after(act, d_ms, t - 1)
                after(act, d_ss, t)
                after(act, e_ss, min(t - 3, NT))
                nc.scalar.activation(sq_junk, tile(XP, t), ACT.Square, accum_out=ss[:, t % 2, :]).then_inc(d_ss, 1)

            copy_x(NT, bank[0], (c_x, NT))
            for s in range(NT + 3):
                t0, t1, t2, t3 = s, s - 1, s - 2, s - 3
                attn = 0 <= t2 < NT
                if t3 >= 0:
                    act.wait_ge(c_ct, t3 + 1)
                    after(act, c_wo, t3)
                    nc.scalar.copy(cxT, bank[5][:, 0:D]).then_inc(c_ctc, 1)
                if s == NT + 1:
                    squares(0)
                if t0 < NT:
                    copy_qk(t0)
                if attn:
                    copy_attn(t2, 0, (c_av, t2))
                if 0 <= t1 < NT:
                    exps(t1, 1.0 / math.sqrt(HDC))
                if t0 + 1 < NT:
                    copy_x(NT + t0 + 1, bank[0], (c_qk, 2 * t0))
                if attn:
                    copy_attn(t2, 2, (c_av, t2))
                    act.wait_ge(c_av, t2 + 1)
                    after(act, c_ct, t2)
                    nc.scalar.copy(cx, bank[4][:, 0:D]).then_inc(c_cx, 1)
                if s in (1, 2):
                    for i in range(2):
                        split(wq_high, wq_low, 8 + 2 * (s - 1) + i, 512, in_wq, wq_hi)
                if 3 <= s < 7:
                    split(wo_high, wo_low, s - 3, 1024, in_wo, wo_hi)
                if s == NT + 1:
                    copy_x(2 * NT, bank[6], (c_qk, 2 * NT))
                if s >= NT:
                    act.wait_ge(c_v, NT)
                    for i in last_pieces[s - NT]:
                        split(wq_high, wq_low, i, 512, in_wq, wq_hi)
                if s == NT + 2:
                    nc.scalar.copy(half(ident_h), ident).then_inc(masked, 1)
                    nc.scalar.copy(half(causal_h), c("causal")).then_inc(masked, 1)

            def gate(t):
                act.wait_ge(e_dif, t + 1)
                nc.scalar.activation(gtmp[:, 0:1], dif[:, :], ACT.Tanh, scale=0.5).then_inc(e_th, 1)

            for s in range(1, NT + 3):
                t0, t1, t2, t3 = s, s - 1, s - 2, s - 3
                main, attn = 0 <= t1 < NT, 0 <= t2 < NT
                for g in range(4):
                    if attn and g == 3:
                        copy_attn(NT + t2, 0, (d_av, 4 * t2))
                    if main:
                        act.wait_ge(d_T, 5 * t1 + g + 1)
                        after(act, d_sc, t1)
                        nc.scalar.copy(qT[:, g * 512:(g + 1) * 512], bank[6 + g % 2]).then_inc(d_qc, 1)
                if attn:
                    copy_attn(NT + t2, 1, (d_av, 4 * t2))
                if main:
                    act.wait_ge(d_T, 5 * t1 + 5)
                    nc.scalar.copy(qT[:, 4 * 512:5 * 512], bank[6]).then_inc(d_qc, 1)
                if t3 >= 0:
                    act.wait_ge(e_T, t3 + 1)
                    after(act, e_lg, t3)
                    nc.scalar.copy(h2T, bank[0][:, 0:D]).then_inc(e_Tc, 1)
                if attn:
                    copy_attn(NT + t2, 2, (d_av, 4 * t2))
                    copy_attn(NT + t2, 3, (d_av, 4 * t2))
                if main:
                    act.wait_ge(d_pj, 6 * t1 + 6)
                    after(act, d_av, 4 * (t1 - 1))
                    nc.scalar.copy(vs[:, t1 % 2, :], bank[1]).then_inc(d_vc, 1)
                if t0 < NT:
                    squares(t0)
                if t3 >= 0:
                    act.wait_ge(e_h2, t3 + 1)
                    nc.scalar.copy(h2r[:, t3 % 2, 1, 0:D], h2r[:, t3 % 2, 0, 0:D]).then_inc(e_h2k, 1)
                    gate(t3)
                if attn:
                    for kv in range(KV):
                        act.wait_ge(d_av, 4 * t2 + kv + 1)
                        after(act, d_wo, t2)
                        nc.scalar.copy(half(oT[0][:, kv * 512:(kv + 1) * 512]), attn_bank(NT, kv)).then_inc(d_oA, 1)
                if t0 < NT:
                    copy_x(2 * NT + t0, bank[6], (d_pj, 6 * (t0 - 1)))
                if main:
                    exps(NT + t1, 1.0 / math.sqrt(HD))
                if attn:
                    act.wait_ge(d_xp, t2 + 1)
                    after(act, e_ms, t2)
                    act.wait_ge(d_ss, min(t0 + 1, NT))
                    nc.scalar.activation(sq_junk, tile(XP, t2), ACT.Square, accum_out=th[:, :]).then_inc(e_ss, 1)

            def f_copy_x(j, u):
                act.wait_ge(f_t, at(j))
                act.wait_ge(f_h, at(j - 3, 4, 3))
                nc.scalar.copy(hsT[:, u, :], bank[5][:, 0:D]).then_inc(f_tc, 1)

            def f_silus(j, n):
                act.wait_ge(f_h, at(j, 4, 2 * n))
                act.wait_ge(f_mul, at(j - 1, 2, n))
                nc.scalar.activation(silu_f[:, n, :], bank[n][:, 0:HF], ACT.Silu).then_inc(f_silu, 1)

            def f_copy(j, u, n):
                act.wait_ge(f_T, at(j, 2, n))
                act.wait_ge(f_y, at(j - 3))
                o, w = ((0, 3 * P), (3 * P, 4 * P))[n]
                nc.scalar.copy(actT_f[:, u, o:o + w], bank[6 + n][:, 0:w]).then_inc(f_Tc, 1)

            def f_step(s, r, head=True, main=True, tail=True):
                if main:
                    f_silus(s - 1, 0)
                if tail:
                    f_copy(s - 2, (r - 2) % 3, 1)
                if head:
                    f_copy_x(s, r % 3)
                if main:
                    f_silus(s - 1, 1)
                    f_copy(s - 1, (r - 1) % 3, 0)

            f_step(0, 0, main=False, tail=False)
            f_step(1, 1, tail=False)
            count = steps(act)
            with act.Fori(0, (TILES_F - 2) // 3) as i:
                for u in range(3):
                    with act.If(count > 3 * i + 2 + u):
                        f_step(3 * i + 2 + u, 2 + u)
            with act.If(count > TILES_F):
                f_step(TILES_F, TILES_F, head=False)
            with act.If(count > TILES_F + 1):
                f_step(TILES_F + 1, TILES_F + 1, head=False, main=False)

        @block.vector
        def _(dve):
            links = [0]

            def link(ins):
                links[0] += 1
                ins.then_inc(chain, 1)
                dve.wait_ge(chain, links[0])


            def norm_stats(n):
                t, q = n % NT, n % 2
                if n < NT:
                    dve.wait_ge(in_x[min(t, 2)], 16 if t < 2 else 16 * (NT - 2))
                else:
                    dve.wait_ge(res, n - NT + 1)
                after(dve, g_ve, n - 1)
                link(nc.vector.bn_stats(stat[:, q, :], tile(X, t)))
                nc.vector.bn_aggr(mv[:, q, :], stat[:, q, :]).then_inc(stats, 1)

            def norm_apply(n, dst, done):
                t, q = n % NT, n % 2
                dve.wait_ge(g_rstd, n + 1)
                dve.wait_ge(stats, n + 1)
                nc.vector.tensor_scalar(dst, tile(X, t), mv[:, q, 0:1], rstd[:, q, :],
                                        ALU.subtract, ALU.mult).then_inc(done, 1)

            def norm_halves(n):
                q = n % 2
                dve.wait_ge(g_rstd, n + 1)
                dve.wait_ge(stats, n + 1)
                for b in range(2):
                    r = slice(S * b, S * b + S)
                    ins = nc.vector.tensor_scalar(xz[r, q, b, :], tile(X, n)[r], mv[r, q, 0:1], rstd[r, q, :],
                                                  ALU.subtract, ALU.mult)
                ins.then_inc(normed, 1)

            def split_b(i):
                dve.wait_ge(wb_hi, i + 1)
                v = slice(i * PIECE_B, (i + 1) * PIECE_B)
                nc.vector.tensor_tensor(half(wb_low[:, v]), wb_low[:, v], half_value(wb_high[:, v]),
                                        ALU.subtract).then_inc(wb_lo, 1)

            link(nc.vector.memset(xz, 0.0))
            norm_stats(0)
            norm_halves(0)
            norm_stats(1)
            norm_halves(1)
            norm_stats(2)
            link(nc.vector.memset(cum[:, 0, :], 0.0))
            for s in range(1, NT + 1):
                if s + 1 < NT:
                    after(dve, a_sc, 2 * s)
                    norm_halves(s + 1)
                if s + 2 < NT:
                    norm_stats(s + 2)
                if s >= 1:
                    t = s - 1
                    dve.wait_ge(a_out, 2 * t + 2)
                    nc.vector.tensor_tensor(tile(X, t), tile(X, t), bank[4 + t % 2][:, 0:D], ALU.add).then_inc(res, 1)
                if 5 <= s < NT:
                    split_b(s - 5)

            dve.wait_ge(in_cst, 16)

            def top_two(logits, ready, read, dif_done, th_src, th_done, t, prob):
                dve.wait_ge(ready, t + 1)
                link(nc.vector.max(top[:, :], logits))
                ins = nc.vector.max_index(topi[:, :], top[:, :], logits)
                if read is not None:
                    ins.then_inc(read, 1)
                    dve.wait_ge(read, t + 1)
                else:
                    link(ins)
                nc.vector.tensor_tensor(dif[:, :], top[:, 1:2], top[:, 0:1], ALU.subtract).then_inc(dif_done, 1)
                link(nc.vector.tensor_copy(topf[:, :], topi[:, 0:2]))
                dve.wait_ge(th_done, t + 1)
                link(nc.vector.tensor_scalar(prob[:, 0:1], th_src, -0.5, 0.5, ALU.mult, ALU.add))
                link(nc.vector.tensor_scalar(prob[:, 1:2], th_src, 0.5, 0.5, ALU.mult, ALU.add))

            def b_gating(t):
                prob = pr[:, 0:2]
                top_two(bank[5][:, D:D + E], b_lg, b_log, b_dif, th[:, :], b_th, t, prob)
                link(nc.vector.tensor_scalar(gtmp[:, :], c("iota_e"), topf[:, 0:1], prob[:, 0:1],
                                             ALU.is_equal, ALU.mult))
                link(nc.vector.tensor_scalar(gates[:, t % 2, :], c("iota_e"), topf[:, 1:2], prob[:, 1:2],
                                             ALU.is_equal, ALU.mult))
                link(nc.vector.tensor_tensor(gates[:, t % 2, :], gates[:, t % 2, :], gtmp[:, :], ALU.add))

            def b_muls(t, g):
                n = NG0 * t + g
                dve.wait_ge(b_silu, n + 1)
                dve.wait_ge(b_h, 2 * n + 2)
                after(dve, b_t, 3 * (t - 1))
                for i in range(2):
                    e = 2 * g + i
                    ins = nc.vector.scalar_tensor_tensor(
                        out=act_b[:, t % 2, e * H0:(e + 1) * H0], in0=silu_b[:, g % 2, i * H0:(i + 1) * H0],
                        scalar=gates[:, t % 2, e:e + 1], in1=bank[2 + g % 2][:, i * H0:(i + 1) * H0],
                        op0=ALU.mult, op1=ALU.mult)
                ins.then_inc(b_mul, 1)

            def low_x(m, src, free):
                dve.wait_ge(c_x, m + 1)
                after(dve, *free)
                nc.vector.tensor_tensor(half(xTl[:, m % 2, :]), src[:, 0:D], half_value(xT[:, m % 2, :]), ALU.subtract).then_inc(c_xl, 1)

            def b_low(t, u):
                dve.wait_ge(b_tA, 3 * t + u + 1)
                after(dve, b_y, t - 1)
                v = slice(4 * u * P, min(4 * u + 4, NC0) * P)
                nc.vector.tensor_tensor(half(actTl_b[t % 2][:, v]), bank[6 + u % 2][:, 0:v.stop - v.start],
                                        half_value(actT_b[:, t % 2, v]), ALU.subtract).then_inc(b_tD, 1)

            for s in range(NT + 2):
                t0, t1, t2 = s, s - 1, s - 2
                main = 0 <= t1 < NT
                if t0 < NT:
                    norm_stats(NT + t0)
                    after(dve, t_x, t0 - 1)
                    norm_apply(NT + t0, xn[:, t0 % 2, :], normed)
                if s == 0:
                    split_b(3)
                if main:
                    b_muls(t1, 0)
                if t2 >= 0:
                    b_low(t2, 2)
                if main:
                    b_muls(t1, 1)
                if t0 < NT:
                    low_x(t0, bank[5], (b_h, 2 * NG0 * (t0 - 1)))
                if main:
                    b_muls(t1, 2)
                if t2 >= 0:
                    dve.wait_ge(b_y, t2 + 1)
                    nc.vector.tensor_tensor(tile(X, t2), tile(X, t2), bank[4][:, 0:D], ALU.add).then_inc(res, 1)
                if main:
                    b_low(t1, 0)
                if t0 < NT:
                    b_gating(t0)
                if main:
                    b_muls(t1, 3)
                    b_low(t1, 1)
                if s == 1:
                    split_b(4)
                    split_b(5)

            sc_v = psc[:, :].rearrange("p (h k) -> p h k", h=NH)
            e_v = e_sb[:, :].rearrange("p (h k) -> p h k", h=NH)

            def over_keys(v, parts=slice(0, P)):
                return v[parts, :].rearrange("p (h o) -> p h o", o=1).to_broadcast([v[parts, :].shape[0], NH, S])

            def softmax_shift(m):
                link(nc.vector.tensor_reduce(mx[:, :], sc_v, AX_X, ALU.max))
                after(dve, s_nv, m)
                after(dve, s_ng, m)
                nc.vector.tensor_tensor(e_v, sc_v, over_keys(mx), ALU.subtract).then_inc(s_sub, 1)

            def softmax_sums(m):
                dve.wait_ge(s_exp, m + 1)
                link(nc.vector.tensor_reduce(sums[:, :], e_v, AX_X, ALU.add))
                after(dve, s_ng, m)
                nc.vector.reciprocal(rsum[:, :], sums[:, :]).then_inc(s_rs, 1)

            def softmax_weights(m):
                dve.wait_ge(s_rs, m + 1)
                after(dve, s_t, 4 * (m - 1))
                if m == 0:
                    dve.wait_ge(zeroed, NT)
                v = bd[0:S, m % 2, :].rearrange("p (h k) -> p h k", h=NH)[:, :, 0:S]
                nc.vector.tensor_tensor(v, e_v[0:S], over_keys(rsum, slice(0, S)), ALU.mult).then_inc(s_nv, 1)

            def copy_attn(m, u, free):
                dve.wait_ge(s_t, 4 * m + u + 1)
                after(dve, *free)
                nc.vector.tensor_copy(aT[:, u * 512:(u + 1) * 512], attn_bank(m, u)).then_inc(s_cD, 1)

            dve.wait_ge(in_rows, 16)
            def split(high, low, i, n, ready, done, before):
                dve.wait_ge(ready, before + 1)
                v = slice(i * n, (i + 1) * n)
                nc.vector.tensor_tensor(half(low[:, v]), low[:, v], half_value(high[:, v]), ALU.subtract).then_inc(done, 1)

            def rms_apply(t):
                dve.wait_ge(d_rms, t + 1)
                after(dve, t_x, 2 * NT + t - 1)
                nc.vector.scalar_tensor_tensor(out=xn[:, t % 2, :], in0=tile(XP, t), scalar=rms[:, t % 2, :],
                                               in1=lnw_row, op0=ALU.mult, op1=ALU.mult).then_inc(normed, 1)

            def low_x2(t):
                dve.wait_ge(c_x, 2 * NT + t + 1)
                after(dve, d_pj, 6 * (t - 1))
                nc.vector.tensor_tensor(half(xTl[:, t % 2, :]), bank[6][:, 0:D], half_value(xT[:, t % 2, :]),
                                        ALU.subtract).then_inc(c_xl, 1)

            norm_stats(2 * NT)
            norm_apply(2 * NT, xn[:, 0, :], normed)
            for s in range(NT + 3):
                t0, t1, t2, t3 = s, s - 1, s - 2, s - 3
                attn = 0 <= t2 < NT
                if t0 + 1 < NT:
                    norm_stats(2 * NT + t0 + 1)
                if 0 <= t1 < NT:
                    dve.wait_ge(c_sc, t1 + 1)
                    softmax_shift(t1)
                if t0 + 1 < NT:
                    after(dve, t_x, NT + t0)
                    norm_apply(2 * NT + t0 + 1, xn[:, (t0 + 1) % 2, :], normed)
                if t0 < KBD_SHARED:
                    dve.wait_ge(c_qkc, 4 * t0 + 2)
                    after(dve, c_sc, t0)
                    for b in range(2):
                        kT = qkT[:, t0 % 2, 1, P + S * b:P + S * b + S]
                        nc.vector.tensor_tensor(
                            kbd[:, 1, b, :].rearrange("p (h n) -> p h n", h=8),
                            kT.rearrange("p (o n) -> p o n", o=1).to_broadcast([P, 8, S]),
                            c("headmask").rearrange("p (h o) -> p h o", o=1).to_broadcast([P, 8, S]),
                            ALU.mult).then_inc(c_kbd, 1)
                if t0 < NT:
                    dve.wait_ge(c_v, t0 + 1)
                    after(dve, c_av, t0 - 3)
                    nc.vector.tensor_tensor(vs_c[:, t0 % 4, :], bank[0][:, D:2 * D], bv_row, ALU.add).then_inc(c_vc, 1)
                if s == NT + 2:
                    low_x2(0)
                if t3 >= 0:
                    dve.wait_ge(c_wo, t3 + 1)
                    link(nc.vector.tensor_tensor(tile(X, t3), tile(X, t3), bank[5][:, D:2 * D], ALU.add))
                    nc.vector.tensor_tensor(tile(X, t3), tile(X, t3), bo_row, ALU.add).then_inc(res, 1)
                if attn:
                    copy_attn(t2, 1, (c_av, t2))
                    copy_attn(t2, 3, (c_av, t2))
                if 0 <= t1 < NT:
                    softmax_sums(t1)
                    softmax_weights(t1)
                if s in (1, 2):
                    for i in range(2):
                        split(wq_high, wq_low, 8 + 2 * (s - 1) + i, 512, wq_hi, wq_lo, 2 * (s - 1) + i)
                if 3 <= s < 7:
                    split(wo_high, wo_low, s - 3, 1024, wo_hi, wo_lo, s - 3)
                if s == NT:
                    norm_stats(3 * NT)
                    norm_apply(3 * NT, tile(XP, 0), d_z)
                if s == NT + 1:
                    rms_apply(0)
                if s >= NT:
                    for n, i in enumerate(last_pieces[s - NT]):
                        split(wq_high, wq_low, i, 512, wq_hi, wq_lo, 4 + sum(map(len, last_pieces[:s - NT])) + n)

            def heads(v):
                return v.rearrange("p (h x n) -> p h x n", h=4, x=2)

            def rope(t, g):
                n = 5 * t + g
                dve.wait_ge(d_pj, 6 * t + g + 1)
                after(dve, d_radd, n - 1)
                src = heads(proj_bank(g))
                cos, sin = (c(w).rearrange("p (o n) -> p o n", o=1).to_broadcast([P, 4, HD])
                            for w in ("cos", "sin"))
                nc.vector.tensor_tensor(ra[:, g % 2, :].rearrange("p (h n) -> p h n", h=4),
                                        proj_bank(g).rearrange("p (h n) -> p h n", h=4), cos, ALU.mult)
                rbv = heads(rb[:, g % 2, :])
                for part in range(2):
                    a, b = CONST["sin"]
                    sn = cst[:, a + part * (HD // 2):a + (part + 1) * (HD // 2)].rearrange(
                        "p (o n) -> p o n", o=1).to_broadcast([P, 4, HD // 2])
                    ins = nc.vector.tensor_tensor(rbv[:, :, part, :], src[:, :, 1 - part, :], sn, ALU.mult)
                ins.then_inc(d_rope, 1)

            def route(t):
                prob = pr[:, 2 * t:2 * t + 2]
                top_two(bank[0][:, D:D + E], e_lg, None, e_dif, gtmp[:, 0:1], e_th, t, prob)
                link(nc.vector.tensor_scalar(hot[:, t, 0, :], c("iota_e"), topf[:, 0:1], None, ALU.is_equal))
                link(nc.vector.tensor_scalar(hot[:, t, 1, :], c("iota_e"), topf[:, 1:2], None, ALU.is_equal))
                link(nc.vector.tensor_tensor(msel[:, t, :], hot[:, t, 0, :], hot[:, t, 1, :], ALU.add))
                nc.vector.tensor_tensor(cum[:, t + 1, :], cum[:, t, :], msel[:, t, :], ALU.add).then_inc(e_sel, 1)

            def places(t):
                dve.wait_ge(e_rank, t + 1)
                link(nc.vector.tensor_tensor(posf[:, :], bank[0][:, D + E:D + 2 * E], c("ebase"), ALU.add))
                link(nc.vector.tensor_tensor(pos2[:, :, :], hot[:, t, :, :],
                                             posf[:, :].rearrange("p (o n) -> p o n", o=1).to_broadcast([P, 2, E]),
                                             ALU.mult))
                link(nc.vector.tensor_reduce(topf[:, :], pos2[:, :, :], AX_X, ALU.add))
                nc.vector.tensor_copy(pos[:, t, :], topf[:, :]).then_inc(e_pos, 1)
                dve.wait_ge(e_pos, t + 1)

            def slot_rows_of(t):
                dve.wait_ge(d_xp, t + 1)
                dve.wait_ge(e_rms, t + 1)
                after(dve, e_sent[t % 2], 32 * (t // 2))
                after(dve, e_Tc, t - 1)
                nc.vector.tensor_copy(h2r[:, t % 2, :, D].bitcast(U32),
                                      cst[:, CONST["dest"][0] + 2 * t:CONST["dest"][0] + 2 * t + 2].bitcast(U32))
                nc.vector.scalar_tensor_tensor(out=h2r[:, t % 2, 0, 0:D], in0=tile(XP, t),
                                               scalar=th[:, :], in1=ffw_row, op0=ALU.mult, op1=ALU.mult).then_inc(e_h2, 1)

            for s in range(1, NT + 3):
                t0, t1, t2, t3 = s, s - 1, s - 2, s - 3
                main, attn = 0 <= t1 < NT, 0 <= t2 < NT
                if main:
                    rope(t1, 0)
                    rope(t1, 1)
                if t0 < NT:
                    norm_stats(3 * NT + t0)
                if main:
                    rope(t1, 2)
                if t3 >= 0:
                    slot_rows_of(t3)
                if main:
                    rope(t1, 3)
                if t0 < NT:
                    norm_apply(3 * NT + t0, tile(XP, t0), d_z)
                if main:
                    rope(t1, 4)
                if t3 >= 0:
                    route(t3)
                if t0 < NT:
                    rms_apply(t0)
                if attn:
                    for kv in range(KV):
                        dve.wait_ge(d_oA, 4 * t2 + kv + 1)
                        after(dve, d_wo, t2)
                        v = slice(kv * 512, (kv + 1) * 512)
                        nc.vector.tensor_tensor(half(oT[1][:, v]), attn_bank(NT, kv), half_value(oT[0][:, v]),
                                                ALU.subtract).then_inc(d_oD, 1)
                if main:
                    dve.wait_ge(d_sc, t1 + 1)
                    softmax_shift(NT + t1)
                if t3 >= 0:
                    places(t3)
                if t0 < NT:
                    low_x2(t0)
                if main:
                    softmax_sums(NT + t1)
                if attn:
                    dve.wait_ge(d_wo, t2 + 1)
                    nc.vector.tensor_tensor(tile(XP, t2), tile(XP, t2), bank[1][:, 0:D], ALU.add).then_inc(d_xp, 1)
                if main:
                    softmax_weights(NT + t1)

            dve.wait_ge(e_tot, 1)
            link(nc.vector.tensor_scalar(tot_i[:, :], bank[4][:, 8:8 + E], float(P - 1), None, ALU.add))
            link(nc.vector.tensor_scalar(tot_i[:, :], tot_i[:, :], 7, None, ALU.logical_shift_right))
            link(nc.vector.tensor_copy(tl[:, :], tot_i[:, :]))
            link(nc.vector.tensor_scalar(tl[:, :], tl[:, :], 1.0, None, ALU.max))
            link(nc.vector.tensor_tensor_scan(cinc[:, :], c("ones")[:, 0:E], tl[:, :], 0.0, ALU.mult, ALU.add))
            b24 = lambda v: v.rearrange("p (n o) -> p n o", o=1).to_broadcast([P, 24, E])
            b8 = lambda v: v.rearrange("p (o n) -> p o n", o=1).to_broadcast([P, 24, E])
            link(nc.vector.tensor_tensor(cmp_[:, :, :], b24(c("iota_t")), b8(cinc[:, :]), ALU.is_ge))
            link(nc.vector.tensor_reduce(tabf[:, 0, :], cmp_[:, :, :], AX_X, ALU.add))
            link(nc.vector.tensor_tensor(cmp_[:, :, :], cmp_[:, :, :], b8(tl[:, :]), ALU.mult))
            link(nc.vector.tensor_reduce(tabf[:, 1, :], cmp_[:, :, :], AX_X, ALU.add))
            link(nc.vector.tensor_scalar(tabf[:, 0, :], tabf[:, 0, :], float(E - 1), None, ALU.min))
            link(nc.vector.tensor_tensor(tabf[:, 1, :], c("iota_t"), tabf[:, 1, :], ALU.subtract))
            link(nc.vector.tensor_scalar(tabf[:, 1, :], tabf[:, 1, :], float(T // P - 1), float(P), ALU.min, ALU.mult))
            link(nc.vector.scalar_tensor_tensor(out=tabf[:, 1, :], in0=tabf[:, 0, :], scalar=float(T),
                                                in1=tabf[:, 1, :], op0=ALU.mult, op1=ALU.add))
            link(nc.vector.tensor_copy(tab[:, 0, :], tabf[:, 1, :]))
            link(nc.vector.tensor_scalar(tab[:, 0, TILES_F:TILES_F + 1], cinc[:, E - 1:E], 2.0, None, ALU.add))
            link(nc.vector.memset(tabf[:, 2, 0:1], 0.0))
            link(nc.vector.tensor_tensor(tabf[:, 2, 1:24], tabf[:, 0, 1:24], tabf[:, 0, 0:23], ALU.not_equal))
            link(nc.vector.scalar_tensor_tensor(out=tabf[:, 2, :], in0=tabf[:, 0, :], scalar=2.0, in1=tabf[:, 2, :],
                                                op0=ALU.is_ge, op1=ALU.mult))
            link(nc.vector.tensor_copy(tab[:, 3, :], tabf[:, 2, :]))
            link(nc.vector.tensor_scalar(tabf[:, 3, :], tabf[:, 0, :], float(P), None, ALU.mult))
            link(nc.vector.tensor_copy(tab[:, 1, :], tabf[:, 3, :]))
            link(nc.vector.tensor_scalar(tabf[:, 5, :], tabf[:, 0, :], float(NSLOT), float(-NSLOT), ALU.is_ge, ALU.mult))
            link(nc.vector.tensor_scalar(tabf[:, 6, :], tabf[:, 0, :], float(2 * NSLOT), float(-NSLOT), ALU.is_ge, ALU.mult))
            link(nc.vector.tensor_tensor(tabf[:, 4, :], tabf[:, 0, :], tabf[:, 5, :], ALU.add))
            link(nc.vector.tensor_tensor(tabf[:, 4, :], tabf[:, 4, :], tabf[:, 6, :], ALU.add))
            link(nc.vector.tensor_scalar(tabf[:, 4, :], tabf[:, 4, :], float(WF), None, ALU.mult))
            nc.vector.tensor_copy(tab[:, 2, :], tabf[:, 4, :]).then_inc(tables, 1)

            def f_muls(j, u, n):
                dve.wait_ge(f_silu, at(j, 2, n))
                dve.wait_ge(f_h, at(j, 4, 2 * n + 1))
                dve.wait_ge(f_T, at(j - 3, 2, 1))
                nc.vector.tensor_tensor(act_f[:, u, n * HF:(n + 1) * HF], silu_f[:, n, :], bank[2 + n][:, 0:HF],
                                        ALU.mult).then_inc(f_mul, 1)

            def f_copy_y(j, u):
                dve.wait_ge(f_y, at(j))
                dve.wait_ge(f_left, at(j - 3))
                nc.vector.tensor_copy(ys[:, u, :], bank[4][:, 0:D]).then_inc(f_ys, 1)

            def f_step(s, sx, main=True, tail=True):
                if main:
                    f_muls(s - 1, (sx[1] - 1) % 3, 0)
                    f_muls(s - 1, (sx[1] - 1) % 3, 1)
                if tail:
                    u = sx[1] - 2
                    f_copy_y(s - 2, u % 3)

            f_step(1, (0, 1), tail=False)
            count = steps(dve)
            with dve.Fori(0, (TILES_F - 2) // 3) as i:
                for u in range(3):
                    with dve.If(count > 3 * i + 2 + u):
                        f_step(3 * i + 2 + u, (i + (2 + u) // 3, (2 + u) % 3))
            with dve.If(count > TILES_F):
                f_step(TILES_F, (TILES_F // 3, TILES_F % 3))
            with dve.If(count > TILES_F + 1):
                f_step(TILES_F + 1, ((TILES_F + 1) // 3, (TILES_F + 1) % 3), main=False)

            dve.wait_ge(e_base, NT)
            for t in range(NT + 1):
                for k, i, done in ((0, t, g_first), (1, t - 1, g_sum)):
                    if 0 <= i < NT:
                        dve.wait_ge(*((g_first, i + 1) if k else (g_in[i], 16)))
                        nc.vector.scalar_tensor_tensor(out=tile(X, i), in0=yk[:, i, k, :],
                                                       scalar=pr[:, 2 * i + k:2 * i + k + 1], in1=tile(X, i),
                                                       op0=ALU.mult, op1=ALU.add).then_inc(done, 1)

        @block.gpsimd
        def _(pool):
            for s_, per in F_PER:
                pool.sem_inc(s_, per * LEAD)
            exponent = minus_half[:, :]
            nc.gpsimd.memset(exponent, -0.5).then_inc(halved, 1)
            pool.wait_ge(halved, 1)

            def inv_sqrt(src, scale, tmp, tmp_done, count, dst, done):
                nc.gpsimd.tensor_scalar(tmp, src, scale, LN_EPS, ALU.mult, ALU.add).then_inc(tmp_done, 1)
                pool.wait_ge(tmp_done, count)
                nc.gpsimd.tensor_tensor(dst, tmp, exponent, ALU.pow).then_inc(done, 1)

            def norm(n, last):
                q = n % 2
                pool.wait_ge(stats, n + 1)
                after(pool, *last)
                inv_sqrt(mv[:, q, 1:2], 1.0, ve[:, q, :], g_ve, n + 1, rstd[:, q, :], g_rstd)

            for n in range(2 * NT):
                norm(n, (normed, n - 1))
                if n >= NT:
                    i = n - NT
                    nc.gpsimd.memset(bd[:, i // 4, i % 4 * 512:(i % 4 + 1) * 512], 0.0).then_inc(zeroed, 1)
            pool.wait_ge(zeroed, NT)

            def weights(m, own, count):
                after(pool, own, count)
                pool.wait_ge(s_exp, m + 1)
                pool.wait_ge(s_rs, m + 1)
                after(pool, s_t, 4 * (m - 1))
                v = bd[S:P, m % 2, :].rearrange("p (h k) -> p h k", h=NH)[:, :, S:P]
                e_v = e_sb[S:P, :].rearrange("p (h k) -> p h k", h=NH)
                r = rsum[S:P, :].rearrange("p (h o) -> p h o", o=1).to_broadcast([S, NH, S])
                nc.gpsimd.tensor_tensor(v, e_v, r, ALU.mult).then_inc(s_ng, 1)
                pool.wait_ge(s_ng, m + 1)

            pool.wait_ge(in_cst, 16)
            hm = c("headmask").rearrange("p (h o) -> p h o", o=1).to_broadcast([P, 8, S])
            norm(2 * NT, (normed, 2 * NT - 1))
            for s in range(NT + 1):
                t0, t1 = s, s - 1
                if t0 + 1 < NT:
                    norm(2 * NT + t0 + 1, (normed, 2 * NT + t0))
                if t0 < NT:
                    after(pool, c_sc, t0)
                    for k in range(1 if t0 < KBD_SHARED else KC):
                        pool.wait_ge(c_qkc, 4 * t0 + 1 + k)
                        for b in range(2):
                            kT = qkT[:, t0 % 2, 1, k * P + S * b:k * P + S * b + S]
                            nc.gpsimd.tensor_tensor(
                                kbd[:, k, b, :].rearrange("p (h n) -> p h n", h=8),
                                kT.rearrange("p (o n) -> p o n", o=1).to_broadcast([P, 8, S]), hm,
                                ALU.mult).then_inc(c_kbd, 1)
                if t1 >= 0:
                    weights(t1, c_kbd, 4 * min(t0 + 1, NT))

            norm(3 * NT, (normed, 3 * NT - 1))
            pool.wait_ge(d_ss, 1)
            inv_sqrt(ss[:, 0, :], 1.0 / D, ms[:, 0, :], d_ms, 1, rms[:, 0, :], d_rms)

            def rms2(t):
                pool.wait_ge(e_ss, t + 1)
                nc.gpsimd.tensor_scalar(gtmp[:, 4:5], th[:, :], 1.0 / D, LN_EPS, ALU.mult, ALU.add).then_inc(e_ms, 1)
                pool.wait_ge(e_ms, t + 1)
                nc.gpsimd.tensor_tensor(th[:, :], gtmp[:, 4:5], exponent, ALU.pow).then_inc(e_rms, 1)

            def send_rows(t):
                pool.wait_ge(e_pos, t + 1)
                pool.wait_ge(e_h2k, t + 1)
                pool.wait_ge(filled, 16 * E * (T // P))
                for k in range(2):
                    nc.gpsimd.indirect_dma_start(
                        slot_rows, bass.IndirectOffsetOnAxis(ap=pos[:, t, k:k + 1], axis=0),
                        h2r[:, t % 2, k, :], None).then_inc(e_sent[t % 2], 16)
                nc.gpsimd.tensor_tensor(tile(X, t), tile(X, t), tile(XP, t), ALU.add).then_inc(e_base, 1)

            for s in range(1, NT + 3):
                t0, t1, t3, t4 = s, s - 1, s - 3, s - 4
                main = 0 <= t1 < NT
                if main:
                    for g in range(5):
                        if g == 2 and t3 >= 0:
                            rms2(t3)
                        if g == 2 and t0 < NT:
                            norm(3 * NT + t0, (d_z, t0 - 1))
                        pool.wait_ge(d_rope, 5 * t1 + g + 1)
                        after(pool, d_T, 5 * (t1 - 1) + g + 1)
                        nc.gpsimd.tensor_tensor(qr[:, g * 512:(g + 1) * 512], ra[:, g % 2, :], rb[:, g % 2, :],
                                                ALU.add).then_inc(d_radd, 1)
                    if t0 < NT:
                        pool.wait_ge(d_ss, t0 + 1)
                        after(pool, normed, 3 * NT + t0 - 1)
                        inv_sqrt(ss[:, t0 % 2, :], 1.0 / D, ms[:, t0 % 2, :], d_ms, t0 + 1, rms[:, t0 % 2, :], d_rms)
                if not main and t3 >= 0:
                    rms2(t3)
                if t4 >= 0:
                    send_rows(t4)
                if main:
                    if t4 >= 0:
                        pool.wait_ge(e_sent[t4 % 2], 32 * (t4 // 2 + 1))
                        pool.wait_ge(e_base, t4 + 1)
                    weights(NT + t1, d_radd, 5 * t1 + 5)
            send_rows(NT - 1)

            def destinations(j, u):
                pool.wait_ge(f_in[u], 16 * (j // 3 + 1))
                nc.gpsimd.tensor_copy(ids[:, u:u + 1], hs[:, u, D:D + 1].bitcast(U32)).then_inc(f_ids, 1)
                pool.wait_ge(f_ids, at(j))

            def send(j, u):
                pool.wait_ge(f_ys, at(j))
                nc.gpsimd.indirect_dma_start(
                    result_rows, bass.IndirectOffsetOnAxis(ap=ids[:, u:u + 1], axis=0),
                    ys[:, u, :], None).then_inc(f_sent[u], 16)
                pool.wait_ge(f_sent[u], 16 * (j // 3 + 1))
                pool.sem_inc(f_left, 1)

            for j in range(2 * T // P + 2):
                if j >= 2:
                    send(j - 2, (j - 2) % 3)
                destinations(j, j % 3)
            count = steps(pool)
            for j in range(2 * T // P + 2, TILES_F + 2):
                with pool.If(count > j):
                    send(j - 2, (j - 2) % 3)
                    if j < TILES_F:
                        destinations(j, j % 3)


def _constants():
    c = np.zeros((P, NCONST), np.float32)
    def put(name, v):
        a, b = CONST[name]
        c[:, a:b] = v
    p = np.arange(P)
    put("ident", np.eye(P))
    put("tri", p[:, None] < p[None, :])
    put("ones", 1.0)
    inv = np.float32(1000000.0) ** (-np.arange(0, HD, 2, dtype=np.float32) / np.float32(HD))
    ang = np.arange(S, dtype=np.float32)[p % S, None] * inv[None, :].astype(np.float32)
    put("cos", np.concatenate([np.cos(ang), np.cos(ang)], 1))
    put("sin", np.concatenate([-np.sin(ang), np.sin(ang)], 1))
    put("causal", np.where(np.arange(S)[None, :] <= (p % S)[:, None], 0.0, NEG))
    put("headmask", (p // HDC)[:, None] == np.arange(8)[None, :])
    put("ebase", T * np.arange(E)[None, :])
    put("iota_e", np.arange(E)[None, :])
    put("iota_t", np.arange(24)[None, :])
    words = c.view(np.uint32)
    t, k = np.meshgrid(np.arange(NT), np.arange(2), indexing="ij")
    a, b = CONST["dest"]
    words[:, a:b] = 2 * (t.reshape(1, -1) * P + p[:, None]) + k.reshape(1, -1)
    words[:, CONST["fill"][1] - 1] = 2 * T + p
    return c


_OUT = ((B, S, D), "float32")


def kernel(**inputs):
    import numpy as _np
    import concourse.bacc as _bacc
    from concourse import mybir as _mybir
    from concourse.bass_utils import run_bass_kernel_spmd as _run

    a = {k: _np.asarray(v) for k, v in inputs.items()}

    def chunks(w):
        n = w.shape[0] // P
        return w.reshape(n, P, w.shape[1]).transpose(1, 0, 2).reshape(P, -1)

    ctx = a["ctx_2048"].reshape(NT, P, D)
    ctxT = ctx.reshape(NT, P, KC, P).transpose(0, 3, 2, 1).reshape(NT, P, D)
    w1, w2 = (a[f"L0_ffn_{n}"].reshape(HID0, D).T for n in ("W1", "W2"))
    w3 = a["L0_ffn_W3"].transpose(0, 2, 1).reshape(HID0, D)
    even_odd = _np.concatenate([_np.arange(0, HD, 2), _np.arange(1, HD, 2)])
    wq = a["L1_ffn_wq"].reshape(D, NH, HD)[:, :, even_odd].reshape(D, NH * HD)
    wk = a["L1_ffn_wk"].reshape(D, KV, HD)[:, :, even_odd].reshape(D, KV * HD)
    f13 = _np.stack([a["L1_ffn_w1"], a["L1_ffn_w3"]], 2)
    f13 = f13.reshape(E, KC, P, 2 * FF).transpose(0, 2, 1, 3).reshape(E, P, KC * 2 * FF)
    f2 = a["L1_ffn_w2"].reshape(E, NCF, P, D).transpose(0, 2, 1, 3).reshape(E, P, NCF * D)
    arrays = {
        "x": a["x"],
        "ctx_a": _np.concatenate([ctx, ctxT], 2),
        "w_b": _np.concatenate([chunks(_np.concatenate([w1, w2], 1)), chunks(w3)], 1),
        "wg_b": chunks(a["L0_ffn_Wg"].T),
        "w_c": _np.concatenate([chunks(a[f"L1_xattn_W{n}"].T) for n in "qkvo"], 1),
        "b_c": _np.concatenate([a["L1_xattn_bq"].reshape(KC, P).T, a["L1_xattn_bk"].reshape(KC, P).T], 1),
        "rows_c": _np.broadcast_to(_np.concatenate([a["L1_xattn_bv"], a["L1_xattn_bo"], a["L1_ffn_ln_w"],
                                                    a["L1_ffn_ff_ln_w"]])[None, :], (P, len(ROWS) * D)),
        "w_qkv": chunks(_np.concatenate([wq, wk, a["L1_ffn_wv"]], 1)),
        "w_o": chunks(a["L1_ffn_wo"]),
        "gate_d": chunks(a["L1_ffn_gate_w"]),
        "w_f": _np.concatenate([f13, f2], 2).reshape(E * P, WF),
        "consts": _constants(),
    }
    nc = _bacc.Bacc("TRN2", target_bir_lowering=False, num_devices=1)
    feed, args = {}, {}
    for name, v in arrays.items():
        v = _np.ascontiguousarray(v)
        feed[f"in_{name}_dram"] = v
        args[name] = nc.dram_tensor(f"in_{name}_dram", v.shape, _mybir.dt.from_np(v.dtype), kind="ExternalInput").ap()
    out = nc.dram_tensor("out_0_dram", _OUT[0], _mybir.dt.from_np(_np.dtype(_OUT[1])), kind="ExternalOutput").ap()
    build(nc, out=out, **args)
    r = _run(nc, [feed], core_ids=[0])
    return r.results[0]["out_0_dram"]
```
